# Optimizing a Trainium2 kernel written in Bass

```python
import numpy as np
import jax
import jax.numpy as jnp

def _softmax(x, axis=-1):
    return jax.nn.softmax(x, axis=axis)

def _gelu(x):
    return jax.nn.gelu(x, approximate=True)

def _silu(x):
    return jax.nn.silu(x)

def _sigmoid(x):
    return jax.nn.sigmoid(x)

def _layernorm(x, axis=-1, eps=1e-05):
    m = jnp.mean(x, axis=axis, keepdims=True)
    v = jnp.var(x, axis=axis, keepdims=True)
    return (x - m) / jnp.sqrt(v + eps)

def _scatter_add(tgt, idx, src, axis=0):
    return tgt.at[idx].add(src)

def _segment_sum(src, seg, n):
    return jax.ops.segment_sum(src, seg, n)
kernel_name = 'mk_decoder_postln_d1_seqx_r4_1db7b8'

def setup_inputs(seed: int=0):
    np.random.seed(seed)
    _w = jnp.asarray

    def _rec_inputs():
        import jax
        import jax.numpy as jnp
        _rk = jax.random.key(seed)
        x = -0.000125 + 0.9999 * jax.random.normal(jax.random.fold_in(_rk, 1), (8, 512, 256), jnp.float32)
        _lenS = 512 - jax.random.randint(jax.random.fold_in(_rk, 7), (8,), 0, max(1, 512 // 4) + 1, jnp.int32)
        _lenS2 = 512 - jax.random.randint(jax.random.fold_in(_rk, 8), (8,), 0, max(1, 512 // 4) + 1, jnp.int32)
        _ctx_1024P = jax.random.normal(jax.random.fold_in(_rk, 11), (8, 16, 256), jnp.float32)
        _ctx_1024c = jax.random.dirichlet(jax.random.fold_in(_rk, 511), 0.3 * jnp.ones((16,), jnp.float32), (8, 512))
        _ctx_1024t = jnp.einsum('bsk,bkd->bsd', _ctx_1024c, _ctx_1024P)
        _ctx_1024t = _ctx_1024t * jax.lax.rsqrt(jnp.mean(jnp.square(_ctx_1024t)) + 1e-12) * 0.953939
        ctx_1024 = -1.52775e-05 + 0.999936 * (_ctx_1024t + 0.3 * jax.random.normal(jax.random.fold_in(_rk, 611), (8, 512, 256), jnp.float32))
        return (x, ctx_1024)
    x, ctx_1024 = _rec_inputs()

    def _L0_attn_setup():
        import jax, jax.numpy as jnp
        import numpy as np
        E = 256
        H = 16
        D = E // H
        K = 17
        SCALE = D ** (-0.5)
        MAX_DIST = float(K // 2)
        MASK_PENALTY = 10000.0

        def _ln(x, g, b, eps=1e-05):
            mu = jnp.mean(x, axis=-1, keepdims=True)
            var = jnp.mean(jnp.square(x - mu), axis=-1, keepdims=True)
            return (x - mu) * jax.lax.rsqrt(var + eps) * g + b
        key = jax.random.key(seed)
        ks = jax.random.split(key, 6)

        def s(k, shape, std):
            return jax.random.normal(k, shape, jnp.float32) * std
        return {'x': jax.random.normal(ks[0], (4, 512, E), jnp.float32), 'Wq': s(ks[1], (E, E), E ** (-0.5)), 'Wkv': s(ks[2], (E, 2 * E), E ** (-0.5)), 'q_g': jnp.ones((D,), jnp.float32), 'q_b': jnp.zeros((D,), jnp.float32), 'k_g': jnp.ones((D,), jnp.float32), 'k_b': jnp.zeros((D,), jnp.float32), 'Wwin': s(ks[3], (E, 2 * H), 0.1 * E ** (-0.5)), 'bwin': jnp.zeros((2 * H,), jnp.float32), 'Wout': s(ks[4], (E, E), E ** (-0.5))}
    _L0_attn_all = _L0_attn_setup()
    _L0_attn_in = {k: v for k, v in _L0_attn_all.items() if k in ('Wq', 'Wkv', 'q_g', 'q_b', 'k_g', 'k_b', 'Wwin', 'bwin', 'Wout')}
    del _L0_attn_all

    def _L0_xattn_setup():
        import jax, jax.numpy as jnp
        import numpy as np
        import math
        D_KEY = 256
        SCALE = math.sqrt(D_KEY)
        MASK_VAL = 10000000000.0
        key = jax.random.key(seed)
        kq, kk, kv = jax.random.split(key, 3)
        B, L, D = (16, 512, 256)
        return {'query': jax.random.normal(kq, (B, L, D), dtype=jnp.float32), 'key': jax.random.normal(kk, (B, L, D), dtype=jnp.float32), 'value': jax.random.normal(kv, (B, L, D), dtype=jnp.float32)}
    _L0_xattn_all = _L0_xattn_setup()
    _L0_xattn_in = {k: v for k, v in _L0_xattn_all.items() if k in ()}
    del _L0_xattn_all

    def _L0_ffn_setup():
        import jax, jax.numpy as jnp
        import numpy as np
        HIDDEN = 256
        NUM_EXPERTS = 8
        TOP_K = 2
        FFN = 1024
        BATCH, SEQ = (4, 512)
        key = jax.random.key(seed)
        k_x, k_r, k_w1, k_w2 = jax.random.split(key, 4)
        x = jax.random.normal(k_x, (BATCH, SEQ, HIDDEN), dtype=jnp.float32)
        router_w = jax.random.normal(k_r, (NUM_EXPERTS, HIDDEN), dtype=jnp.float32) * (1.0 / np.sqrt(HIDDEN))
        lim = float(np.sqrt(6.0 / (FFN + HIDDEN)))
        expert_w1 = jax.random.uniform(k_w1, (NUM_EXPERTS, FFN, HIDDEN), dtype=jnp.float32, minval=-lim, maxval=lim)
        expert_w2 = jax.random.uniform(k_w2, (NUM_EXPERTS, HIDDEN, FFN), dtype=jnp.float32, minval=-lim, maxval=lim)
        return {'x': x, 'router_w': router_w, 'expert_w1': expert_w1, 'expert_w2': expert_w2}
    _L0_ffn_all = _L0_ffn_setup()
    _L0_ffn_in = {k: v for k, v in _L0_ffn_all.items() if k in ('router_w', 'expert_w1', 'expert_w2')}
    del _L0_ffn_all
    return {'x': x, 'ctx_1024': ctx_1024, 'L0_attn_Wq': _L0_attn_in['Wq'], 'L0_attn_Wkv': _L0_attn_in['Wkv'], 'L0_attn_q_g': _L0_attn_in['q_g'], 'L0_attn_q_b': _L0_attn_in['q_b'], 'L0_attn_k_g': _L0_attn_in['k_g'], 'L0_attn_k_b': _L0_attn_in['k_b'], 'L0_attn_Wwin': _L0_attn_in['Wwin'], 'L0_attn_bwin': _L0_attn_in['bwin'], 'L0_attn_Wout': _L0_attn_in['Wout'], 'L0_ffn_router_w': _L0_ffn_in['router_w'], 'L0_ffn_expert_w1': _L0_ffn_in['expert_w1'], 'L0_ffn_expert_w2': _L0_ffn_in['expert_w2']}

def reference(x, ctx_1024, L0_attn_Wq, L0_attn_Wkv, L0_attn_q_g, L0_attn_q_b, L0_attn_k_g, L0_attn_k_b, L0_attn_Wwin, L0_attn_bwin, L0_attn_Wout, L0_ffn_router_w, L0_ffn_expert_w1, L0_ffn_expert_w2):
    import jax
    import jax.numpy as jnp

    def _L0_attn_ref(x, Wq, Wkv, q_g, q_b, k_g, k_b, Wwin, bwin, Wout):
        import jax, jax.numpy as jnp
        import numpy as np
        E = 256
        H = 16
        D = E // H
        K = 17
        SCALE = D ** (-0.5)
        MAX_DIST = float(K // 2)
        MASK_PENALTY = 10000.0

        def _ln(x, g, b, eps=1e-05):
            mu = jnp.mean(x, axis=-1, keepdims=True)
            var = jnp.mean(jnp.square(x - mu), axis=-1, keepdims=True)
            return (x - mu) * jax.lax.rsqrt(var + eps) * g + b
        B, L, C = x.shape
        silu = jax.nn.silu
        q = _ln(silu(x @ Wq).reshape(B, L, H, D), q_g, q_b)
        kv = silu(x @ Wkv)
        k = _ln(kv[..., :C].reshape(B, L, H, D), k_g, k_b).reshape(B, L, C)
        v = kv[..., C:]
        wp = silu(x @ Wwin + bwin)
        width = jax.nn.sigmoid(wp[..., :H]) * MAX_DIST + 0.5
        sharp = jax.nn.sigmoid(wp[..., H:]) * 9.5 + 0.5
        pad_l, pad_r = ((K - 1) // 2, K // 2)
        k_pad = jnp.pad(k, ((0, 0), (pad_l, pad_r), (0, 0)))
        v_pad = jnp.pad(v, ((0, 0), (pad_l, pad_r), (0, 0)))
        rel = jnp.abs(jnp.arange(K, dtype=jnp.float32) - K // 2)
        scores = jnp.stack([jnp.einsum('blhd,blhd->blh', q, k_pad[:, w:w + L].reshape(B, L, H, D)) for w in range(K)], axis=-1) * SCALE
        soft_mask = jax.nn.sigmoid((width[..., None] - rel) * sharp[..., None])
        attn = jax.nn.softmax(scores - (1.0 - soft_mask) * MASK_PENALTY, axis=-1)
        out = sum((attn[..., w][..., None] * v_pad[:, w:w + L].reshape(B, L, H, D) for w in range(K)))
        out = out.reshape(B, L, C)
        return silu(out @ Wout)

    def _L0_xattn_ref(query, key, value):
        import jax, jax.numpy as jnp
        import numpy as np
        import math
        D_KEY = 256
        SCALE = math.sqrt(D_KEY)
        MASK_VAL = 10000000000.0
        scores = jnp.einsum('bqd,bkd->bqk', query, key)
        L = key.shape[1]
        tri = jnp.triu(jnp.ones((L, L), dtype=scores.dtype), k=1) * MASK_VAL
        scores = scores - tri[None, :, :]
        probs = jax.nn.softmax(scores / SCALE, axis=-1)
        return jnp.einsum('bqk,bkd->bqd', probs, value)

    def _L0_ffn_ref(x, router_w, expert_w1, expert_w2):
        import jax, jax.numpy as jnp
        import numpy as np
        HIDDEN = 256
        NUM_EXPERTS = 8
        TOP_K = 2
        FFN = 1024
        BATCH, SEQ = (4, 512)
        B, S, D = x.shape
        xf = x.reshape(-1, D)
        scores = xf @ router_w.T
        top_v, top_i = jax.lax.top_k(scores, TOP_K)
        routing_w = jax.nn.softmax(top_v, axis=-1)
        out = jnp.zeros_like(xf)
        for e in range(NUM_EXPERTS):
            w_e = jnp.sum(jnp.where(top_i == e, routing_w, 0.0), axis=-1)
            h = jax.nn.gelu(xf @ expert_w1[e].T, approximate=False)
            out = out + h @ expert_w2[e].T * w_e[:, None]
        return out.reshape(B, S, D)
    x = _layernorm(x + _L0_attn_ref(x, L0_attn_Wq, L0_attn_Wkv, L0_attn_q_g, L0_attn_q_b, L0_attn_k_g, L0_attn_k_b, L0_attn_Wwin, L0_attn_bwin, L0_attn_Wout), axis=-1)
    x = _layernorm(x + _L0_xattn_ref(x, ctx_1024, ctx_1024), axis=-1)
    x = _layernorm(x + _L0_ffn_ref(x, L0_ffn_router_w, L0_ffn_expert_w1, L0_ffn_expert_w2), axis=-1)
    return x

_drawn_inputs = setup_inputs


def setup_inputs(seed=0):
    import zlib

    import numpy as np

    out = dict(_drawn_inputs(seed))
    spreads = {'L0_attn_q_g': (1.0, 0.2),
     'L0_attn_q_b': (0.0, 0.318),
     'L0_attn_k_g': (1.0, 0.2),
     'L0_attn_k_b': (0.0, 0.8),
     'L0_attn_bwin': (0.0, 0.272)}
    factors = {}
    for name, (base, spread) in spreads.items():
        noise = np.random.default_rng([zlib.crc32(name.encode()), seed]).standard_normal(out[name].shape)
        drawn = base * np.exp(spread * noise) if base else spread * noise
        out[name] = jnp.asarray(drawn.astype(out[name].dtype))
    for name, factor in factors.items():
        out[name] = (out[name] * factor).astype(out[name].dtype)
    return out
```

```python
from contextlib import ExitStack

import concourse.bass as bass
from concourse import mybir

F32 = mybir.dt.float32
I32 = mybir.dt.int32
U32 = mybir.dt.uint32
BF16 = mybir.dt.bfloat16
ALU = mybir.AluOpType
ACT = mybir.ActivationFunctionType
AX = mybir.AxisListType

P = 128
B, L, E = 8, 512, 256
T = B * L
C = E // P
H, D = 16, 16
K = 17
R = K // 2
CHUNK = T // P
ROWS = CHUNK + 2 * R
PER = L // CHUNK
QKVW = 3 * E + 2 * H
EPS = 1e-5
SCALE = D ** -0.5
PENALTY = 1e4
W0 = (K + 1) // 2
WEIGHT_LOADS = 16 * (4 * C + 5 + 2)
QT = L // P
TILES = T // P
MASKED = 1e10
LOW = 10700
N_EXP, TOP, F = 8, 2, 1024
FB = F // P
SLOTS = TOP * T // P + N_EXP
AT_IDENT = 0
AT_REACH = AT_IDENT + P
AT_MASK = AT_REACH + K
AT_BELOW = AT_MASK + P
AT_COUNT = AT_BELOW + P
AT_TILE = AT_COUNT + P
AT_ROW = AT_TILE + TOP * TILES
AT_SPILL = AT_ROW + 1
N_CONST = AT_SPILL + SLOTS


def host_consts():
    import numpy as np
    i, j = np.arange(P)[:, None], np.arange(P)[None, :]
    wide = lambda a: np.broadcast_to(a, (P, len(a)))
    parts = [
        i == j,
        wide(np.abs(np.arange(K) - R)),
        np.where(j > i, -MASKED, 0.0),
        i < j,
        wide(np.arange(P)),
        wide(np.arange(TOP * TILES)),
        i + 1.0,
        TOP * T + P * np.arange(SLOTS)[None, :] + i + 1.0,
    ]
    return np.ascontiguousarray(np.concatenate(parts, axis=1).astype(np.float32))


def steps(eng, n, body, peeled=2):
    for t in range(peeled):
        body(t, t % 2, t // 2)
    with eng.Fori(peeled // 2, n // 2) as i:
        for u in (0, 1):
            body(2 * i + u, u, i)


def past(t, k):
    return not isinstance(t, int) or t >= k


def row(ap, t):
    return ap[:, bass.ds(t, 1)]


def decoder_layer(nc, x, x_steps, ctx, ctx_t, Wq, Wkv, q_g, q_b, k_g, k_b, Wwin, bwin, Wout,
                  router_t, w1_t, w2_t, shape_consts, out):
    stack = ExitStack()
    with stack:
        def sb(name, shape, dt=F32):
            return stack.enter_context(nc.sbuf_tensor(name, shape, dt))

        def sem(name):
            return stack.enter_context(nc.semaphore(name))

        x1_dram = nc.dram_tensor("x1_dram", [T, E], F32, kind="Internal").ap()
        x_chunk = x.rearrange("(p s) e -> p s e", s=CHUNK)
        x1_seq = x1_dram.rearrange("(b l) e -> b l e", l=L)
        x1_chunk = x1_dram.rearrange("(p s) e -> p s e", s=CHUNK)

        big = sb("big", [P, (CHUNK + 2 * ROWS) * E])
        mid = sb("mid", [P, 2 * K * E])
        low = sb("low", [P, LOW])
        low_used = {}

        def carve(region, start, *shape):
            n = 1
            for m in shape:
                n *= m
            names = " ".join("abcd"[:len(shape)])
            ap = region[:, start:start + n]
            if len(shape) > 1:
                ap = ap.rearrange(f"p ({names}) -> p {names}", **dict(zip("abcd", shape)))
            return ap

        def next_low(phase, *shape):
            start = low_used.get(phase, 0)
            n = 1
            for m in shape:
                n *= m
            low_used[phase] = start + n
            assert start + n <= LOW, (phase, start + n)
            return carve(low, start, *shape)

        consts = sb("consts", [P, N_CONST])
        ident = consts[:, AT_IDENT:AT_IDENT + P]
        reach = consts[:, AT_REACH:AT_REACH + K]
        ones_pp = sb("ones_pp", [P, P])
        ones_row = ones_pp[0:1, :]
        b_win = sb("b_win", [1, 2 * H])
        minus_half = sb("minus_half", [P, 2 * H])

        router_w = sb("router_w", [P, C, N_EXP])

        x2_dram = nc.dram_tensor("x2_dram", [T, E], F32, kind="Internal").ap()
        x2_seq = x2_dram.rearrange("(b l) e -> b l e", l=L)
        x2 = carve(mid, 0, TILES, E)
        ctx_sb = next_low("cross", 2, QT, E)
        ctx_ts = next_low("cross", 2, C, L)
        x1_n = next_low("cross", 2, QT, E)
        tok_t = next_low("cross", C, L)
        probs = next_low("cross", 2, L)
        probs_t = next_low("cross", 2, QT, P)
        sum2 = next_low("cross", QT, E)
        top_peak = next_low("cross", 2, QT)
        bias2 = next_low("cross", 2, QT)
        row_sum = next_low("cross", 2, QT)
        inv_row = next_low("cross", 2, QT)
        stats2 = next_low("cross", 2, QT, 6)
        mean2 = next_low("cross", 2, QT)
        rstd2 = next_low("cross", 2, QT)
        logits = next_low("cross", 2, QT, N_EXP)
        top8 = next_low("cross", 2, QT, 8)
        where8 = next_low("cross", 2, QT, 8)

        keep_at = TILES * E
        slot_src = carve(mid, keep_at, SLOTS).bitcast(I32)
        slot_dst = carve(mid, keep_at + SLOTS, SLOTS).bitcast(I32)
        slot_exp = carve(mid, keep_at + 2 * SLOTS, SLOTS).bitcast(I32)
        top_v = carve(mid, keep_at + 3 * SLOTS, TOP, TILES)
        top_i = carve(mid, keep_at + 3 * SLOTS + TOP * TILES, TOP, TILES)
        chosen = next_low("route", TOP, TILES, N_EXP)
        picked = next_low("route", TILES, N_EXP)
        upto = [next_low("route", TILES, N_EXP) for _ in range(2)]
        place = next_low("route", TILES, N_EXP)
        placed = next_low("route", TOP, TILES, N_EXP)
        is_row = carve(low, 0, TOP * TILES, P // 2).bitcast(BF16)
        low_used["route"] = TOP * TILES * P // 2
        lots = next_low("route", 2, N_EXP)
        lots_n = next_low("route", N_EXP)
        lots_i = next_low("route", N_EXP).bitcast(I32)
        spot = next_low("route", TOP, TILES)
        spot_i = next_low("route", 2, TOP, TILES).bitcast(I32)
        spot_row = next_low("route", TOP * TILES)
        spot_slot = next_low("route", TOP * TILES)
        slot_past = next_low("route", SLOTS, N_EXP)
        slot_f = next_low("route", 4, SLOTS)
        is_slot = next_low("route", TOP * TILES, SLOTS).bitcast(BF16)

        ys_dram = nc.dram_tensor("ys_dram", [(TOP * TILES + SLOTS) * P, E], F32, kind="Internal").ap()
        ys_group = ys_dram[0:TOP * T, :].rearrange("(g l) e -> g l e", l=QT * P)
        out_group = out.rearrange("(g l) e -> g l e", l=QT * P)
        w1_sb = carve(big, 0, N_EXP, C, F)
        w2_sb = carve(big, N_EXP * C * F, N_EXP, FB, E)
        src_col = next_low("experts", 2, 1).bitcast(I32)
        dst_col = next_low("experts", 2, 1).bitcast(I32)
        rows = next_low("experts", 2, E)
        rows_t = next_low("experts", 2, C, P)
        hid = next_low("experts", 2, F)
        hid_t = next_low("experts", 2, FB, P)
        y_rows = next_low("experts", 2, E)

        y_pick = [next_low("end", 2, QT, E) for _ in range(TOP)]
        sum3 = next_low("end", 2, QT, E)
        stats3 = next_low("end", 2, QT, 6)
        mean3 = next_low("end", 2, QT)
        rstd3 = next_low("end", 2, QT)

        q_all = carve(big, 0, CHUNK, E)
        k_all = carve(big, CHUNK * E, ROWS, E)
        v_all = carve(big, (CHUNK + ROWS) * E, ROWS, E)
        qk_prod = mid[:, 0:K * E]
        av_prod = [carve(mid, K * E, W0, E), carve(mid, (K + W0) * E, K - W0, E)]
        act_qk = carve(mid, 0, 2, 2 * E)
        cen_qk = carve(mid, 4 * E, 2, 2 * E)
        sq_qk = carve(mid, 8 * E, 2, 2 * E)
        head_var = carve(mid, 12 * E, CHUNK, 2 * H)
        head_rstd = carve(mid, 16 * E, CHUNK, 2 * H)
        newton = carve(mid, 20 * E, CHUNK, 2 * H)
        w_in = next_low("window", C, QKVW)
        x_step = next_low("window", 2, C, P)
        win = next_low("window", CHUNK, 2 * H)
        gains = next_low("window", 2, D)
        head_sum = next_low("window", 2, 2 * H)
        gate = carve(low, 0, CHUNK, R + 1, H)
        low_used["window"] = CHUNK * (R + 1) * H
        w_out = next_low("window", C, E)
        biases = next_low("window", 2, D)
        sharp = next_low("window", CHUNK, H)
        edge = next_low("window", CHUNK, H)
        stats = next_low("window", CHUNK, 6)
        mean1 = next_low("window", CHUNK)
        rstd1 = next_low("window", CHUNK)
        score = next_low("window", 2, K * H)
        prob = next_low("window", 2, K * H)
        peak = next_low("window", 2, H)
        total = next_low("window", 2, H)
        inv_total = next_low("window", 2, H)
        mixed_t = next_low("window", 2, C, P)
        tanh_y = next_low("window", 2, E)
        x_res = next_low("window", 2, E)
        res = next_low("window", 2, E)
        bn6 = next_low("window", 2, 6)
        mean1 = next_low("window", CHUNK)

        psum = stack.enter_context(nc.psum_tensor("psum", [P, 8, 512], F32))

        weights_loaded = sem("weights_loaded")
        fills_made = sem("fills_made")
        halo_zeroed = sem("halo_zeroed")
        x_step_loaded = [sem("x_step_loaded0"), sem("x_step_loaded1")]
        qkv_done = sem("qkv_done")
        silu_done = sem("silu_done")
        centred = sem("centred")
        squared = sem("squared")
        var_done = sem("var_done")
        halo_loaded = sem("halo_loaded")
        sig_done = sem("sig_done")
        gained = sem("gained")
        var_eps = sem("var_eps")
        root_done = sem("root_done")
        gate_done = sem("gate_done")
        gate_args = sem("gate_args")
        rstd_heads = sem("rstd_heads")
        q_scaled = sem("q_scaled")
        newton_step = sem("newton_step")
        k_scaled = sem("k_scaled")
        k_ready = sem("k_ready")
        q_ready = sem("q_ready")
        width_done = sem("width_done")
        gate_arg = sem("gate_arg")
        score_ready = sem("score_ready")
        exp_done = sem("exp_done")
        inv_ready = sem("inv_ready")
        prob_ready = sem("prob_ready")
        av_ready = sem("av_ready")
        av_used = sem("av_used")
        mixed_done = sem("mixed_done")
        mixed_copied = sem("mixed_copied")
        y_done = sem("y_done")
        tanh_done = sem("tanh_done")
        x_res_loaded = [sem("x_res_loaded0"), sem("x_res_loaded1")]
        res_done = sem("res_done")
        res_kept = sem("res_kept")
        mean_diff = sem("mean_diff")
        mean_diff_sq = sem("mean_diff_sq")
        mean_added = sem("mean_added")
        var_between = sem("var_between")
        var_even = sem("var_even")
        var_made = sem("var_made")
        rstd_ready = sem("rstd_ready")
        x1_ready = sem("x1_ready")
        x1_stored = sem("x1_stored")
        prob_made = sem("prob_made")
        head_mean_summed = sem("head_mean_summed")
        silu_y_made = sem("silu_y_made")
        res_summed = sem("res_summed")
        qk_multiplied = sem("qk_multiplied")
        qk_summed = sem("qk_summed")
        penalised = sem("penalised")
        peak_found = sem("peak_found")
        total_found = sem("total_found")

        pool_waited = sem("pool_waited")
        dve_waited = sem("dve_waited")
        normed2 = sem("normed2")
        stats2_done = sem("stats2_done")
        stats3_done = sem("stats3_done")
        slot_hits = sem("slot_hits")
        x1t_done = sem("x1t_done")
        tok_copied = sem("tok_copied")
        s_done = sem("s_done")
        peak_ready = sem("peak_ready")
        masked = sem("masked")
        peak_neg = sem("peak_neg")
        exp2_done = sem("exp2_done")
        pt_done = sem("pt_done")
        pt_copied = sem("pt_copied")
        av_done = sem("av_done")
        inv2_made = sem("inv2_made")
        sum2_done = sem("sum2_done")
        x2_ready = sem("x2_ready")
        x2t_done = sem("x2t_done")
        x2t_copied = sem("x2t_copied")
        router_done = sem("router_done")
        logits_copied = sem("logits_copied")
        top_found = sem("top_found")
        where_found = sem("where_found")
        top_kept = sem("top_kept")
        w_loaded = sem("w_loaded")
        gap_made = sem("gap_made")
        gap_exp = sem("gap_exp")
        gap_plus1 = sem("gap_plus1")
        gate1_made = sem("gate1_made")
        gates_made = sem("gates_made")
        chosen_made = sem("chosen_made")
        picked_made = sem("picked_made")
        counted = sem("counted")
        tile_sums = sem("tile_sums")
        scan_step = sem("scan_step")
        place_made = sem("place_made")
        lots_step = sem("lots_step")
        placed_made = sem("placed_made")
        spot_made = sem("spot_made")
        spot_int = sem("spot_int")
        spot_parts = sem("spot_parts")
        spot_back = sem("spot_back")
        rows_marked = sem("rows_marked")
        slots_marked = sem("slots_marked")
        table_done = sem("table_done")
        slot_step = sem("slot_step")
        routed = sem("routed")
        past_made = sem("past_made")
        src_copied = sem("src_copied")
        dst_copied = sem("dst_copied")
        rows_t_done = sem("rows_t_done")
        rows_t_copied = sem("rows_t_copied")
        up_done = sem("up_done")
        gelu_done = sem("gelu_done")
        hid_t_done = sem("hid_t_done")
        hid_t_copied = sem("hid_t_copied")
        down_done = sem("down_done")
        y_copied = sem("y_copied")
        mix1_done = sem("mix1_done")
        mix2_done = sem("mix2_done")
        out_ready = sem("out_ready")
        ctx_loaded = [sem("ctx_loaded0"), sem("ctx_loaded1")]
        out_stored = [sem("out_stored0"), sem("out_stored1")]
        rows_loaded = [sem("rows_loaded0"), sem("rows_loaded1")]
        x2_stored = [sem("x2_stored0"), sem("x2_stored1")]
        y_loaded = [sem("y_loaded0"), sem("y_loaded1")]
        ys_stored = [sem("ys_stored0"), sem("ys_stored1")]

        block = stack.enter_context(nc.Block())

        @block.sync
        def _(sp):
            sp.dma_start(consts[:, :], shape_consts).then_inc(weights_loaded, 16)
            for c in range(C):
                for w, a in ((Wq, 0), (Wkv, E), (Wwin, 3 * E)):
                    sp.dma_start(w_in[:, c, a:a + w.shape[1]], w[c * P:(c + 1) * P, :]).then_inc(weights_loaded, 16)
                sp.dma_start(w_out[:, c, :], Wout[c * P:(c + 1) * P, :]).then_inc(weights_loaded, 16)
            sp.dma_start(router_w[:, :, :], router_t.rearrange("(c p) n -> p c n", p=P)).then_inc(weights_loaded, 16)
            for m, (g, b) in enumerate(((q_g, q_b), (k_g, k_b))):
                sp.dma_start(gains[:, m, :], g.partition_broadcast(P)).then_inc(weights_loaded, 16)
                sp.dma_start(biases[:, m, :], b.partition_broadcast(P)).then_inc(weights_loaded, 16)
            sp.dma_start(b_win[:, :], bwin.rearrange("(a n) -> a n", a=1)).then_inc(weights_loaded, 16)

            def load_x_step(t, u, i):
                if past(t, 2):
                    sp.wait_ge(qkv_done, t - 1)
                src = x_steps[bass.ds(t, 1)].rearrange("a (c q) p -> q (a c) p", q=P)
                sp.dma_start(x_step[:, u], src).then_inc(x_step_loaded[u], 16)
            steps(sp, CHUNK, load_x_step)

            sp.wait_ge(halo_zeroed, 4)
            sp.wait_ge(silu_done, CHUNK)
            for kv in (v_all, k_all):
                if kv is k_all:
                    sp.wait_ge(k_ready, 1)
                for b in range(B):
                    a, z = b * PER, (b + 1) * PER
                    sp.dma_start(kv[a + 1:z, 0:R, :], kv[a:z - 1, CHUNK:CHUNK + R, :]).then_inc(halo_loaded, 16)
                    sp.dma_start(kv[a:z - 1, R + CHUNK:ROWS, :], kv[a + 1:z, R:2 * R, :]).then_inc(halo_loaded, 16)

            def load_x_res(t, u, i):
                if past(t, 2):
                    sp.wait_ge(res_done, t - 1)
                sp.dma_start(x_res[:, u, :], x_chunk[:, bass.ds(t, 1), :].rearrange("p a e -> p (a e)")).then_inc(x_res_loaded[u], 16)
            steps(sp, CHUNK, load_x_res)

            for g in range(4):
                n = CHUNK // 4
                sp.wait_ge(x1_ready, n * (g + 1))
                sp.dma_start(x1_chunk[:, g * n:(g + 1) * n, :], q_all[:, g * n:(g + 1) * n, :]).then_inc(x1_stored, 16)
            sp.wait_ge(x1_stored, 64)

            def load_sequence(b, u, i):
                if past(b, 2):
                    sp.wait_ge(sum2_done, QT * (b - 1))
                rows_of = "a (t p) e -> p (a t) e"
                sp.dma_start(x1_n[:, u], x1_seq[bass.ds(b, 1)].rearrange(rows_of, p=P)).then_inc(ctx_loaded[u], 16)
                sp.dma_start(ctx_ts[:, u], ctx_t[bass.ds(b, 1)].rearrange("a (c p) l -> p (a c) l", p=P)).then_inc(ctx_loaded[u], 16)
                sp.dma_start(ctx_sb[:, u], ctx[bass.ds(b, 1)].rearrange(rows_of, p=P)).then_inc(ctx_loaded[u], 16)
                sp.dma_start(w1_sb[:, bass.ds(b, 1)].rearrange("p a c f -> p (a c) f"),
                             w1_t[bass.ds(b, 1)].rearrange("a (c p) f -> p (a c) f", p=P)).then_inc(w_loaded, 16)
                sp.dma_start(w2_sb[:, bass.ds(b, 1)].rearrange("p a j e -> p (a j) e"),
                             w2_t[bass.ds(b, 1)].rearrange("a (j p) e -> p (a j) e", p=P)).then_inc(w_loaded, 16)
                if past(b, 1):
                    store_x2(b - 1, 1 - u)

            def store_x2(b, u):
                sp.wait_ge(x2_ready, QT * (b + 1))
                sp.dma_start(x2_seq[bass.ds(b, 1)].rearrange("a (t p) e -> p (a t) e", p=P),
                             x2[:, bass.ds(QT * b, QT), :]).then_inc(x2_stored[u], 16)
            steps(sp, B, load_sequence)
            store_x2(B - 1, 1)

            def load_picked(g, u, i):
                if past(g, 2):
                    sp.wait_ge(mix2_done, QT * (g - 1))
                for k in range(TOP):
                    sp.dma_start(y_pick[k][:, u], ys_group[bass.ds(k * (TILES // QT) + g, 1)].rearrange(
                        "a (t p) e -> p (a t) e", p=P)).then_inc(y_loaded[u], 16)
                if past(g, 1):
                    store_out(g - 1, 1 - u)

            def store_out(g, u):
                sp.wait_ge(out_ready, QT * (g + 1))
                sp.dma_start(out_group[bass.ds(g, 1)].rearrange("a (t p) e -> p (a t) e", p=P),
                             sum3[:, u]).then_inc(out_stored[u], 16)
            for u in (0, 1):
                sp.wait_ge(ys_stored[u], 16 * (SLOTS // 2))
            steps(sp, TILES // QT, load_picked)
            store_out(TILES // QT - 1, 1)
            for u in (0, 1):
                sp.wait_ge(out_stored[u], 16 * (TILES // QT // 2))

        @block.tensor
        def _(pe):
            pe.wait_ge(weights_loaded, WEIGHT_LOADS)
            pe.wait_ge(fills_made, 2)

            def project(t, u, i):
                pe.wait_ge(x_step_loaded[u], 16 * i + 16)
                if past(t, 2):
                    pe.wait_ge(silu_done, t - 1)
                for c in range(C):
                    nc.tensor.matmul(psum[:, u, :], x_step[:, u, c, :], w_in[:, c, 0:512],
                                     start=(c == 0), stop=(c == C - 1))
                for c in range(C):
                    nc.tensor.matmul(psum[:, 2 + u, 0:QKVW - 512], x_step[:, u, c, :], w_in[:, c, 512:QKVW],
                                     start=(c == 0), stop=False, skip_group_check=True)
                nc.tensor.matmul(psum[:, 2 + u, E:E + 2 * H], ones_row, b_win[:, :],
                                 start=False, stop=True, skip_group_check=True).then_inc(qkv_done, 1)
            steps(pe, CHUNK, project)
            pe.wait_ge(silu_done, CHUNK)

            def mix(t, u, i):
                if past(t, 2):
                    pe.wait_ge(mixed_copied, t - 1)
                for half, (a, n) in enumerate(((0, W0), (W0, K - W0))):
                    pe.wait_ge(av_ready, 2 * t + half + 1)
                    for w in range(n):
                        for c in range(C):
                            last = nc.tensor.matmul(psum[:, 2 * u + c, 0:P], av_prod[half][:, w, c * P:(c + 1) * P],
                                                    ident, start=(a + w == 0), stop=(a + w == K - 1))
                    last.then_inc(av_used, 1)
                pe.wait_ge(mixed_copied, t + 1)
                if past(t, 2):
                    pe.wait_ge(res_done, t - 1)
                for c in range(C):
                    last = nc.tensor.matmul(psum[:, 4 + u, 0:E], mixed_t[:, u, c, :], w_out[:, c, :],
                                            start=(c == 0), stop=(c == C - 1))
                last.then_inc(y_done, 1)
            steps(pe, CHUNK, mix, 4)
            pe.wait_ge(tanh_done, CHUNK)

            def attend(b, u, i):
                pe.wait_ge(ctx_loaded[u], 48 * i + 48)
                if past(b, 1):
                    pe.wait_ge(sum2_done, QT * b)
                for c in range(C):
                    for t in range(QT):
                        last = nc.tensor.transpose(psum[:, 6 + c, t * P:(t + 1) * P], x1_n[:, u, t, c * P:(c + 1) * P], ident)
                last.then_inc(x1t_done, 1)
                pe.wait_ge(tok_copied, 2 * b + 2)
                for t in range(QT):
                    if past(b, 1):
                        pe.wait_ge(exp2_done, QT * b - QT + t + 1)
                    for c in range(C):
                        last = nc.tensor.matmul(psum[:, t, 0:(t + 1) * P], tok_t[:, c, t * P:(t + 1) * P],
                                                ctx_ts[:, u, c, 0:(t + 1) * P], start=(c == 0), stop=(c == C - 1))
                    last.then_inc(s_done, 1)
                if past(b, 1):
                    route(b - 1)
                for t in range(QT + 1):
                    if t < QT:
                        pe.wait_ge(exp2_done, QT * b + t + 1)
                        if t >= 2:
                            pe.wait_ge(pt_copied, QT * b + t - 1)
                        elif past(b, 1):
                            pe.wait_ge(pt_copied, QT * b + t - 1)
                            pe.wait_ge(logits_copied, b)
                        for k in range(t + 1):
                            last = nc.tensor.transpose(psum[:, 4 + t % 2, k * P:(k + 1) * P],
                                                       probs[:, t % 2, k * P:(k + 1) * P], ident)
                        last.then_inc(pt_done, 1)
                    if t:
                        q = t - 1
                        pe.wait_ge(pt_copied, QT * b + q + 1)
                        if q >= 2:
                            pe.wait_ge(sum2_done, QT * b + q - 1)
                        for k in range(q + 1):
                            last = nc.tensor.matmul(psum[:, 6 + q % 2, 0:E], probs_t[:, q % 2, k, :], ctx_sb[:, u, k, :],
                                                    start=(k == 0), stop=(k == q))
                        last.then_inc(av_done, 1)

            def route(b):
                pe.wait_ge(x2_ready, QT * (b + 1))
                for c in range(C):
                    for t in range(QT):
                        last = nc.tensor.transpose(psum[:, 6 + c, t * P:(t + 1) * P],
                                                   sum2[:, t, c * P:(c + 1) * P], ident)
                last.then_inc(x2t_done, 1)
                pe.wait_ge(x2t_copied, 2 * b + 2)
                for t in range(QT):
                    for c in range(C):
                        last = nc.tensor.matmul(psum[:, 5, t * N_EXP:(t + 1) * N_EXP], tok_t[:, c, t * P:(t + 1) * P],
                                                router_w[:, c, :], start=(c == 0), stop=(c == C - 1))
                last.then_inc(router_done, 1)
            steps(pe, B, attend)
            pe.wait_ge(sum2_done, T // P)
            route(B - 1)

            pe.wait_ge(picked_made, 1)
            nc.tensor.matmul(psum[:, 0, 0:TILES * N_EXP], consts[:, AT_BELOW:AT_BELOW + P],
                             picked.rearrange("p t n -> p (t n)"), start=True, stop=True)
            nc.tensor.matmul(psum[:, 1, 0:TILES * N_EXP], ones_pp[:, :],
                             picked.rearrange("p t n -> p (t n)"), start=True, stop=True).then_inc(counted, 1)
            pe.wait_ge(rows_marked, 1)
            pe.wait_ge(slots_marked, 2)
            for j in range(TOP * TILES):
                last = nc.tensor.matmul(psum[:, 2, 0:2 * SLOTS], is_row[:, j, :], is_slot[:, j, :],
                                        start=(j == 0), stop=(j == TOP * TILES - 1))
            last.then_inc(table_done, 1)

            pe.wait_ge(routed, 1)
            pe.wait_ge(w_loaded, 32 * N_EXP)

            def transpose_rows(s, u, i):
                pe.wait_ge(rows_loaded[u], 16 * i + 16)
                if past(s, 1):
                    pe.wait_ge(rows_t_copied, s)
                for c in range(C):
                    last = nc.tensor.transpose(psum[:, 0, c * P:(c + 1) * P], rows[:, u, c * P:(c + 1) * P], ident)
                last.then_inc(rows_t_done, 1)

            def expert(s):
                return pe.value_load(slot_exp[0:1, bass.ds(s, 1)], min_val=0, max_val=N_EXP - 1)

            def up(s, u, e):
                pe.wait_ge(rows_t_copied, s + 1)
                if past(s, 1):
                    pe.wait_ge(gelu_done, s)
                for h in range(2):
                    for c in range(C):
                        last = nc.tensor.matmul(psum[:, 2 + h, :], rows_t[:, u, c, :],
                                                w1_sb[:, bass.ds(e, 1), c, h * 512:(h + 1) * 512].rearrange("p a f -> p (a f)"),
                                                start=(c == 0), stop=(c == C - 1))
                last.then_inc(up_done, 1)

            def transpose_hidden(s, u):
                pe.wait_ge(gelu_done, s + 1)
                if past(s, 1):
                    pe.wait_ge(hid_t_copied, 2 * s)
                for j in range(FB):
                    last = nc.tensor.transpose(psum[:, 4 + j // 4, j % 4 * P:(j % 4 + 1) * P], hid[:, u, j * P:(j + 1) * P], ident)
                last.then_inc(hid_t_done, 1)

            def down(s, u, e):
                pe.wait_ge(hid_t_copied, 2 * s + 2)
                if past(s, 1):
                    pe.wait_ge(y_copied, s)
                for j in range(FB):
                    last = nc.tensor.matmul(psum[:, 6, 0:E], hid_t[:, u, j, :],
                                            w2_sb[:, bass.ds(e, 1), j, :].rearrange("p a e -> p (a e)"),
                                            start=(j == 0), stop=(j == FB - 1))
                last.then_inc(down_done, 1)

            def lot(s, u, i):
                e = expert(s)
                if past(s, 1):
                    e_before = expert(s - 1)
                    transpose_hidden(s - 1, 1 - u)
                transpose_rows(s, u, i)
                up(s, u, e)
                if past(s, 1):
                    down(s - 1, 1 - u, e_before)
            steps(pe, SLOTS, lot, 4)
            transpose_hidden(SLOTS - 1, 1)
            down(SLOTS - 1, 1, expert(SLOTS - 1))

        @block.scalar
        def _(act):
            def square(t, u):
                act.wait_ge(centred, t + 1)
                if past(t, 2):
                    act.wait_ge(var_done, t - 1)
                nc.scalar.activation(sq_qk[:, u, :], cen_qk[:, u, :], ACT.Square).then_inc(squared, 1)

            def silu(t, u, i):
                act.wait_ge(qkv_done, t + 1)
                if past(t, 2):
                    act.wait_ge(centred, t - 1)
                nc.scalar.activation(act_qk[:, u, :], psum[:, u, :], ACT.Silu)
                nc.scalar.activation(row(v_all, t + R), psum[:, 2 + u:3 + u, 0:E], ACT.Silu)
                nc.scalar.activation(row(win, t), psum[:, 2 + u:3 + u, E:E + 2 * H], ACT.Silu).then_inc(silu_done, 1)
                if past(t, 1):
                    square(t - 1, 1 - u)
            steps(act, CHUNK, silu, 4)
            square(CHUNK - 1, 1)
            act.wait_ge(silu_done, CHUNK)
            nc.scalar.activation(win[:, :, :], win[:, :, :], ACT.Sigmoid).then_inc(sig_done, 1)
            act.wait_ge(var_eps, 1)
            nc.scalar.activation(head_rstd[:, :, :], head_var[:, :, :], ACT.Sqrt).then_inc(root_done, 1)
            act.wait_ge(gate_arg, 1)
            nc.scalar.activation(gate[:, :, :, :], gate[:, :, :, :], ACT.Sigmoid).then_inc(gate_done, 1)

            def mixed_out(t, u):
                act.wait_ge(av_used, 2 * t + 2)
                if past(t, 2):
                    act.wait_ge(y_done, t - 1)
                nc.scalar.activation(mixed_t[:, u], psum[:, 2 * u:2 * u + 2, 0:P], ACT.Copy).then_inc(mixed_copied, 1)
                act.wait_ge(y_done, t + 1)
                if past(t, 2):
                    act.wait_ge(res_done, t - 1)
                nc.scalar.activation(tanh_y[:, u, :], psum[:, 4 + u, 0:E], ACT.Tanh, scale=0.5).then_inc(tanh_done, 1)

            def window(t, u, i):
                act.wait_ge(score_ready, t + 1)
                nc.scalar.activation(score[:, u, :], score[:, u, :], ACT.Exp, scale=SCALE).then_inc(exp_done, 1)
                if past(t, 2):
                    keep(t - 2, u)
                if past(t, 1):
                    mixed_out(t - 1, 1 - u)

            def keep(t, u):
                act.wait_ge(res_done, t + 1)
                nc.scalar.activation(row(q_all, t), res[:, u:u + 1, :], ACT.Copy)
                nc.scalar.activation(row(stats, t), bn6[:, u:u + 1, :], ACT.Copy).then_inc(res_kept, 1)
            steps(act, CHUNK, window, 4)
            keep(CHUNK - 2, 0)
            mixed_out(CHUNK - 1, 1)
            keep(CHUNK - 1, 1)

            def attend(b, u, i):
                act.wait_ge(x1t_done, b + 1)
                if past(b, 2):
                    act.wait_ge(router_done, b - 1)
                nc.scalar.activation(tok_t[:, 0, :], psum[:, 6, :], ACT.Copy).then_inc(tok_copied, 1)

                def exp(t):
                    act.wait_ge(peak_ready, QT * b + t + 1)
                    if t >= 2:
                        act.wait_ge(pt_done, QT * b + t - 1)
                    elif past(b, 1):
                        act.wait_ge(pt_done, QT * b + t - 1)
                    nc.scalar.activation(probs[:, t % 2, 0:(t + 1) * P], psum[:, t, 0:(t + 1) * P], ACT.Exp,
                                         bias=bias2[:, u, t:t + 1], scale=1.0 / E ** 0.5,
                                         accum_out=row_sum[:, u, t:t + 1]).then_inc(exp2_done, 1)

                def copy(t):
                    act.wait_ge(pt_done, QT * b + t + 1)
                    if t >= 2:
                        act.wait_ge(av_done, QT * b + t - 1)
                    elif past(b, 1):
                        act.wait_ge(av_done, QT * b + t - 1)
                    nc.scalar.activation(probs_t[:, t % 2, 0:t + 1, :], psum[:, 4 + t % 2, 0:(t + 1) * P].rearrange(
                        "p (k n) -> p k n", n=P), ACT.Copy).then_inc(pt_copied, 1)
                exp(0)
                exp(1)
                if past(b, 1):
                    x2_transposed(b - 1)
                copy(0)
                exp(2)
                copy(1)
                exp(3)
                copy(2)
                copy(3)

            def x2_transposed(b):
                act.wait_ge(x2t_done, b + 1)
                nc.scalar.activation(tok_t[:, 0, :], psum[:, 6, :], ACT.Copy).then_inc(x2t_copied, 1)
            act.wait_ge(x1_ready, CHUNK)
            steps(act, B, attend)
            x2_transposed(B - 1)

            act.wait_ge(gap_made, 1)
            nc.scalar.activation(top_v[:, 1, :], top_v[:, 1, :], ACT.Exp).then_inc(gap_exp, 1)

            def lot(s, u, i):
                act.wait_ge(rows_t_done, s + 1)
                if past(s, 2):
                    act.wait_ge(up_done, s - 1)
                nc.scalar.activation(rows_t[:, u].rearrange("p c n -> p (c n)"), psum[:, 0, 0:E], ACT.Copy).then_inc(rows_t_copied, 1)
                if past(s, 1):
                    hidden_out(s - 1, 1 - u)
                act.wait_ge(up_done, s + 1)
                if past(s, 2):
                    act.wait_ge(hid_t_done, s - 1)
                nc.scalar.activation(hid[:, u, :].rearrange("p (h f) -> p h f", h=2), psum[:, 2:4, :], ACT.Gelu).then_inc(gelu_done, 1)

            def hidden_out(s, u):
                act.wait_ge(hid_t_done, s + 1)
                if past(s, 2):
                    act.wait_ge(down_done, s - 1)
                nc.scalar.activation(hid_t[:, u, 0:4, :].rearrange("p j n -> p (j n)"), psum[:, 4, :], ACT.Copy).then_inc(hid_t_copied, 1)
            act.wait_ge(routed, 1)
            steps(act, SLOTS, lot, 4)
            hidden_out(SLOTS - 1, 1)

        @block.gpsimd
        def _(pool):
            def done(ins, signal, count):
                ins.then_inc(signal, 1)
                pool.wait_ge(signal, count)

            nc.gpsimd.memset(k_all[:, 0:R, :], 0.0).then_inc(halo_zeroed, 1)
            nc.gpsimd.memset(k_all[:, R + CHUNK:ROWS, :], 0.0).then_inc(halo_zeroed, 1)
            nc.gpsimd.memset(v_all[:, 0:R, :], 0.0).then_inc(halo_zeroed, 1)
            nc.gpsimd.memset(v_all[:, R + CHUNK:ROWS, :], 0.0).then_inc(halo_zeroed, 1)
            nc.gpsimd.memset(ones_pp[:, :], 1.0).then_inc(fills_made, 1)
            nc.gpsimd.memset(minus_half[:, :], -0.5).then_inc(fills_made, 1)
            pool.wait_ge(fills_made, 2)

            def gain_qk(t, u, i):
                pool.wait_ge(centred, t + 1)
                for m, dst in enumerate((row(q_all, t), row(k_all, t + R))):
                    heads = cen_qk[:, u, m * E:(m + 1) * E].rearrange("p (h d) -> p h d", d=D)
                    nc.gpsimd.tensor_tensor(dst.rearrange("p a (h d) -> p (a h) d", d=D), heads,
                                            gains[:, m:m + 1, :].to_broadcast([P, H, D]), ALU.mult).then_inc(gained, 1)

            pool.wait_ge(weights_loaded, WEIGHT_LOADS)
            steps(pool, CHUNK, gain_qk)
            pool.wait_ge(gained, 2 * CHUNK)
            pool.wait_ge(rstd_heads, 1)
            for g in range(2):
                part = q_all[:, g * CHUNK // 2:(g + 1) * CHUNK // 2, :].rearrange("p s (h d) -> p s h d", d=D)
                scale = head_rstd[:, g * CHUNK // 2:(g + 1) * CHUNK // 2, 0:H].unsqueeze(3)
                nc.gpsimd.tensor_tensor(part, part, scale.to_broadcast([P, CHUNK // 2, H, D]), ALU.mult).then_inc(q_scaled, 1)
            pool.wait_ge(gate_done, 1)

            def weigh_values(t, u):
                pool.wait_ge(inv_ready, t + 1)
                done(nc.gpsimd.tensor_tensor(prob[:, u, :].rearrange("p (w h) -> p w h", h=H),
                                             score[:, u, :].rearrange("p (w h) -> p w h", h=H),
                                             inv_total[:, u, :].unsqueeze(1).to_broadcast([P, K, H]), ALU.mult), prob_made, t + 1)
                for half, (a, n) in enumerate(((0, W0), (W0, K - W0))):
                    if past(t, 1):
                        pool.wait_ge(av_used, 2 * t + half - 1)
                    values = v_all[:, bass.ds(t + a, n), :].rearrange("p w (h d) -> p (w h) d", d=D)
                    weights = prob[:, u, a * H:(a + n) * H].unsqueeze(2).to_broadcast([P, n * H, D])
                    nc.gpsimd.tensor_tensor(av_prod[half][:, :, :].rearrange("p w (h d) -> p (w h) d", d=D),
                                            values, weights, ALU.mult).then_inc(av_ready, 1)

            steps(pool, CHUNK, lambda t, u, i: weigh_values(t, u))

            def root(var, n, count):
                pool.wait_ge(var_made, count)
                nc.gpsimd.tensor_tensor(var, var, minus_half[:, 0:n], ALU.pow).then_inc(rstd_ready, 1)
            root(rstd1[:, :], CHUNK, 1)
            steps(pool, B, lambda b, u, i: root(rstd2[:, u, :], QT, b + 2))

            pool.wait_ge(routed, 1)
            for u in (0, 1):
                pool.wait_ge(x2_stored[u], 16 * (B // 2))

            def lot(s, u, i):
                if past(s, 2):
                    pool.wait_ge(rows_t_done, s - 1)
                nc.gpsimd.tensor_copy(src_col[:, u, :], slot_src[:, bass.ds(s, 1)]).then_inc(src_copied, 1)
                pool.wait_ge(src_copied, s + 1).then_inc(pool_waited, 1)
                nc.gpsimd.indirect_dma_start(rows[:, u, :], None, x2_dram, bass.IndirectOffsetOnAxis(src_col[:, u, :], 0)
                                             ).then_inc(rows_loaded[u], 16)
                if past(s, 2):
                    send(s - 2, u, i - 1)

            def send(s, u, i):
                pool.wait_ge(y_copied, s + 1)
                if past(s, 2):
                    pool.wait_ge(ys_stored[u], 16 * i)
                nc.gpsimd.tensor_copy(dst_col[:, u, :], slot_dst[:, bass.ds(s, 1)]).then_inc(dst_copied, 1)
                pool.wait_ge(dst_copied, s + 1).then_inc(pool_waited, 1)
                nc.gpsimd.indirect_dma_start(ys_dram, bass.IndirectOffsetOnAxis(dst_col[:, u, :], 0), y_rows[:, u, :], None
                                             ).then_inc(ys_stored[u], 16)
            steps(pool, SLOTS, lot, 4)
            send(SLOTS - 2, 0, SLOTS // 2 - 1)
            send(SLOTS - 1, 1, SLOTS // 2 - 1)
            steps(pool, TILES // QT, lambda g, u, i: root(rstd3[:, u, :], QT, g + B + 2))

        @block.vector
        def _(dve):
            def done(ins, signal, count):
                ins.then_inc(signal, 1)
                dve.wait_ge(signal, count)

            def moments(st, mean, var, count):
                done(nc.vector.tensor_tensor(mean, st[:, :, 1], st[:, :, 4], ALU.subtract), mean_diff, count + 1)
                done(nc.vector.tensor_tensor(var, mean, mean, ALU.mult), mean_diff_sq, count + 1)
                nc.vector.tensor_tensor(mean, st[:, :, 1], st[:, :, 4], ALU.add).then_inc(mean_added, 1)
                done(nc.vector.tensor_scalar(var, var, 0.25, EPS, ALU.mult, ALU.add), var_between, count + 1)
                done(nc.vector.scalar_tensor_tensor(var, st[:, :, 2], 1.0 / E, var, ALU.mult, ALU.add), var_even, count + 1)
                dve.wait_ge(mean_added, count + 1)
                nc.vector.tensor_scalar(mean, mean, 0.5, None, ALU.mult)
                nc.vector.scalar_tensor_tensor(var, st[:, :, 5], 1.0 / E, var, ALU.mult, ALU.add).then_inc(var_made, 1)

            def variance(t, u):
                dve.wait_ge(squared, t + 1).then_inc(dve_waited, 1)
                nc.vector.tensor_reduce(row(head_var, t).rearrange("p a x -> p (a x)"),
                                        sq_qk[:, u, :].rearrange("p (x d) -> p x d", d=D),
                                        op=ALU.add, axis=AX.X).then_inc(var_done, 1)

            def centre(t, u, i):
                dve.wait_ge(silu_done, t + 1)
                heads = act_qk[:, u, :].rearrange("p (x d) -> p x d", d=D)
                done(nc.vector.tensor_reduce(head_sum[:, u, :], heads, op=ALU.add, axis=AX.X), head_mean_summed, t + 1)
                if past(t, 2):
                    dve.wait_ge(gained, 2 * t - 2)
                nc.vector.scalar_tensor_tensor(cen_qk[:, u, :].rearrange("p (x d) -> p x d", d=D),
                                               head_sum[:, u, :].unsqueeze(2).to_broadcast([P, 2 * H, D]), -1.0 / D, heads,
                                               ALU.mult, ALU.add).then_inc(centred, 1)
                if past(t, 1):
                    variance(t - 1, 1 - u)
            dve.wait_ge(weights_loaded, WEIGHT_LOADS)
            steps(dve, CHUNK, centre, 4)
            variance(CHUNK - 1, 1)

            dve.wait_ge(var_done, CHUNK)
            done(nc.vector.tensor_scalar(head_var[:, :, :], head_var[:, :, :], 1.0 / D, EPS, ALU.mult, ALU.add), var_eps, 1)
            dve.wait_ge(sig_done, 1)
            nc.vector.tensor_scalar(sharp[:, :, :], win[:, :, H:2 * H], 9.5, 0.5, ALU.mult, ALU.add).then_inc(width_done, 1)
            nc.vector.tensor_scalar(edge[:, :, :], win[:, :, 0:H], float(R), 0.5, ALU.mult, ALU.add).then_inc(width_done, 1)
            dve.wait_ge(width_done, 2)
            done(nc.vector.tensor_tensor(edge[:, :, :], edge[:, :, :], sharp[:, :, :], ALU.mult), width_done, 3)
            dve.wait_ge(root_done, 1)
            done(nc.vector.reciprocal(head_rstd[:, :, :], head_rstd[:, :, :]), newton_step, 1)
            done(nc.vector.tensor_tensor(newton[:, :, :], head_var[:, :, :], head_rstd[:, :, :], ALU.mult), newton_step, 2)
            done(nc.vector.tensor_tensor(newton[:, :, :], newton[:, :, :], head_rstd[:, :, :], ALU.mult), newton_step, 3)
            done(nc.vector.tensor_scalar(newton[:, :, :], newton[:, :, :], -0.5, 1.5, ALU.mult, ALU.add), newton_step, 4)
            done(nc.vector.tensor_tensor(head_rstd[:, :, :], head_rstd[:, :, :], newton[:, :, :], ALU.mult), rstd_heads, 1)
            dve.wait_ge(gained, 2 * CHUNK)
            keys = k_all[:, R:R + CHUNK, :].rearrange("p s (h d) -> p s h d", d=D)
            done(nc.vector.tensor_tensor(keys, keys, head_rstd[:, :, H:2 * H].unsqueeze(3).to_broadcast([P, CHUNK, H, D]),
                                         ALU.mult), k_scaled, 1)
            keys = k_all[:, R:R + CHUNK, :].rearrange("p s (h d) -> p (s h) d", d=D)
            nc.vector.tensor_tensor(keys, keys, biases[:, 1:2, :].to_broadcast([P, CHUNK * H, D]), ALU.add).then_inc(k_ready, 1)
            for r in range(R + 1):
                nc.vector.scalar_tensor_tensor(gate[:, :, r, :], sharp[:, :, :], float(r), edge[:, :, :], ALU.mult,
                                               ALU.subtract).then_inc(gate_args, 1)
            dve.wait_ge(gate_args, R + 1).then_inc(gate_arg, 1)
            for g in range(2):
                dve.wait_ge(q_scaled, g + 1)
                part = q_all[:, g * CHUNK // 2:(g + 1) * CHUNK // 2, :].rearrange("p s (h d) -> p (s h) d", d=D)
                nc.vector.tensor_tensor(part, part, biases[:, 0:1, :].to_broadcast([P, CHUNK // 2 * H, D]),
                                        ALU.add).then_inc(q_ready, 1)
            dve.wait_ge(q_ready, 2)
            dve.wait_ge(gate_done, 1)

            def residual(t, u, i):
                dve.wait_ge(tanh_done, t + 1)
                dve.wait_ge(x_res_loaded[u], 16 * i + 16)
                done(nc.vector.scalar_tensor_tensor(tanh_y[:, u, :], tanh_y[:, u, :], 1.0, psum[:, 4 + u, 0:E],
                                                    ALU.add, ALU.mult), silu_y_made, t + 1)
                if past(t, 2):
                    dve.wait_ge(res_kept, t - 1)
                done(nc.vector.scalar_tensor_tensor(res[:, u, :], tanh_y[:, u, :], 0.5, x_res[:, u, :], ALU.mult, ALU.add), res_summed, t + 1)
                nc.vector.bn_stats(bn6[:, u, :], res[:, u, :]).then_inc(res_done, 1)

            def window(t, u, i):
                queries = row(q_all, t).to_broadcast([P, K, E])
                done(nc.vector.tensor_tensor(qk_prod[:, :].rearrange("p (w c) -> p w c", c=E), queries,
                                             k_all[:, bass.ds(t, K), :], ALU.mult), qk_multiplied, t + 1)
                if past(t, 2):
                    dve.wait_ge(prob_made, t - 1)
                done(nc.vector.tensor_reduce(score[:, u, :], qk_prod[:, :].rearrange("p (x d) -> p x d", d=D),
                                             op=ALU.add, axis=AX.X), qk_summed, t + 1)
                by_offset = score[:, u, :].rearrange("p (w h) -> p w h", h=H)
                gates = row(gate, t).rearrange("p a r h -> p (a r) h")
                nc.vector.scalar_tensor_tensor(by_offset[:, R:, :], gates, -PENALTY / SCALE, by_offset[:, R:, :],
                                               ALU.mult, ALU.add).then_inc(penalised, 1)
                nc.vector.scalar_tensor_tensor(by_offset[:, R - 1::-1, :], gates[:, 1:, :], -PENALTY / SCALE,
                                               by_offset[:, R - 1::-1, :], ALU.mult, ALU.add).then_inc(penalised, 1)
                dve.wait_ge(penalised, 2 * t + 2)
                by_head = score[:, u, :].rearrange("p (w h) -> p h w", h=H)
                done(nc.vector.tensor_reduce(peak[:, u, :], by_head, op=ALU.max, axis=AX.X), peak_found, t + 1)
                nc.vector.tensor_tensor(score[:, u, :].rearrange("p (w h) -> p w h", h=H),
                                        score[:, u, :].rearrange("p (w h) -> p w h", h=H),
                                        peak[:, u, :].unsqueeze(1).to_broadcast([P, K, H]),
                                        ALU.subtract).then_inc(score_ready, 1)
                if past(t, 2):
                    residual(t - 2, u, i - 1)
                dve.wait_ge(exp_done, t + 1)
                done(nc.vector.tensor_reduce(total[:, u, :], by_head, op=ALU.add, axis=AX.X), total_found, t + 1)
                nc.vector.reciprocal(inv_total[:, u, :], total[:, u, :]).then_inc(inv_ready, 1)
            dve.wait_ge(halo_loaded, 16 * 4 * B)
            steps(dve, CHUNK, window, 4)
            residual(CHUNK - 2, 0, CHUNK // 2 - 1)
            residual(CHUNK - 1, 1, CHUNK // 2 - 1)

            dve.wait_ge(res_kept, CHUNK)
            moments(stats, mean1, rstd1, 0)
            dve.wait_ge(rstd_ready, 1)

            def norm1(t, u, i):
                dst = q_all[:, bass.ds(t, 1), :].rearrange("p a e -> p (a e)")
                nc.vector.tensor_scalar(dst, dst, mean1[:, bass.ds(t, 1)], rstd1[:, bass.ds(t, 1)], ALU.subtract,
                                        ALU.mult).then_inc(x1_ready, 1)
            steps(dve, CHUNK, norm1)

            def attend(b, u, i):
                dve.wait_ge(x1t_done, b + 1)
                if past(b, 2):
                    dve.wait_ge(router_done, b - 1)
                nc.vector.tensor_copy(tok_t[:, 1, :], psum[:, 7, :]).then_inc(tok_copied, 1)
                if past(b, 1):
                    norm2(b - 1, 1 - u)
                for t in range(QT):
                    dve.wait_ge(s_done, QT * b + t + 1)
                    diag = psum[:, t, t * P:(t + 1) * P]
                    done(nc.vector.tensor_tensor(diag, diag, consts[:, AT_MASK:AT_MASK + P], ALU.add), masked, QT * b + t + 1)
                    done(nc.vector.tensor_reduce(top_peak[:, u, t:t + 1], psum[:, t, 0:(t + 1) * P], op=ALU.max, axis=AX.X),
                         peak_neg, QT * b + t + 1)
                    nc.vector.tensor_scalar(bias2[:, u, t:t + 1], top_peak[:, u, t:t + 1], -1.0 / E ** 0.5, None,
                                            ALU.mult).then_inc(peak_ready, 1)
                if past(b, 1):
                    choose(b - 1, 1 - u)
                for t in range(QT):
                    dve.wait_ge(av_done, QT * b + t + 1)
                    done(nc.vector.reciprocal(inv_row[:, u, t:t + 1], row_sum[:, u, t:t + 1]), inv2_made, QT * b + t + 1)
                    nc.vector.scalar_tensor_tensor(sum2[:, t, :], psum[:, 6 + t % 2, 0:E], inv_row[:, u, t:t + 1],
                                                   x1_n[:, u, t, :], ALU.mult, ALU.add).then_inc(sum2_done, 1)
                    dve.wait_ge(sum2_done, QT * b + t + 1)
                    nc.vector.bn_stats(stats2[:, u, t, :], sum2[:, t, :]).then_inc(stats2_done, 1)
                dve.wait_ge(stats2_done, QT * (b + 1))
                moments(stats2[:, u], mean2[:, u, :], rstd2[:, u, :], b + 1)

            def norm2(b, u):
                dve.wait_ge(rstd_ready, b + 2)
                for t in range(QT):
                    nc.vector.tensor_scalar(sum2[:, t, :], sum2[:, t, :], mean2[:, u, t:t + 1], rstd2[:, u, t:t + 1],
                                            ALU.subtract, ALU.mult).then_inc(normed2, 1)
                dve.wait_ge(normed2, QT * (b + 1))
                nc.vector.tensor_copy(x2[:, bass.ds(QT * b, QT), :], sum2[:, :, :]).then_inc(x2_ready, QT)

            def choose(b, u):
                dve.wait_ge(x2t_done, b + 1)
                nc.vector.tensor_copy(tok_t[:, 1, :], psum[:, 7, :]).then_inc(x2t_copied, 1)
                dve.wait_ge(router_done, b + 1)
                nc.vector.tensor_copy(logits[:, u].rearrange("p t n -> p (t n)"), psum[:, 5, 0:QT * N_EXP]).then_inc(logits_copied, 1)
                dve.wait_ge(logits_copied, b + 1).then_inc(dve_waited, 1)
                for t in range(QT):
                    nc.vector.max(top8[:, u, t, :], logits[:, u, t, :]).then_inc(top_found, 1)
                dve.wait_ge(top_found, QT * (b + 1)).then_inc(dve_waited, 1)
                for t in range(QT):
                    nc.vector.max_index(where8[:, u, t, :].bitcast(U32), top8[:, u, t, :], logits[:, u, t, :]).then_inc(where_found, 1)
                dve.wait_ge(where_found, QT * (b + 1))
                nc.vector.tensor_copy(top_v[:, :, bass.ds(QT * b, QT)], top8[:, u, :, 0:TOP].rearrange("p t k -> p k t"))
                nc.vector.tensor_copy(top_i[:, :, bass.ds(QT * b, QT)],
                                      where8[:, u, :, 0:TOP].bitcast(U32).rearrange("p t k -> p k t")).then_inc(top_kept, 1)
            steps(dve, B, attend)
            norm2(B - 1, 1)
            choose(B - 1, 1)

            dve.wait_ge(top_kept, B)
            nc.vector.tensor_tensor(top_v[:, 1, :], top_v[:, 1, :], top_v[:, 0, :], ALU.subtract).then_inc(gap_made, 1)
            count = consts[:, AT_COUNT:AT_COUNT + P]
            done(nc.vector.tensor_tensor(chosen, top_i.unsqueeze(3).to_broadcast([P, TOP, TILES, N_EXP]),
                                         count[:, 0:N_EXP].unsqueeze(1).unsqueeze(1).to_broadcast([P, TOP, TILES, N_EXP]),
                                         ALU.is_equal), chosen_made, 1)
            nc.vector.tensor_tensor(picked, chosen[:, 0], chosen[:, 1], ALU.add).then_inc(picked_made, 1)
            dve.wait_ge(counted, 1)
            tile_count = psum[:, 1, 0:TILES * N_EXP].rearrange("p (t n) -> p t n", n=N_EXP)
            n_scan = 1
            done(nc.vector.tensor_copy(upto[0], tile_count), scan_step, n_scan)
            at, hop = 0, 1
            while hop < TILES:
                nc.vector.tensor_copy(upto[1 - at][:, 0:hop, :], upto[at][:, 0:hop, :])
                n_scan += 1
                done(nc.vector.tensor_tensor(upto[1 - at][:, hop:, :], upto[at][:, hop:, :], upto[at][:, 0:TILES - hop, :],
                                             ALU.add), scan_step, n_scan)
                at, hop = 1 - at, 2 * hop
            n_lots = 0

            def lots_done(ins):
                nonlocal n_lots
                n_lots += 1
                done(ins, lots_step, n_lots)
            lots_done(nc.vector.tensor_scalar(lots_i, upto[at][:, TILES - 1, :], float(P - 1), None, ALU.add))
            lots_done(nc.vector.tensor_scalar(lots_i, lots_i, P.bit_length() - 1, None, ALU.logical_shift_right))
            lots_done(nc.vector.tensor_copy(lots_n, lots_i))
            lots_done(nc.vector.tensor_copy(lots[:, 0, :], lots_n))
            now, hop = 0, 1
            while hop < N_EXP:
                nc.vector.tensor_copy(lots[:, 1 - now, 0:hop], lots[:, now, 0:hop])
                lots_done(nc.vector.tensor_tensor(lots[:, 1 - now, hop:], lots[:, now, hop:], lots[:, now, 0:N_EXP - hop], ALU.add))
                now, hop = 1 - now, 2 * hop
            lots_end = lots[:, now, :]
            done(nc.vector.tensor_tensor(place, upto[at], tile_count, ALU.subtract), place_made, 1)
            done(nc.vector.tensor_tensor(place, place, psum[:, 0, 0:TILES * N_EXP].rearrange("p (t n) -> p t n", n=N_EXP),
                                         ALU.add), place_made, 2)
            lots_done(nc.vector.tensor_tensor(lots_n, lots_end, lots_n, ALU.subtract))
            lots_done(nc.vector.tensor_scalar(lots_n, lots_n, float(P), None, ALU.mult))
            done(nc.vector.tensor_tensor(place, place, lots_n.unsqueeze(1).to_broadcast([P, TILES, N_EXP]), ALU.add), place_made, 3)
            done(nc.vector.tensor_tensor(placed, chosen, place.unsqueeze(1).to_broadcast([P, TOP, TILES, N_EXP]), ALU.mult),
                 placed_made, 1)
            done(nc.vector.tensor_reduce(spot, placed, op=ALU.add, axis=AX.X), spot_made, 1)
            done(nc.vector.tensor_copy(spot_i[:, 0], spot), spot_int, 1)
            nc.vector.tensor_scalar(spot_i[:, 1], spot_i[:, 0], P.bit_length() - 1, None, ALU.logical_shift_right).then_inc(spot_parts, 1)
            dve.wait_ge(spot_parts, 1)
            done(nc.vector.tensor_scalar(spot_i[:, 0], spot_i[:, 0], P - 1, None, ALU.bitwise_and), spot_parts, 2)
            flat = "p k t -> p (k t)"
            nc.vector.tensor_copy(spot_slot, spot_i[:, 1].rearrange(flat)).then_inc(spot_back, 1)
            done(nc.vector.tensor_copy(spot_row, spot_i[:, 0].rearrange(flat)), spot_back, 2)
            n_pairs = TOP * TILES
            nc.vector.tensor_tensor(is_row, spot_row.unsqueeze(2).to_broadcast([P, n_pairs, P]),
                                    count.unsqueeze(1).to_broadcast([P, n_pairs, P]), ALU.is_equal).then_inc(rows_marked, 1)
            done(nc.vector.tensor_tensor(is_slot[:, :, SLOTS:], spot_slot.unsqueeze(2).to_broadcast([P, n_pairs, SLOTS]),
                                         count[:, 0:SLOTS].unsqueeze(1).to_broadcast([P, n_pairs, SLOTS]), ALU.is_equal),
                 slot_hits, 1)
            nc.vector.tensor_tensor(is_slot[:, :, 0:SLOTS], is_slot[:, :, SLOTS:],
                                    consts[:, AT_TILE:AT_TILE + n_pairs].unsqueeze(2).to_broadcast([P, n_pairs, SLOTS]),
                                    ALU.mult).then_inc(slots_marked, 1)
            dve.wait_ge(slots_marked, 1)
            nc.vector.tensor_scalar(is_slot[:, :, SLOTS:], is_slot[:, :, SLOTS:], consts[:, AT_ROW:AT_ROW + 1], None,
                                    ALU.mult).then_inc(slots_marked, 1)
            done(nc.vector.tensor_tensor(slot_past, count[:, 0:SLOTS].unsqueeze(2).to_broadcast([P, SLOTS, N_EXP]),
                                         lots_end.unsqueeze(1).to_broadcast([P, SLOTS, N_EXP]), ALU.is_ge), past_made, 1)
            done(nc.vector.tensor_reduce(slot_f[:, 0, :], slot_past, op=ALU.add, axis=AX.X), past_made, 2)
            done(nc.vector.tensor_scalar(slot_exp, slot_f[:, 0, :], float(N_EXP - 1), None, ALU.min), past_made, 3)
            dve.wait_ge(gap_exp, 1)
            done(nc.vector.tensor_scalar(top_v[:, 0, :], top_v[:, 1, :], 1.0, None, ALU.add), gap_plus1, 1)
            done(nc.vector.reciprocal(top_v[:, 0, :], top_v[:, 0, :]), gate1_made, 1)
            nc.vector.tensor_tensor(top_v[:, 1, :], top_v[:, 1, :], top_v[:, 0, :], ALU.mult).then_inc(gates_made, 1)
            dve.wait_ge(table_done, 1)
            n_slot = 0

            def slot_done(ins):
                nonlocal n_slot
                n_slot += 1
                done(ins, slot_step, n_slot)
            slot_done(nc.vector.tensor_copy(slot_f[:, 3, :], psum[:, 2, SLOTS:2 * SLOTS]))
            slot_done(nc.vector.scalar_tensor_tensor(slot_f[:, 1, :], psum[:, 2, 0:SLOTS], float(P), slot_f[:, 3, :],
                                                     ALU.mult, ALU.add))
            slot_done(nc.vector.tensor_scalar(slot_f[:, 2, :], slot_f[:, 1, :], 0.0, None, ALU.is_equal))
            slot_done(nc.vector.tensor_tensor(slot_f[:, 3, :], slot_f[:, 1, :], slot_f[:, 2, :], ALU.add))
            slot_done(nc.vector.tensor_scalar(slot_src, slot_f[:, 3, :], -1.0, None, ALU.add))
            slot_done(nc.vector.tensor_scalar(slot_src, slot_src, T - 1, None, ALU.bitwise_and))
            slot_done(nc.vector.tensor_tensor(slot_f[:, 2, :], slot_f[:, 2, :], consts[:, AT_SPILL:AT_SPILL + SLOTS], ALU.mult))
            slot_done(nc.vector.tensor_tensor(slot_f[:, 1, :], slot_f[:, 1, :], slot_f[:, 2, :], ALU.add))
            nc.vector.tensor_scalar(slot_dst, slot_f[:, 1, :], -1.0, None, ALU.add).then_inc(routed, 1)

            def lot(s, u, i):
                if past(s, 1):
                    hidden_out(s - 1, 1 - u)
                if past(s, 2):
                    result_out(s - 2, u, i - 1)

            def hidden_out(s, u):
                dve.wait_ge(hid_t_done, s + 1)
                if past(s, 2):
                    dve.wait_ge(down_done, s - 1)
                nc.vector.tensor_copy(hid_t[:, u, 4:8, :].rearrange("p j n -> p (j n)"), psum[:, 5, :]).then_inc(hid_t_copied, 1)

            def result_out(s, u, i):
                dve.wait_ge(down_done, s + 1)
                if past(s, 2):
                    dve.wait_ge(ys_stored[u], 16 * i)
                nc.vector.tensor_copy(y_rows[:, u, :], psum[:, 6, 0:E]).then_inc(y_copied, 1)
            steps(dve, SLOTS, lot, 4)
            result_out(SLOTS - 2, 0, SLOTS // 2 - 1)
            hidden_out(SLOTS - 1, 1)
            result_out(SLOTS - 1, 1, SLOTS // 2 - 1)

            dve.wait_ge(gates_made, 1)

            def finish(g, u, i):
                dve.wait_ge(y_loaded[u], 32 * i + 32)
                if past(g, 2):
                    dve.wait_ge(out_stored[u], 16 * i)
                for t in range(QT):
                    done(nc.vector.scalar_tensor_tensor(sum3[:, u, t, :], y_pick[0][:, u, t, :], top_v[:, 0, bass.ds(QT * g + t, 1)],
                                                        x2[:, bass.ds(QT * g + t, 1), :].rearrange("p a e -> p (a e)"),
                                                        ALU.mult, ALU.add), mix1_done, QT * g + t + 1)
                    done(nc.vector.scalar_tensor_tensor(sum3[:, u, t, :], y_pick[1][:, u, t, :], top_v[:, 1, bass.ds(QT * g + t, 1)],
                                                        sum3[:, u, t, :], ALU.mult, ALU.add), mix2_done, QT * g + t + 1)
                    nc.vector.bn_stats(stats3[:, u, t, :], sum3[:, u, t, :]).then_inc(stats3_done, 1)
                dve.wait_ge(stats3_done, QT * (g + 1))
                moments(stats3[:, u], mean3[:, u, :], rstd3[:, u, :], g + B + 1)
                if past(g, 1):
                    norm3(g - 1, 1 - u)

            def norm3(g, u):
                dve.wait_ge(rstd_ready, g + B + 2)
                for t in range(QT):
                    nc.vector.tensor_scalar(sum3[:, u, t, :], sum3[:, u, t, :], mean3[:, u, t:t + 1], rstd3[:, u, t:t + 1],
                                            ALU.subtract, ALU.mult).then_inc(out_ready, 1)
            steps(dve, TILES // QT, finish)
            norm3(TILES // QT - 1, 1)


def kernel(x, ctx_1024, L0_attn_Wq, L0_attn_Wkv, L0_attn_q_g, L0_attn_q_b, L0_attn_k_g, L0_attn_k_b, L0_attn_Wwin,
           L0_attn_bwin, L0_attn_Wout, L0_ffn_router_w, L0_ffn_expert_w1, L0_ffn_expert_w2):
    import numpy as np
    import concourse.bacc as bacc
    from concourse.bass_utils import run_bass_kernel_spmd

    laid = np.ascontiguousarray
    tokens = np.asarray(x).reshape(T, E)
    ctx = np.asarray(ctx_1024)
    arrays = {
        "x": laid(tokens),
        "x_steps": laid(tokens.reshape(P, CHUNK, E).transpose(1, 2, 0)),
        "ctx": laid(ctx),
        "ctx_t": laid(ctx.transpose(0, 2, 1)),
        "Wq": laid(L0_attn_Wq), "Wkv": laid(L0_attn_Wkv),
        "q_g": laid(L0_attn_q_g), "q_b": laid(L0_attn_q_b), "k_g": laid(L0_attn_k_g), "k_b": laid(L0_attn_k_b),
        "Wwin": laid(L0_attn_Wwin), "bwin": laid(L0_attn_bwin), "Wout": laid(L0_attn_Wout),
        "router_t": laid(np.asarray(L0_ffn_router_w).T),
        "w1_t": laid(np.asarray(L0_ffn_expert_w1).transpose(0, 2, 1)),
        "w2_t": laid(np.asarray(L0_ffn_expert_w2).transpose(0, 2, 1)),
        "shape_consts": host_consts(),
    }
    nc = bacc.Bacc("TRN2", target_bir_lowering=False, num_devices=1)
    aps = {n: nc.dram_tensor(n, a.shape, mybir.dt.from_np(a.dtype), kind="ExternalInput").ap() for n, a in arrays.items()}
    out = nc.dram_tensor("out", (T, E), F32, kind="ExternalOutput").ap()
    decoder_layer(nc, out=out, **aps)
    got = run_bass_kernel_spmd(nc, [arrays], core_ids=[0])
    return got.results[0]["out"].reshape(B, L, E)
```

```python
from contextlib import ExitStack

import concourse.bass as bass
from concourse import mybir

F32 = mybir.dt.float32
I32 = mybir.dt.int32
U32 = mybir.dt.uint32
BF16 = mybir.dt.bfloat16
F16 = mybir.dt.float16
ALU = mybir.AluOpType
ACT = mybir.ActivationFunctionType
AX = mybir.AxisListType

P = 128
B, L, E = 8, 512, 256
T = B * L
C = E // P
H, D = 16, 16
K = 17
R = K // 2
CHUNK = T // P
ROWS = CHUNK + 2 * R
GROUPS = 4
GROUP = CHUNK // GROUPS
PER = L // CHUNK
QKVW = 3 * E + 2 * H
EPS = 1e-5
SCALE = D ** -0.5
PENALTY = 1e4
W0 = (K + 1) // 2
WEIGHT_LOADS = 16 * (4 * C + 5 + 2)
QT = L // P
TILES = T // P
MASKED = 1e10
LOW = 10856
N_EXP, TOP, F = 8, 2, 1024
FB = F // P
EW = C * F
PIECES = CHUNK
PIECE = N_EXP * EW // PIECES
F32_BIAS, F32_MANT = 127, 23
TOP_BITS = 15
X_BITS = 11
SLOTS = TOP * T // P + N_EXP
AT_IDENT = 0
AT_REACH = AT_IDENT + P
AT_MASK = AT_REACH + K
AT_BELOW = AT_MASK + P
AT_COUNT = AT_BELOW + P
AT_TILE = AT_COUNT + P
AT_ROW = AT_TILE + TOP * TILES
AT_SPILL = AT_ROW + 1
N_CONST = AT_SPILL + SLOTS


def host_consts():
    import numpy as np
    i, j = np.arange(P)[:, None], np.arange(P)[None, :]
    wide = lambda a: np.broadcast_to(a, (P, len(a)))
    parts = [
        i == j,
        wide(np.abs(np.arange(K) - R)),
        np.where(j > i, -MASKED, 0.0),
        i < j,
        wide(np.arange(P)),
        wide(np.arange(TOP * TILES)),
        i + 1.0,
        TOP * T + P * np.arange(SLOTS)[None, :] + i + 1.0,
    ]
    return np.ascontiguousarray(np.concatenate(parts, axis=1).astype(np.float32))


def steps(eng, n, body, peeled=2, start=0):
    first = max(start, peeled)
    for t in range(start, first):
        body(t, t % 2, t // 2)
    with eng.Fori(first // 2, n // 2) as i:
        for u in (0, 1):
            body(2 * i + u, u, i)


def past(t, k):
    return not isinstance(t, int) or t >= k


def row(ap, t):
    return ap[:, bass.ds(t, 1)]


def decoder_layer(nc, x, x_steps, ctx, ctx_t, Wq, Wkv, q_g, q_b, k_g, k_b, Wwin, bwin, Wout,
                  router_t, w1_t, w2_t, shape_consts, out):
    stack = ExitStack()
    with stack:
        def sb(name, shape, dt=F32):
            return stack.enter_context(nc.sbuf_tensor(name, shape, dt))

        def sem(name):
            return stack.enter_context(nc.semaphore(name))

        x1_dram = nc.dram_tensor("x1_dram", [T, E], F32, kind="Internal").ap()
        x_chunk = x.rearrange("(p s) e -> p s e", s=CHUNK)
        x1_seq = x1_dram.rearrange("(b l) e -> b l e", l=L)
        x1_chunk = x1_dram.rearrange("(p s) e -> p s e", s=CHUNK)

        arena = sb("arena", [P, LOW + (CHUNK + 2 * ROWS) * E])
        low = arena[:, 0:LOW]
        big = arena[:, LOW:]
        mid = sb("mid", [P, 2 * K * E])
        low_used = {}

        def carve(region, start, *shape):
            n = 1
            for m in shape:
                n *= m
            names = " ".join("abcd"[:len(shape)])
            ap = region[:, start:start + n]
            if len(shape) > 1:
                ap = ap.rearrange(f"p ({names}) -> p {names}", **dict(zip("abcd", shape)))
            return ap

        def next_low(phase, *shape):
            start = low_used.get(phase, 0)
            n = 1
            for m in shape:
                n *= m
            low_used[phase] = start + n
            assert start + n <= LOW, (phase, start + n)
            return carve(low, start, *shape)

        consts = sb("consts", [P, N_CONST])
        ident = consts[:, AT_IDENT:AT_IDENT + P]
        reach = consts[:, AT_REACH:AT_REACH + K]
        ones_pp = sb("ones_pp", [P, P])
        ones_row = ones_pp[0:1, :]
        b_win = sb("b_win", [1, 2 * H])
        minus_half = sb("minus_half", [P, 2 * H])

        router_w = sb("router_w", [P, C, N_EXP])

        x2_dram = nc.dram_tensor("x2_dram", [T, E], F32, kind="Internal").ap()
        x2_seq = x2_dram.rearrange("(b l) e -> b l e", l=L)
        x2 = carve(mid, 0, TILES, E)
        ctx_sb = next_low("cross", 2, QT, E)
        ctx_ts = next_low("cross", 2, C, L)
        x1_n = next_low("cross", 2, QT, E)
        tok_t = next_low("cross", C, L)
        probs = next_low("cross", 2, L)
        probs_t = next_low("cross", 2, QT, P)
        top_peak = next_low("cross", 2, QT)
        bias2 = next_low("cross", 2, QT)
        row_sum = next_low("cross", 2, QT)
        inv_row = next_low("cross", 2, QT)
        stats2 = next_low("cross", 2, QT, 6)
        mean2 = next_low("cross", 2, QT)
        rstd2 = next_low("cross", 2, QT)
        logits = next_low("cross", 2, QT, N_EXP)
        top8 = next_low("cross", 2, QT, 8)
        where8 = next_low("cross", 2, QT, 8)
        assert low_used["cross"] <= LOW - EW // 2

        keep_at = TILES * E
        slot_src = carve(mid, keep_at, SLOTS).bitcast(I32)
        slot_dst = carve(mid, keep_at + SLOTS, SLOTS).bitcast(I32)
        slot_word = carve(mid, keep_at + 2 * SLOTS, SLOTS // 2).bitcast(I32)
        top_v = carve(mid, keep_at + 3 * SLOTS, TOP, TILES)
        top_i = carve(mid, keep_at + 3 * SLOTS + TOP * TILES, TOP, TILES)
        chosen = next_low("route", TOP, TILES, N_EXP)
        picked = next_low("route", TILES, N_EXP)
        upto = [next_low("route", TILES, N_EXP) for _ in range(2)]
        place = next_low("route", TILES, N_EXP)
        placed = next_low("route", TOP, TILES, N_EXP)
        is_row = carve(low, 0, TOP * TILES, P // 2).bitcast(BF16)
        low_used["route"] = TOP * TILES * P // 2
        lots = next_low("route", 2, N_EXP)
        lots_n = next_low("route", N_EXP)
        lots_i = next_low("route", N_EXP).bitcast(I32)
        rest_at = keep_at + 3 * SLOTS + 2 * TOP * TILES
        spot = carve(mid, rest_at, TOP, TILES)
        spot_i = next_low("route", 2, TOP, TILES).bitcast(I32)
        spot_row = carve(mid, rest_at + TOP * TILES, TOP * TILES)
        spot_slot = next_low("route", TOP * TILES)
        slot_past = next_low("route", SLOTS, N_EXP)
        slot_f = next_low("route", 4, SLOTS)
        is_slot = next_low("route", TOP * TILES, SLOTS).bitcast(BF16)
        assert low_used["route"] <= LOW - EW // 2

        ys_dram = nc.dram_tensor("ys_dram", [(TOP * TILES + SLOTS) * P, E], F32, kind="Internal").ap()
        ys_group = ys_dram[0:TOP * T, :].rearrange("(g l) e -> g l e", l=QT * P)
        out_group = out.rearrange("(g l) e -> g l e", l=QT * P)
        w_f32 = carve(big, 0, N_EXP, 2, EW)
        arena16 = arena[:, :].bitcast(F16)
        w_low = arena16[:, 2 * LOW:2 * LOW + 4 * N_EXP * EW].rearrange("p (e k x) -> p e k x", k=2, x=2 * EW)
        w_high = arena16[:, 2 * LOW - EW:2 * LOW - EW + 4 * N_EXP * EW].rearrange("p (e k x) -> p e k x", k=2, x=2 * EW)
        w_parts = arena16[:, 2 * LOW - EW:2 * LOW - EW + 4 * N_EXP * EW].rearrange("p (e k x) -> p e k x", k=4, x=EW)
        scale_at = rest_at + 2 * TOP * TILES
        scale_bits = carve(mid, scale_at, 8).bitcast(I32)
        w_scale = carve(mid, scale_at, 8)
        w1_scale, w2_scale, up_scale, hid_scale, y_scale1, y_scale2 = (w_scale[:, k:k + 1] for k in range(6))
        w_exp = carve(mid, scale_at + 8, 2).bitcast(I32)
        assert scale_at + 10 <= 2 * K * E
        src_col = next_low("experts", 2, 1).bitcast(I32)
        dst_col = next_low("experts", 2, 1).bitcast(I32)
        rows = next_low("experts", 2, E)
        rows_hi = next_low("experts", 2, E // 2).bitcast(F16)
        rows_lo = next_low("experts", 2, E // 2).bitcast(F16)
        hid = next_low("experts", 2, F)
        hid_hi = next_low("experts", 2, F // 2).bitcast(F16)
        hid_lo = next_low("experts", 2, F // 2).bitcast(F16)
        y_side = next_low("experts", 2, E)
        y_rows = next_low("experts", 2, E)

        y_pick = [next_low("end", 2, QT, E) for _ in range(TOP)]
        sum3 = next_low("end", 2, QT, E)
        out_rows = next_low("end", 2, QT, E)
        stats3 = next_low("end", 2, QT, 6)
        mean3 = next_low("end", 2, QT)
        rstd3 = next_low("end", 2, QT)

        q_all = carve(big, 0, CHUNK, E)
        k_all = carve(big, CHUNK * E, ROWS, E)
        v_all = carve(big, (CHUNK + ROWS) * E, ROWS, E)
        qk_prod = mid[:, 0:K * E]
        av_prod = [carve(mid, K * E, W0, E), carve(mid, (K + W0) * E, K - W0, E)]
        act_qk = carve(mid, 0, 2, 2 * E)
        cen_qk = carve(mid, 4 * E, 2, 2 * E)
        sq_qk = carve(mid, 8 * E, 2, 2 * E)
        head_var = carve(mid, 12 * E, CHUNK, 2 * H)
        head_rstd = carve(mid, 16 * E, CHUNK, 2 * H)
        newton = carve(mid, 20 * E, CHUNK, 2 * H)
        w_in = next_low("window", C, QKVW)
        x_step = next_low("window", 2, C, P)
        win = next_low("window", CHUNK, 2 * H)
        gains = next_low("window", 2, D)
        head_sum = next_low("window", 2, 2 * H)
        gate = carve(low, 0, CHUNK, R + 1, H)
        low_used["window"] = CHUNK * (R + 1) * H
        w_out = next_low("window", C, E)
        biases = next_low("window", 2, D)
        sharp = next_low("window", CHUNK, H)
        edge = next_low("window", CHUNK, H)
        stats = next_low("window", CHUNK, 6)
        mean1 = next_low("window", CHUNK)
        rstd1 = next_low("window", CHUNK)
        score = next_low("window", 2, K * H)
        prob = next_low("window", 2, K * H)
        peak = next_low("window", 2, H)
        total = next_low("window", 2, H)
        inv_total = next_low("window", 2, H)
        w_piece = next_low("window", 2, PIECE)
        w_squares = next_low("window", 2, PIECES)
        w_sum = next_low("window", 2)
        mixed_t = next_low("window", 2, C, P)
        tanh_y = next_low("window", 2, E)
        x_res = next_low("window", 2, E)
        y_sb = next_low("window", 2, E)
        bn6 = next_low("window", 2, 6)

        psum = stack.enter_context(nc.psum_tensor("psum", [P, 8, 512], F32))

        weights_loaded = sem("weights_loaded")
        fills_made = sem("fills_made")
        halo_zeroed = sem("halo_zeroed")
        x_step_loaded = [sem("x_step_loaded0"), sem("x_step_loaded1")]
        qkv_done = sem("qkv_done")
        silu_done = sem("silu_done")
        centred = sem("centred")
        squared = sem("squared")
        var_done = sem("var_done")
        halo_loaded = sem("halo_loaded")
        sig_done = sem("sig_done")
        gained = sem("gained")
        var_eps = sem("var_eps")
        root_done = sem("root_done")
        gate_done = sem("gate_done")
        gate_args = sem("gate_args")
        rstd_heads = sem("rstd_heads")
        q_scaled = sem("q_scaled")
        newton_step = sem("newton_step")
        k_scaled = sem("k_scaled")
        k_ready = sem("k_ready")
        q_ready = sem("q_ready")
        width_done = sem("width_done")
        gate_arg = sem("gate_arg")
        score_ready = sem("score_ready")
        exp_done = sem("exp_done")
        inv_ready = sem("inv_ready")
        prob_ready = sem("prob_ready")
        av_ready = sem("av_ready")
        av_used = sem("av_used")
        mixed_done = sem("mixed_done")
        mixed_copied = sem("mixed_copied")
        y_done = sem("y_done")
        tanh_done = sem("tanh_done")
        x1_last = sem("x1_last")
        norm1_shift = sem("norm1_shift")
        y_parts = sem("y_parts")
        x_res_loaded = [sem("x_res_loaded0"), sem("x_res_loaded1")]
        res_done = sem("res_done")
        res_kept = sem("res_kept")
        mean_diff = sem("mean_diff")
        mean_diff_sq = sem("mean_diff_sq")
        mean_added = sem("mean_added")
        var_between = sem("var_between")
        var_even = sem("var_even")
        var_made = sem("var_made")
        rstd_ready = sem("rstd_ready")
        x1_ready = sem("x1_ready")
        x1_stored = sem("x1_stored")
        prob_made = sem("prob_made")
        head_mean_summed = sem("head_mean_summed")
        silu_y_made = sem("silu_y_made")
        res_summed = sem("res_summed")
        qk_multiplied = sem("qk_multiplied")
        qk_summed = sem("qk_summed")
        penalised = sem("penalised")
        peak_found = sem("peak_found")
        total_found = sem("total_found")

        pool_waited = sem("pool_waited")
        dve_waited = sem("dve_waited")
        normed2 = sem("normed2")
        stats2_done = sem("stats2_done")
        stats3_done = sem("stats3_done")
        slot_hits = sem("slot_hits")
        x1t_done = sem("x1t_done")
        tok_copied = sem("tok_copied")
        s_done = sem("s_done")
        peak_ready = sem("peak_ready")
        masked = sem("masked")
        peak_neg = sem("peak_neg")
        exp2_done = sem("exp2_done")
        pt_done = sem("pt_done")
        pt_copied = sem("pt_copied")
        av_done = sem("av_done")
        inv2_made = sem("inv2_made")
        sum2_done = sem("sum2_done")
        x2_ready = sem("x2_ready")
        x2t_done = sem("x2t_done")
        x2t_copied = sem("x2t_copied")
        router_done = sem("router_done")
        logits_copied = sem("logits_copied")
        top_found = sem("top_found")
        where_found = sem("where_found")
        top_kept = sem("top_kept")
        w_loaded = sem("w_loaded")
        w_piece_loaded = sem("w_piece_loaded")
        w_squared = sem("w_squared")
        w_summed = sem("w_summed")
        w_total = sem("w_total")
        w_exps = sem("w_exps")
        w_scaled = sem("w_scaled")
        w_multiplied = sem("w_multiplied")
        w_high_made = sem("w_high_made")
        w_low_made = sem("w_low_made")
        gap_made = sem("gap_made")
        gap_exp = sem("gap_exp")
        gap_plus1 = sem("gap_plus1")
        gate1_made = sem("gate1_made")
        gates_made = sem("gates_made")
        chosen_made = sem("chosen_made")
        picked_made = sem("picked_made")
        counted = sem("counted")
        tile_sums = sem("tile_sums")
        scan_step = sem("scan_step")
        place_made = sem("place_made")
        lots_step = sem("lots_step")
        placed_made = sem("placed_made")
        spot_made = sem("spot_made")
        spot_int = sem("spot_int")
        spot_parts = sem("spot_parts")
        spot_back = sem("spot_back")
        rows_marked = sem("rows_marked")
        slots_marked = sem("slots_marked")
        table_done = sem("table_done")
        slot_step = sem("slot_step")
        routed = sem("routed")
        past_made = sem("past_made")
        src_copied = sem("src_copied")
        dst_copied = sem("dst_copied")
        rows_t_done = sem("rows_t_done")
        rows_high = sem("rows_high")
        rows_low = sem("rows_low")
        up_done = sem("up_done")
        gelu_done = sem("gelu_done")
        hid_high = sem("hid_high")
        hid_low = sem("hid_low")
        down_done = sem("down_done")
        y_copied = sem("y_copied")
        y_beside = sem("y_beside")
        mix1_done = sem("mix1_done")
        mix2_done = sem("mix2_done")
        out_ready = sem("out_ready")
        shift3_made = sem("shift3_made")
        ctx_loaded = [sem("ctx_loaded0"), sem("ctx_loaded1")]
        out_stored = [sem("out_stored0"), sem("out_stored1")]
        rows_loaded = [sem("rows_loaded0"), sem("rows_loaded1")]
        x2_stored = [sem("x2_stored0"), sem("x2_stored1")]
        y_loaded = [sem("y_loaded0"), sem("y_loaded1")]
        ys_stored = [sem("ys_stored0"), sem("ys_stored1")]

        block = stack.enter_context(nc.Block())

        @block.sync
        def _(sp):
            sp.dma_start(consts[:, :], shape_consts).then_inc(weights_loaded, 16)
            for c in range(C):
                for w, a in ((Wq, 0), (Wkv, E), (Wwin, 3 * E)):
                    sp.dma_start(w_in[:, c, a:a + w.shape[1]], w[c * P:(c + 1) * P, :]).then_inc(weights_loaded, 16)
                sp.dma_start(w_out[:, c, :], Wout[c * P:(c + 1) * P, :]).then_inc(weights_loaded, 16)
            sp.dma_start(router_w[:, :, :], router_t.rearrange("(c p) n -> p c n", p=P)).then_inc(weights_loaded, 16)
            for m, (g, b) in enumerate(((q_g, q_b), (k_g, k_b))):
                sp.dma_start(gains[:, m, :], g.partition_broadcast(P)).then_inc(weights_loaded, 16)
                sp.dma_start(biases[:, m, :], b.partition_broadcast(P)).then_inc(weights_loaded, 16)
            sp.dma_start(b_win[:, :], bwin.rearrange("(a n) -> a n", a=1)).then_inc(weights_loaded, 16)

            def load_x_step(t, u, i):
                if past(t, 2):
                    sp.wait_ge(qkv_done, t - 1)
                src = x_steps[bass.ds(t, 1)].rearrange("a (c q) p -> q (a c) p", q=P)
                sp.dma_start(x_step[:, u], src).then_inc(x_step_loaded[u], 16)
            steps(sp, CHUNK, load_x_step)

            sp.wait_ge(halo_zeroed, 4)
            sp.wait_ge(silu_done, CHUNK)
            for kv in (v_all, k_all):
                if kv is k_all:
                    sp.wait_ge(k_ready, 1)
                for b in range(B):
                    a, z = b * PER, (b + 1) * PER
                    sp.dma_start(kv[a + 1:z, 0:R, :], kv[a:z - 1, CHUNK:CHUNK + R, :]).then_inc(halo_loaded, 16)
                    sp.dma_start(kv[a:z - 1, R + CHUNK:ROWS, :], kv[a + 1:z, R:2 * R, :]).then_inc(halo_loaded, 16)

            def load_x_res(t, u, i):
                if past(t, 1):
                    sp.wait_ge(w_squared, 2 * t)
                for k, w in enumerate((w1_t, w2_t)):
                    parts = w.rearrange("e r c -> (e r c)").rearrange("(n p x) -> n p x", p=P, x=PIECE)
                    sp.dma_start(w_piece[:, k, :], parts[bass.ds(t, 1)].rearrange("a p x -> p (a x)")).then_inc(w_piece_loaded, 16)
                if past(t, 2):
                    sp.wait_ge(res_kept, t - 1)
                sp.dma_start(x_res[:, u, :], x_chunk[:, bass.ds(t, 1), :].rearrange("p a e -> p (a e)")).then_inc(x_res_loaded[u], 16)
            steps(sp, CHUNK, load_x_res)

            for g in range(GROUPS):
                if g < GROUPS - 1:
                    sp.wait_ge(x1_ready, GROUP * (g + 1))
                else:
                    sp.wait_ge(x1_last, GROUP)
                part = slice(g * GROUP, (g + 1) * GROUP)
                sp.dma_start(x1_chunk[:, part, :], q_all[:, part, :]).then_inc(x1_stored, 16)
            sp.wait_ge(x1_stored, 16 * GROUPS)

            def load_sequence(b, u, i):
                if past(b, 2):
                    sp.wait_ge(sum2_done, QT * (b - 1))
                    sp.wait_ge(x2t_done, b - 1)
                    sp.wait_ge(x2_ready, QT * (b - 1))
                rows_of = "a (t p) e -> p (a t) e"
                sp.dma_start(x1_n[:, u], x1_seq[bass.ds(b, 1)].rearrange(rows_of, p=P)).then_inc(ctx_loaded[u], 16)
                sp.dma_start(ctx_ts[:, u], ctx_t[bass.ds(b, 1)].rearrange("a (c p) l -> p (a c) l", p=P)).then_inc(ctx_loaded[u], 16)
                sp.dma_start(ctx_sb[:, u], ctx[bass.ds(b, 1)].rearrange(rows_of, p=P)).then_inc(ctx_loaded[u], 16)
                for k, (w, x) in enumerate(((w1_t, F), (w2_t, E))):
                    sp.dma_start(w_f32[:, bass.ds(b, 1), k, :].rearrange("p a (r x) -> p (a r) x", x=x),
                                 w[bass.ds(b, 1)].rearrange("a (r p) x -> p (a r) x", p=P)).then_inc(w_loaded, 16)
                if past(b, 1):
                    store_x2(b - 1, 1 - u)

            def store_x2(b, u):
                sp.wait_ge(x2_ready, QT * (b + 1))
                sp.dma_start(x2_seq[bass.ds(b, 1)].rearrange("a (t p) e -> p (a t) e", p=P),
                             x2[:, bass.ds(QT * b, QT), :]).then_inc(x2_stored[u], 16)
            steps(sp, B, load_sequence)
            store_x2(B - 1, 1)

            def load_picked(g, u, i):
                if past(g, 2):
                    sp.wait_ge(mix2_done, QT * (g - 1))
                for k in range(TOP):
                    sp.dma_start(y_pick[k][:, u], ys_group[bass.ds(k * (TILES // QT) + g, 1)].rearrange(
                        "a (t p) e -> p (a t) e", p=P)).then_inc(y_loaded[u], 16)
            for u in (0, 1):
                sp.wait_ge(ys_stored[u], 16 * (SLOTS // 2))
            steps(sp, TILES // QT, load_picked)
            for u in (0, 1):
                sp.wait_ge(out_stored[u], 16 * (TILES // QT // 2))

        @block.tensor
        def _(pe):
            pe.wait_ge(weights_loaded, WEIGHT_LOADS)
            pe.wait_ge(fills_made, 2)

            def project(t, u, i):
                pe.wait_ge(x_step_loaded[u], 16 * i + 16)
                if past(t, 2):
                    pe.wait_ge(silu_done, t - 1)
                for c in range(C):
                    nc.tensor.matmul(psum[:, u, :], x_step[:, u, c, :], w_in[:, c, 0:512],
                                     start=(c == 0), stop=(c == C - 1))
                for c in range(C):
                    nc.tensor.matmul(psum[:, 2 + u, 0:QKVW - 512], x_step[:, u, c, :], w_in[:, c, 512:QKVW],
                                     start=(c == 0), stop=False, skip_group_check=True)
                nc.tensor.matmul(psum[:, 2 + u, E:E + 2 * H], ones_row, b_win[:, :],
                                 start=False, stop=True, skip_group_check=True).then_inc(qkv_done, 1)
            steps(pe, CHUNK, project)
            pe.wait_ge(silu_done, CHUNK)

            def mix(t, u, i):
                if past(t, 2):
                    pe.wait_ge(mixed_copied, t - 1)
                for half, (a, n) in enumerate(((0, W0), (W0, K - W0))):
                    pe.wait_ge(av_ready, 2 * t + half + 1)
                    for w in range(n):
                        for c in range(C):
                            last = nc.tensor.matmul(psum[:, 2 * u + c, 0:P], av_prod[half][:, w, c * P:(c + 1) * P],
                                                    ident, start=(a + w == 0), stop=(a + w == K - 1))
                    last.then_inc(av_used, 1)
                pe.wait_ge(mixed_copied, t + 1)
                if past(t, 2):
                    pe.wait_ge(y_parts, t - 1)
                for c in range(C):
                    last = nc.tensor.matmul(psum[:, 4 + u, 0:E], mixed_t[:, u, c, :], w_out[:, c, :],
                                            start=(c == 0), stop=(c == C - 1))
                last.then_inc(y_done, 1)
            steps(pe, CHUNK, mix, 4)
            pe.wait_ge(y_parts, CHUNK)
            pe.wait_ge(w_summed, 1)
            nc.tensor.matmul(psum[:, 0, 0:2], ones_pp[:, :], w_sum[:, :], start=True, stop=True).then_inc(w_total, 1)

            def attend(b, u, i):
                pe.wait_ge(ctx_loaded[u], 48 * i + 48)
                if past(b, 1):
                    pe.wait_ge(sum2_done, QT * b)
                for c in range(C):
                    for t in range(QT):
                        last = nc.tensor.transpose(psum[:, 6 + c, t * P:(t + 1) * P], x1_n[:, u, t, c * P:(c + 1) * P], ident)
                last.then_inc(x1t_done, 1)
                pe.wait_ge(tok_copied, 2 * b + 2)
                for t in range(QT):
                    if past(b, 1):
                        pe.wait_ge(exp2_done, QT * b - QT + t + 1)
                    for c in range(C):
                        last = nc.tensor.matmul(psum[:, t, 0:(t + 1) * P], tok_t[:, c, t * P:(t + 1) * P],
                                                ctx_ts[:, u, c, 0:(t + 1) * P], start=(c == 0), stop=(c == C - 1))
                    last.then_inc(s_done, 1)
                if past(b, 1):
                    route(b - 1, 1 - u)
                for t in range(QT + 1):
                    if t < QT:
                        pe.wait_ge(exp2_done, QT * b + t + 1)
                        if t >= 2:
                            pe.wait_ge(pt_copied, QT * b + t - 1)
                        elif past(b, 1):
                            pe.wait_ge(pt_copied, QT * b + t - 1)
                            pe.wait_ge(logits_copied, b)
                        for k in range(t + 1):
                            last = nc.tensor.transpose(psum[:, 4 + t % 2, k * P:(k + 1) * P],
                                                       probs[:, t % 2, k * P:(k + 1) * P], ident)
                        last.then_inc(pt_done, 1)
                    if t:
                        q = t - 1
                        pe.wait_ge(pt_copied, QT * b + q + 1)
                        if q >= 2:
                            pe.wait_ge(sum2_done, QT * b + q - 1)
                        for k in range(q + 1):
                            last = nc.tensor.matmul(psum[:, 6 + q % 2, 0:E], probs_t[:, q % 2, k, :], ctx_sb[:, u, k, :],
                                                    start=(k == 0), stop=(k == q))
                        last.then_inc(av_done, 1)

            def route(b, b_u):
                pe.wait_ge(x2_ready, QT * (b + 1))
                for c in range(C):
                    for t in range(QT):
                        last = nc.tensor.transpose(psum[:, 6 + c, t * P:(t + 1) * P],
                                                   x1_n[:, b_u, t, c * P:(c + 1) * P], ident)
                last.then_inc(x2t_done, 1)
                pe.wait_ge(x2t_copied, 2 * b + 2)
                for t in range(QT):
                    for c in range(C):
                        last = nc.tensor.matmul(psum[:, 5, t * N_EXP:(t + 1) * N_EXP], tok_t[:, c, t * P:(t + 1) * P],
                                                router_w[:, c, :], start=(c == 0), stop=(c == C - 1))
                last.then_inc(router_done, 1)
            steps(pe, B, attend)
            pe.wait_ge(sum2_done, T // P)
            route(B - 1, 1)

            pe.wait_ge(picked_made, 1)
            nc.tensor.matmul(psum[:, 0, 0:TILES * N_EXP], consts[:, AT_BELOW:AT_BELOW + P],
                             picked.rearrange("p t n -> p (t n)"), start=True, stop=True)
            nc.tensor.matmul(psum[:, 1, 0:TILES * N_EXP], ones_pp[:, :],
                             picked.rearrange("p t n -> p (t n)"), start=True, stop=True).then_inc(counted, 1)
            pe.wait_ge(rows_marked, 1)
            pe.wait_ge(slots_marked, 2)
            for j in range(TOP * TILES):
                last = nc.tensor.matmul(psum[:, 2, 0:2 * SLOTS], is_row[:, j, :], is_slot[:, j, :],
                                        start=(j == 0), stop=(j == TOP * TILES - 1))
            last.then_inc(table_done, 1)

            pe.wait_ge(routed, 1)
            pe.wait_ge(w_low_made, 2 * N_EXP)

            def block_of(w, e, k, at, n):
                return w[:, bass.ds(e, 1), k, at:at + n].rearrange("p a n -> p (a n)")

            def transpose_rows(s, u, i):
                pe.wait_ge(rows_loaded[u], 16 * i + 16)
                for c in range(C):
                    last = nc.tensor.transpose(psum[:, u, c * P:(c + 1) * P], rows[:, u, c * P:(c + 1) * P], ident)
                last.then_inc(rows_t_done, 1)

            def up(u, e, j):
                dst = psum[:, 2 + 2 * u + j // 4, j % 4 * P:(j % 4 + 1) * P]
                for k, (w, x) in enumerate(((w_high, rows_hi), (w_high, rows_lo), (w_low, rows_hi))):
                    for c in range(C):
                        last = nc.tensor.matmul(dst, block_of(w, e, 0, c * F + j * P, P), x[:, u, c * P:(c + 1) * P],
                                                start=(k == 0 and c == 0), stop=(k == 2 and c == C - 1))
                return last

            def down(u, e, j):
                both = w_parts[:, bass.ds(e, 1), 2:4, j * E:(j + 1) * E].rearrange("p a k n -> p (a k) n")
                high = w_parts[:, bass.ds(e, 1), 2:3, j * E:(j + 1) * E].rearrange("p a k n -> p (a k) n")
                nc.tensor.matmul(psum[:, 6 + u, :], hid_hi[:, u, j * P:(j + 1) * P], both, start=(j == 0), stop=False,
                                 skip_group_check=True)
                return nc.tensor.matmul(psum[:, 6 + u, E:2 * E], hid_lo[:, u, j * P:(j + 1) * P], high, start=False,
                                        stop=(j == FB - 1), skip_group_check=True)

            def products(s, u, e_up, e_down):
                if e_up is not None:
                    pe.wait_ge(rows_low, s)
                if e_down is not None:
                    pe.wait_ge(hid_low, s - 2)
                    if past(s, 5):
                        pe.wait_ge(y_copied, s - 4)
                for j in range(FB):
                    if e_up is not None:
                        last_up = up(1 - u, e_up, j)
                    if e_down is not None:
                        last_down = down(1 - u, e_down, j)
                if e_up is not None:
                    last_up.then_inc(up_done, 1)
                if e_down is not None:
                    last_down.then_inc(down_done, 1)

            def expert(word, lots_back):
                return (word >> {0: 0, -1: 3, 2: 6, 1: 9, 4: 12, 3: 15}[lots_back]) & (N_EXP - 1)

            def load_word(i):
                return pe.value_load(slot_word[0:1, bass.ds(i, 1)], min_val=0, max_val=N_EXP ** 6 - 1)
            word = None

            def lot(s, u, i):
                nonlocal word
                if u == 0:
                    word = load_word(i)
                transpose_rows(s, u, i)
                products(s, u, expert(word, 1 - u) if past(s, 1) else None, expert(word, 3 - u) if past(s, 3) else None)
            steps(pe, SLOTS, lot, 6)
            word = load_word(SLOTS // 2 - 1)
            products(SLOTS, 0, expert(word, -1), expert(word, 1))
            products(SLOTS + 1, 1, None, expert(word, 0))
            products(SLOTS + 2, 0, None, expert(word, -1))

        @block.scalar
        def _(act):
            def square(t, u):
                act.wait_ge(centred, t + 1)
                if past(t, 2):
                    act.wait_ge(var_done, t - 1)
                nc.scalar.activation(sq_qk[:, u, :], cen_qk[:, u, :], ACT.Square).then_inc(squared, 1)

            def silu(t, u, i):
                act.wait_ge(qkv_done, t + 1)
                if past(t, 2):
                    act.wait_ge(centred, t - 1)
                nc.scalar.activation(act_qk[:, u, :], psum[:, u, :], ACT.Silu)
                nc.scalar.activation(row(v_all, t + R), psum[:, 2 + u:3 + u, 0:E], ACT.Silu)
                nc.scalar.activation(row(win, t), psum[:, 2 + u:3 + u, E:E + 2 * H], ACT.Silu).then_inc(silu_done, 1)
                if past(t, 1):
                    square(t - 1, 1 - u)
            steps(act, CHUNK, silu, 4)
            square(CHUNK - 1, 1)
            act.wait_ge(silu_done, CHUNK)
            nc.scalar.activation(win[:, :, :], win[:, :, :], ACT.Sigmoid).then_inc(sig_done, 1)
            act.wait_ge(var_eps, 1)
            nc.scalar.activation(head_rstd[:, :, :], head_var[:, :, :], ACT.Sqrt).then_inc(root_done, 1)
            act.wait_ge(gate_arg, 1)
            nc.scalar.activation(gate[:, :, :, :], gate[:, :, :, :], ACT.Sigmoid).then_inc(gate_done, 1)

            def mixed_out(t, u):
                act.wait_ge(av_used, 2 * t + 2)
                if past(t, 2):
                    act.wait_ge(y_done, t - 1)
                nc.scalar.activation(mixed_t[:, u], psum[:, 2 * u:2 * u + 2, 0:P], ACT.Copy).then_inc(mixed_copied, 1)
                act.wait_ge(y_done, t + 1)
                if past(t, 2):
                    act.wait_ge(res_summed, t - 1)
                nc.scalar.activation(tanh_y[:, u, :], psum[:, 4 + u, 0:E], ACT.Tanh, scale=0.5).then_inc(tanh_done, 1)
                nc.scalar.activation(y_sb[:, u, :], psum[:, 4 + u, 0:E], ACT.Copy)
                act.wait_ge(tanh_done, t + 1)
                nc.scalar.activation(tanh_y[:, u, :], tanh_y[:, u, :], ACT.Copy, scale=0.5, bias=0.5).then_inc(y_parts, 1)

            def window(t, u, i):
                act.wait_ge(score_ready, t + 1)
                nc.scalar.activation(score[:, u, :], score[:, u, :], ACT.Exp, scale=SCALE).then_inc(exp_done, 1)
                if past(t, 2):
                    mixed_out(t - 2, u)
                if past(t, 3):
                    keep(t - 3, 1 - u)
                square_weights(t, u, i)

            def square_weights(t, u, i):
                act.wait_ge(w_piece_loaded, 32 * t + 32)
                for k in range(2):
                    nc.scalar.activation(w_piece[:, k, :], w_piece[:, k, :], ACT.Square,
                                         accum_out=w_squares[:, k, bass.ds(t, 1)]).then_inc(w_squared, 1)

            def keep(t, u):
                act.wait_ge(res_done, t + 1)
                nc.scalar.activation(row(q_all, t), x_res[:, u:u + 1, :], ACT.Copy)
                nc.scalar.activation(row(stats, t), bn6[:, u:u + 1, :], ACT.Copy).then_inc(res_kept, 1)

            def norm1(g):
                act.wait_ge(norm1_shift, g + 1)
                for t in range(g * GROUP, (g + 1) * GROUP):
                    nc.scalar.activation(q_all[:, t, :], q_all[:, t, :], ACT.Identity, bias=mean1[:, t:t + 1],
                                         scale=rstd1[:, t:t + 1]).then_inc(x1_ready, 1)
            for g in range(GROUPS):
                steps(act, (g + 1) * GROUP, window, 6, g * GROUP)
                if g >= 2:
                    norm1(g - 2)
            mixed_out(CHUNK - 2, 0)
            keep(CHUNK - 3, 1)
            mixed_out(CHUNK - 1, 1)
            keep(CHUNK - 2, 0)
            keep(CHUNK - 1, 1)
            norm1(GROUPS - 2)

            def attend(b, u, i):
                act.wait_ge(x1t_done, b + 1)
                if past(b, 2):
                    act.wait_ge(router_done, b - 1)
                nc.scalar.activation(tok_t[:, 0, :], psum[:, 6, :], ACT.Copy).then_inc(tok_copied, 1)

                if past(b, 1):
                    high_part(b - 1, 0)

                def exp(t):
                    act.wait_ge(peak_ready, QT * b + t + 1)
                    if t >= 2:
                        act.wait_ge(pt_done, QT * b + t - 1)
                    elif past(b, 1):
                        act.wait_ge(pt_done, QT * b + t - 1)
                    nc.scalar.activation(probs[:, t % 2, 0:(t + 1) * P], psum[:, t, 0:(t + 1) * P], ACT.Exp,
                                         bias=bias2[:, u, t:t + 1], scale=1.0 / E ** 0.5,
                                         accum_out=row_sum[:, u, t:t + 1]).then_inc(exp2_done, 1)

                def copy(t):
                    act.wait_ge(pt_done, QT * b + t + 1)
                    if t >= 2:
                        act.wait_ge(av_done, QT * b + t - 1)
                    elif past(b, 1):
                        act.wait_ge(av_done, QT * b + t - 1)
                    nc.scalar.activation(probs_t[:, t % 2, 0:t + 1, :], psum[:, 4 + t % 2, 0:(t + 1) * P].rearrange(
                        "p (k n) -> p k n", n=P), ACT.Copy).then_inc(pt_copied, 1)
                exp(0)
                exp(1)
                if past(b, 1):
                    x2_transposed(b - 1)
                copy(0)
                exp(2)
                copy(1)
                exp(3)
                copy(2)
                copy(3)
                if past(b, 1):
                    high_part(b - 1, 1)

            def high_part(e, k):
                act.wait_ge(w_loaded, 32 * e + 32)
                act.wait_ge(w_scaled, 1)
                matrix = w_f32[:, bass.ds(e, 1), k, :]
                nc.scalar.activation(matrix, matrix, ACT.Identity, scale=w_scale[:, k:k + 1]).then_inc(w_multiplied, 1)
                act.wait_ge(w_multiplied, 2 * e + k + 1)
                if k or past(e, 1):
                    act.wait_ge(w_low_made, 2 * e + k)
                nc.scalar.activation(w_high[:, bass.ds(e, 1), k, 0:EW], matrix, ACT.Copy).then_inc(w_high_made, 1)

            def x2_transposed(b):
                act.wait_ge(x2t_done, b + 1)
                nc.scalar.activation(tok_t[:, 0, :], psum[:, 6, :], ACT.Copy).then_inc(x2t_copied, 1)
            act.wait_ge(x1_last, GROUP)
            steps(act, B, attend)
            x2_transposed(B - 1)
            high_part(N_EXP - 1, 0)
            high_part(N_EXP - 1, 1)

            act.wait_ge(gap_made, 1)
            nc.scalar.activation(top_v[:, 1, :], top_v[:, 1, :], ACT.Exp).then_inc(gap_exp, 1)

            def lot(s, u, i):
                act.wait_ge(rows_t_done, s + 1)
                nc.scalar.activation(rows_hi[:, u, :], psum[:, u, 0:E], ACT.Copy, scale=2.0 ** X_BITS).then_inc(rows_high, 1)
                if past(s, 3):
                    result_beside(s - 3, 1 - u)
                if past(s, 1):
                    gelu(s - 1, 1 - u)

            def result_beside(s, u):
                act.wait_ge(down_done, s + 1)
                if past(s, 2):
                    act.wait_ge(y_copied, s - 1)
                nc.scalar.activation(y_side[:, u, :], psum[:, 6 + u, E:2 * E], ACT.Identity, scale=y_scale1).then_inc(y_beside, 1)

            def gelu(s, u):
                act.wait_ge(up_done, s + 1)
                if past(s, 2):
                    act.wait_ge(hid_low, s - 1)
                nc.scalar.activation(hid[:, u, :].rearrange("p (h f) -> p h f", h=2), psum[:, 2 + 2 * u:4 + 2 * u, :], ACT.Gelu,
                                     scale=up_scale).then_inc(gelu_done, 1)
            act.wait_ge(routed, 1)
            steps(act, SLOTS, lot, 6)
            result_beside(SLOTS - 3, 1)
            gelu(SLOTS - 1, 1)
            result_beside(SLOTS - 2, 0)
            result_beside(SLOTS - 1, 1)

            def norm3(g, u, i):
                if past(g, 2):
                    act.wait_ge(out_stored[u], 16 * i)
                act.wait_ge(shift3_made, g + 1)
                for t in range(QT):
                    nc.scalar.activation(out_rows[:, u, t, :], sum3[:, u, t, :], ACT.Identity, bias=mean3[:, u, t:t + 1],
                                         scale=rstd3[:, u, t:t + 1]).then_inc(out_ready, 1)
                act.wait_ge(out_ready, QT * (g + 1))
                act.dma_start(out_group[bass.ds(g, 1)].rearrange("a (t p) e -> p (a t) e", p=P),
                              out_rows[:, u]).then_inc(out_stored[u], 16)
            steps(act, TILES // QT, norm3)

        @block.gpsimd
        def _(pool):
            def done(ins, signal, count):
                ins.then_inc(signal, 1)
                pool.wait_ge(signal, count)

            nc.gpsimd.memset(k_all[:, 0:R, :], 0.0).then_inc(halo_zeroed, 1)
            nc.gpsimd.memset(k_all[:, R + CHUNK:ROWS, :], 0.0).then_inc(halo_zeroed, 1)
            nc.gpsimd.memset(v_all[:, 0:R, :], 0.0).then_inc(halo_zeroed, 1)
            nc.gpsimd.memset(v_all[:, R + CHUNK:ROWS, :], 0.0).then_inc(halo_zeroed, 1)
            nc.gpsimd.memset(ones_pp[:, :], 1.0).then_inc(fills_made, 1)
            nc.gpsimd.memset(minus_half[:, :], -0.5).then_inc(fills_made, 1)
            pool.wait_ge(fills_made, 2)

            def gain_qk(t, u, i):
                pool.wait_ge(centred, t + 1)
                for m, dst in enumerate((row(q_all, t), row(k_all, t + R))):
                    heads = cen_qk[:, u, m * E:(m + 1) * E].rearrange("p (h d) -> p h d", d=D)
                    nc.gpsimd.tensor_tensor(dst.rearrange("p a (h d) -> p (a h) d", d=D), heads,
                                            gains[:, m:m + 1, :].to_broadcast([P, H, D]), ALU.mult).then_inc(gained, 1)

            pool.wait_ge(weights_loaded, WEIGHT_LOADS)
            steps(pool, CHUNK, gain_qk)
            pool.wait_ge(gained, 2 * CHUNK)
            pool.wait_ge(rstd_heads, 1)
            for g in range(2):
                part = q_all[:, g * CHUNK // 2:(g + 1) * CHUNK // 2, :].rearrange("p s (h d) -> p s h d", d=D)
                scale = head_rstd[:, g * CHUNK // 2:(g + 1) * CHUNK // 2, 0:H].unsqueeze(3)
                nc.gpsimd.tensor_tensor(part, part, scale.to_broadcast([P, CHUNK // 2, H, D]), ALU.mult).then_inc(q_scaled, 1)
            pool.wait_ge(gate_done, 1)

            def weigh_values(t, u):
                pool.wait_ge(inv_ready, t + 1)
                done(nc.gpsimd.tensor_tensor(prob[:, u, :].rearrange("p (w h) -> p w h", h=H),
                                             score[:, u, :].rearrange("p (w h) -> p w h", h=H),
                                             inv_total[:, u, :].unsqueeze(1).to_broadcast([P, K, H]), ALU.mult), prob_made, t + 1)
                for half, (a, n) in enumerate(((0, W0), (W0, K - W0))):
                    if past(t, 1):
                        pool.wait_ge(av_used, 2 * t + half - 1)
                    values = v_all[:, bass.ds(t + a, n), :].rearrange("p w (h d) -> p (w h) d", d=D)
                    weights = prob[:, u, a * H:(a + n) * H].unsqueeze(2).to_broadcast([P, n * H, D])
                    nc.gpsimd.tensor_tensor(av_prod[half][:, :, :].rearrange("p w (h d) -> p (w h) d", d=D),
                                            values, weights, ALU.mult).then_inc(av_ready, 1)

            def silu(t, u):
                pool.wait_ge(y_parts, t + 1)
                nc.gpsimd.tensor_tensor(tanh_y[:, u, :], tanh_y[:, u, :], y_sb[:, u, :], ALU.mult).then_inc(silu_y_made, 1)

            def window(t, u, i):
                pool.wait_ge(peak_found, t + 1)
                scores = score[:, u, :].rearrange("p (w h) -> p w h", h=H)
                nc.gpsimd.tensor_tensor(scores, scores, peak[:, u, :].unsqueeze(1).to_broadcast([P, K, H]),
                                        ALU.subtract).then_inc(score_ready, 1)
                if past(t, 1):
                    weigh_values(t - 1, 1 - u)
                if past(t, 2):
                    silu(t - 2, u)

            def root(var, n, count):
                pool.wait_ge(var_made, count)
                nc.gpsimd.tensor_tensor(var, var, minus_half[:, 0:n], ALU.pow).then_inc(rstd_ready, 1)

            for g in range(GROUPS):
                steps(pool, (g + 1) * GROUP, window, 6, g * GROUP)
                if g >= 1:
                    root(rstd1[:, (g - 1) * GROUP:g * GROUP], GROUP, g)
            weigh_values(CHUNK - 1, 1)
            silu(CHUNK - 2, 0)
            silu(CHUNK - 1, 1)
            root(rstd1[:, CHUNK - GROUP:], GROUP, GROUPS)

            def low_part(e, k):
                pool.wait_ge(w_high_made, 2 * e + k + 1)
                nc.gpsimd.tensor_tensor(w_low[:, bass.ds(e, 1), k, 0:EW], w_f32[:, bass.ds(e, 1), k, :],
                                        w_high[:, bass.ds(e, 1), k, 0:EW], ALU.subtract).then_inc(w_low_made, 1)

            def attend(b, u, i):
                if past(b, 1):
                    low_part(b - 1, 0)
                root(rstd2[:, u, :], QT, GROUPS + b + 1)
                if past(b, 1):
                    low_part(b - 1, 1)
            steps(pool, B, attend)
            low_part(N_EXP - 1, 0)
            low_part(N_EXP - 1, 1)

            pool.wait_ge(routed, 1)
            for u in (0, 1):
                pool.wait_ge(x2_stored[u], 16 * (B // 2))

            def lot(s, u, i):
                if past(s, 2):
                    pool.wait_ge(rows_t_done, s - 1)
                nc.gpsimd.tensor_copy(src_col[:, u, :], slot_src[:, bass.ds(s, 1)]).then_inc(src_copied, 1)
                pool.wait_ge(src_copied, s + 1).then_inc(pool_waited, 1)
                nc.gpsimd.indirect_dma_start(rows[:, u, :], None, x2_dram, bass.IndirectOffsetOnAxis(src_col[:, u, :], 0)
                                             ).then_inc(rows_loaded[u], 16)
                if past(s, 4):
                    send(s - 4, u, i - 2)

            def send(s, u, i):
                pool.wait_ge(y_copied, s + 1)
                if past(s, 2):
                    pool.wait_ge(ys_stored[u], 16 * i)
                nc.gpsimd.tensor_copy(dst_col[:, u, :], slot_dst[:, bass.ds(s, 1)]).then_inc(dst_copied, 1)
                pool.wait_ge(dst_copied, s + 1).then_inc(pool_waited, 1)
                nc.gpsimd.indirect_dma_start(ys_dram, bass.IndirectOffsetOnAxis(dst_col[:, u, :], 0), y_rows[:, u, :], None
                                             ).then_inc(ys_stored[u], 16)
            steps(pool, SLOTS, lot, 6)
            send(SLOTS - 4, 0, SLOTS // 2 - 2)
            send(SLOTS - 3, 1, SLOTS // 2 - 2)
            send(SLOTS - 2, 0, SLOTS // 2 - 1)
            send(SLOTS - 1, 1, SLOTS // 2 - 1)
            steps(pool, TILES // QT, lambda g, u, i: root(rstd3[:, u, :], QT, GROUPS + B + g + 1))

        @block.vector
        def _(dve):
            def done(ins, signal, count):
                ins.then_inc(signal, 1)
                dve.wait_ge(signal, count)

            def moments(st, mean, var, count):
                done(nc.vector.tensor_tensor(mean, st[:, :, 1], st[:, :, 4], ALU.subtract), mean_diff, count + 1)
                done(nc.vector.tensor_tensor(var, mean, mean, ALU.mult), mean_diff_sq, count + 1)
                nc.vector.tensor_tensor(mean, st[:, :, 1], st[:, :, 4], ALU.add).then_inc(mean_added, 1)
                done(nc.vector.tensor_scalar(var, var, 0.25, EPS, ALU.mult, ALU.add), var_between, count + 1)
                done(nc.vector.scalar_tensor_tensor(var, st[:, :, 2], 1.0 / E, var, ALU.mult, ALU.add), var_even, count + 1)
                dve.wait_ge(mean_added, count + 1)
                nc.vector.tensor_scalar(mean, mean, 0.5, None, ALU.mult)
                nc.vector.scalar_tensor_tensor(var, st[:, :, 5], 1.0 / E, var, ALU.mult, ALU.add).then_inc(var_made, 1)

            def variance(t, u):
                dve.wait_ge(squared, t + 1).then_inc(dve_waited, 1)
                nc.vector.tensor_reduce(row(head_var, t).rearrange("p a x -> p (a x)"),
                                        sq_qk[:, u, :].rearrange("p (x d) -> p x d", d=D),
                                        op=ALU.add, axis=AX.X).then_inc(var_done, 1)

            def centre(t, u, i):
                dve.wait_ge(silu_done, t + 1)
                heads = act_qk[:, u, :].rearrange("p (x d) -> p x d", d=D)
                done(nc.vector.tensor_reduce(head_sum[:, u, :], heads, op=ALU.add, axis=AX.X), head_mean_summed, t + 1)
                if past(t, 2):
                    dve.wait_ge(gained, 2 * t - 2)
                nc.vector.scalar_tensor_tensor(cen_qk[:, u, :].rearrange("p (x d) -> p x d", d=D),
                                               head_sum[:, u, :].unsqueeze(2).to_broadcast([P, 2 * H, D]), -1.0 / D, heads,
                                               ALU.mult, ALU.add).then_inc(centred, 1)
                if past(t, 1):
                    variance(t - 1, 1 - u)
            dve.wait_ge(weights_loaded, WEIGHT_LOADS)
            steps(dve, CHUNK, centre, 4)
            variance(CHUNK - 1, 1)

            dve.wait_ge(var_done, CHUNK)
            done(nc.vector.tensor_scalar(head_var[:, :, :], head_var[:, :, :], 1.0 / D, EPS, ALU.mult, ALU.add), var_eps, 1)
            dve.wait_ge(sig_done, 1)
            nc.vector.tensor_scalar(sharp[:, :, :], win[:, :, H:2 * H], 9.5, 0.5, ALU.mult, ALU.add).then_inc(width_done, 1)
            nc.vector.tensor_scalar(edge[:, :, :], win[:, :, 0:H], float(R), 0.5, ALU.mult, ALU.add).then_inc(width_done, 1)
            dve.wait_ge(width_done, 2)
            done(nc.vector.tensor_tensor(edge[:, :, :], edge[:, :, :], sharp[:, :, :], ALU.mult), width_done, 3)
            dve.wait_ge(root_done, 1)
            done(nc.vector.reciprocal(head_rstd[:, :, :], head_rstd[:, :, :]), newton_step, 1)
            done(nc.vector.tensor_tensor(newton[:, :, :], head_var[:, :, :], head_rstd[:, :, :], ALU.mult), newton_step, 2)
            done(nc.vector.tensor_tensor(newton[:, :, :], newton[:, :, :], head_rstd[:, :, :], ALU.mult), newton_step, 3)
            done(nc.vector.tensor_scalar(newton[:, :, :], newton[:, :, :], -0.5, 1.5, ALU.mult, ALU.add), newton_step, 4)
            done(nc.vector.tensor_tensor(head_rstd[:, :, :], head_rstd[:, :, :], newton[:, :, :], ALU.mult), rstd_heads, 1)
            dve.wait_ge(gained, 2 * CHUNK)
            keys = k_all[:, R:R + CHUNK, :].rearrange("p s (h d) -> p s h d", d=D)
            done(nc.vector.tensor_tensor(keys, keys, head_rstd[:, :, H:2 * H].unsqueeze(3).to_broadcast([P, CHUNK, H, D]),
                                         ALU.mult), k_scaled, 1)
            keys = k_all[:, R:R + CHUNK, :].rearrange("p s (h d) -> p (s h) d", d=D)
            nc.vector.tensor_tensor(keys, keys, biases[:, 1:2, :].to_broadcast([P, CHUNK * H, D]), ALU.add).then_inc(k_ready, 1)
            for r in range(R + 1):
                nc.vector.scalar_tensor_tensor(gate[:, :, r, :], sharp[:, :, :], float(r), edge[:, :, :], ALU.mult,
                                               ALU.subtract).then_inc(gate_args, 1)
            dve.wait_ge(gate_args, R + 1).then_inc(gate_arg, 1)
            for g in range(2):
                dve.wait_ge(q_scaled, g + 1)
                part = q_all[:, g * CHUNK // 2:(g + 1) * CHUNK // 2, :].rearrange("p s (h d) -> p (s h) d", d=D)
                nc.vector.tensor_tensor(part, part, biases[:, 0:1, :].to_broadcast([P, CHUNK // 2 * H, D]),
                                        ALU.add).then_inc(q_ready, 1)
            dve.wait_ge(q_ready, 2)
            dve.wait_ge(gate_done, 1)

            def window(t, u, i):
                queries = row(q_all, t).to_broadcast([P, K, E])
                nc.vector.tensor_tensor(qk_prod[:, :].rearrange("p (w c) -> p w c", c=E), queries,
                                        k_all[:, bass.ds(t, K), :], ALU.mult).then_inc(qk_multiplied, 1)
                if past(t, 1):
                    sum_up(t - 1, 1 - u)
                dve.wait_ge(qk_multiplied, t + 1)
                if past(t, 2):
                    dve.wait_ge(prob_made, t - 1)
                nc.vector.tensor_reduce(score[:, u, :], qk_prod[:, :].rearrange("p (x d) -> p x d", d=D),
                                        op=ALU.add, axis=AX.X).then_inc(qk_summed, 1)
                if past(t, 1):
                    invert(t - 1, 1 - u)
                by_offset = score[:, u, :].rearrange("p (w h) -> p w h", h=H)
                gates = row(gate, t).rearrange("p a r h -> p (a r) h")
                dve.wait_ge(qk_summed, t + 1)
                nc.vector.scalar_tensor_tensor(by_offset[:, R:, :], gates, -PENALTY / SCALE, by_offset[:, R:, :],
                                               ALU.mult, ALU.add).then_inc(penalised, 1)
                nc.vector.scalar_tensor_tensor(by_offset[:, R - 1::-1, :], gates[:, 1:, :], -PENALTY / SCALE,
                                               by_offset[:, R - 1::-1, :], ALU.mult, ALU.add).then_inc(penalised, 1)
                if past(t, 3):
                    add_x(t - 3, 1 - u, i - 2 + u)
                dve.wait_ge(penalised, 2 * t + 2)
                nc.vector.tensor_reduce(peak[:, u, :], score[:, u, :].rearrange("p (w h) -> p h w", h=H), op=ALU.max,
                                        axis=AX.X).then_inc(peak_found, 1)
                if past(t, 3):
                    take_stats(t - 3, 1 - u)

            def sum_up(t, u):
                dve.wait_ge(exp_done, t + 1)
                nc.vector.tensor_reduce(total[:, u, :], score[:, u, :].rearrange("p (w h) -> p h w", h=H), op=ALU.add,
                                        axis=AX.X).then_inc(total_found, 1)

            def invert(t, u):
                dve.wait_ge(total_found, t + 1)
                nc.vector.reciprocal(inv_total[:, u, :], total[:, u, :]).then_inc(inv_ready, 1)

            def add_x(t, u, i):
                dve.wait_ge(silu_y_made, t + 1)
                dve.wait_ge(x_res_loaded[u], 16 * i + 16)
                nc.vector.tensor_tensor(x_res[:, u, :], x_res[:, u, :], tanh_y[:, u, :], ALU.add).then_inc(res_summed, 1)

            def take_stats(t, u):
                dve.wait_ge(res_summed, t + 1)
                if past(t, 2):
                    dve.wait_ge(res_kept, t - 1)
                nc.vector.bn_stats(bn6[:, u, :], x_res[:, u, :]).then_inc(res_done, 1)

            def group_moments(g):
                part = slice(g * GROUP, (g + 1) * GROUP)
                dve.wait_ge(res_kept, (g + 1) * GROUP)
                moments(stats[:, part], mean1[:, part], rstd1[:, part], g)

            def group_shift(g):
                part = slice(g * GROUP, (g + 1) * GROUP)
                dve.wait_ge(rstd_ready, g + 1)
                nc.vector.scalar_tensor_tensor(mean1[:, part], mean1[:, part], -1.0, rstd1[:, part], ALU.mult,
                                               ALU.mult).then_inc(norm1_shift, 1)
            dve.wait_ge(halo_loaded, 16 * 4 * B)
            for g in range(GROUPS):
                steps(dve, (g + 1) * GROUP, window, 6, g * GROUP)
                if g >= 2:
                    group_shift(g - 2)
                if g >= 1:
                    group_moments(g - 1)
            sum_up(CHUNK - 1, 1)
            invert(CHUNK - 1, 1)
            for t in range(CHUNK - 3, CHUNK):
                add_x(t, t % 2, t // 2)
                take_stats(t, t % 2)

            dve.wait_ge(w_squared, 2 * CHUNK).then_inc(dve_waited, 1)
            nc.vector.tensor_reduce(w_sum[:, :], w_squares[:, :, :], op=ALU.add, axis=AX.X).then_inc(w_summed, 1)

            group_shift(GROUPS - 2)
            group_moments(GROUPS - 1)
            dve.wait_ge(rstd_ready, GROUPS)
            for t in range(CHUNK - GROUP, CHUNK):
                nc.vector.tensor_scalar(q_all[:, t, :], q_all[:, t, :], mean1[:, t:t + 1], rstd1[:, t:t + 1], ALU.subtract,
                                        ALU.mult).then_inc(x1_last, 1)
            dve.wait_ge(w_total, 1)
            done(nc.vector.tensor_copy(w_sum[:, :], psum[:, 0, 0:2]), w_exps, 1)
            done(nc.vector.tensor_scalar(w_exp, w_sum[:, :].bitcast(I32), F32_MANT, None, ALU.logical_shift_right), w_exps, 2)
            done(nc.vector.tensor_scalar(w_exp, w_exp, F32_BIAS + 2, None, ALU.add), w_exps, 3)
            done(nc.vector.tensor_scalar(w_exp, w_exp, 1, None, ALU.logical_shift_right), w_exps, 4)
            hid_bits = TOP_BITS - (E.bit_length() - 1) // 2
            for col, k, sign, add in ((0, 0, -1, 2 * F32_BIAS + TOP_BITS), (1, 1, -1, 2 * F32_BIAS + TOP_BITS),
                                      (2, 0, 1, -X_BITS - TOP_BITS), (3, 0, -1, 2 * F32_BIAS + hid_bits),
                                      (4, 0, 1, -hid_bits), (5, 1, 1, -TOP_BITS)):
                nc.vector.tensor_scalar(scale_bits[:, col:col + 1], w_exp[:, k:k + 1], sign, add, ALU.mult, ALU.add).then_inc(w_exps, 1)
            dve.wait_ge(w_exps, 10)
            nc.vector.tensor_scalar(scale_bits[:, 0:6], scale_bits[:, 0:6], F32_MANT, None, ALU.logical_shift_left).then_inc(w_scaled, 1)

            def attend(b, u, i):
                dve.wait_ge(x1t_done, b + 1)
                if past(b, 2):
                    dve.wait_ge(router_done, b - 1)
                nc.vector.tensor_copy(tok_t[:, 1, :], psum[:, 7, :]).then_inc(tok_copied, 1)
                if past(b, 1):
                    norm2(b - 1, 1 - u)
                for t in range(QT):
                    dve.wait_ge(s_done, QT * b + t + 1)
                    diag = psum[:, t, t * P:(t + 1) * P]
                    done(nc.vector.tensor_tensor(diag, diag, consts[:, AT_MASK:AT_MASK + P], ALU.add), masked, QT * b + t + 1)
                    done(nc.vector.tensor_reduce(top_peak[:, u, t:t + 1], psum[:, t, 0:(t + 1) * P], op=ALU.max, axis=AX.X),
                         peak_neg, QT * b + t + 1)
                    nc.vector.tensor_scalar(bias2[:, u, t:t + 1], top_peak[:, u, t:t + 1], -1.0 / E ** 0.5, None,
                                            ALU.mult).then_inc(peak_ready, 1)
                if past(b, 1):
                    choose(b - 1, 1 - u)
                for t in range(QT):
                    dve.wait_ge(av_done, QT * b + t + 1)
                    done(nc.vector.reciprocal(inv_row[:, u, t:t + 1], row_sum[:, u, t:t + 1]), inv2_made, QT * b + t + 1)
                    nc.vector.scalar_tensor_tensor(x1_n[:, u, t, :], psum[:, 6 + t % 2, 0:E], inv_row[:, u, t:t + 1],
                                                   x1_n[:, u, t, :], ALU.mult, ALU.add).then_inc(sum2_done, 1)
                    dve.wait_ge(sum2_done, QT * b + t + 1)
                    nc.vector.bn_stats(stats2[:, u, t, :], x1_n[:, u, t, :]).then_inc(stats2_done, 1)
                dve.wait_ge(stats2_done, QT * (b + 1))
                moments(stats2[:, u], mean2[:, u, :], rstd2[:, u, :], GROUPS + b)

            def norm2(b, u):
                dve.wait_ge(rstd_ready, GROUPS + b + 1)
                for t in range(QT):
                    nc.vector.tensor_scalar(x1_n[:, u, t, :], x1_n[:, u, t, :], mean2[:, u, t:t + 1], rstd2[:, u, t:t + 1],
                                            ALU.subtract, ALU.mult).then_inc(normed2, 1)
                dve.wait_ge(normed2, QT * (b + 1))
                nc.vector.tensor_copy(x2[:, bass.ds(QT * b, QT), :], x1_n[:, u]).then_inc(x2_ready, QT)

            def choose(b, u):
                dve.wait_ge(x2t_done, b + 1)
                nc.vector.tensor_copy(tok_t[:, 1, :], psum[:, 7, :]).then_inc(x2t_copied, 1)
                dve.wait_ge(router_done, b + 1)
                nc.vector.tensor_copy(logits[:, u].rearrange("p t n -> p (t n)"), psum[:, 5, 0:QT * N_EXP]).then_inc(logits_copied, 1)
                dve.wait_ge(logits_copied, b + 1).then_inc(dve_waited, 1)
                for t in range(QT):
                    nc.vector.max(top8[:, u, t, :], logits[:, u, t, :]).then_inc(top_found, 1)
                dve.wait_ge(top_found, QT * (b + 1)).then_inc(dve_waited, 1)
                for t in range(QT):
                    nc.vector.max_index(where8[:, u, t, :].bitcast(U32), top8[:, u, t, :], logits[:, u, t, :]).then_inc(where_found, 1)
                dve.wait_ge(where_found, QT * (b + 1))
                nc.vector.tensor_copy(top_v[:, :, bass.ds(QT * b, QT)], top8[:, u, :, 0:TOP].rearrange("p t k -> p k t"))
                nc.vector.tensor_copy(top_i[:, :, bass.ds(QT * b, QT)],
                                      where8[:, u, :, 0:TOP].bitcast(U32).rearrange("p t k -> p k t")).then_inc(top_kept, 1)
            steps(dve, B, attend)
            norm2(B - 1, 1)
            choose(B - 1, 1)

            dve.wait_ge(top_kept, B)
            nc.vector.tensor_tensor(top_v[:, 1, :], top_v[:, 1, :], top_v[:, 0, :], ALU.subtract).then_inc(gap_made, 1)
            count = consts[:, AT_COUNT:AT_COUNT + P]
            done(nc.vector.tensor_tensor(chosen, top_i.unsqueeze(3).to_broadcast([P, TOP, TILES, N_EXP]),
                                         count[:, 0:N_EXP].unsqueeze(1).unsqueeze(1).to_broadcast([P, TOP, TILES, N_EXP]),
                                         ALU.is_equal), chosen_made, 1)
            nc.vector.tensor_tensor(picked, chosen[:, 0], chosen[:, 1], ALU.add).then_inc(picked_made, 1)
            dve.wait_ge(counted, 1)
            tile_count = psum[:, 1, 0:TILES * N_EXP].rearrange("p (t n) -> p t n", n=N_EXP)
            n_scan = 1
            done(nc.vector.tensor_copy(upto[0], tile_count), scan_step, n_scan)
            at, hop = 0, 1
            while hop < TILES:
                nc.vector.tensor_copy(upto[1 - at][:, 0:hop, :], upto[at][:, 0:hop, :])
                n_scan += 1
                done(nc.vector.tensor_tensor(upto[1 - at][:, hop:, :], upto[at][:, hop:, :], upto[at][:, 0:TILES - hop, :],
                                             ALU.add), scan_step, n_scan)
                at, hop = 1 - at, 2 * hop
            n_lots = 0

            def lots_done(ins):
                nonlocal n_lots
                n_lots += 1
                done(ins, lots_step, n_lots)
            lots_done(nc.vector.tensor_scalar(lots_i, upto[at][:, TILES - 1, :], float(P - 1), None, ALU.add))
            lots_done(nc.vector.tensor_scalar(lots_i, lots_i, P.bit_length() - 1, None, ALU.logical_shift_right))
            lots_done(nc.vector.tensor_copy(lots_n, lots_i))
            lots_done(nc.vector.tensor_copy(lots[:, 0, :], lots_n))
            now, hop = 0, 1
            while hop < N_EXP:
                nc.vector.tensor_copy(lots[:, 1 - now, 0:hop], lots[:, now, 0:hop])
                lots_done(nc.vector.tensor_tensor(lots[:, 1 - now, hop:], lots[:, now, hop:], lots[:, now, 0:N_EXP - hop], ALU.add))
                now, hop = 1 - now, 2 * hop
            lots_end = lots[:, now, :]
            done(nc.vector.tensor_tensor(place, upto[at], tile_count, ALU.subtract), place_made, 1)
            done(nc.vector.tensor_tensor(place, place, psum[:, 0, 0:TILES * N_EXP].rearrange("p (t n) -> p t n", n=N_EXP),
                                         ALU.add), place_made, 2)
            lots_done(nc.vector.tensor_tensor(lots_n, lots_end, lots_n, ALU.subtract))
            lots_done(nc.vector.tensor_scalar(lots_n, lots_n, float(P), None, ALU.mult))
            done(nc.vector.tensor_tensor(place, place, lots_n.unsqueeze(1).to_broadcast([P, TILES, N_EXP]), ALU.add), place_made, 3)
            done(nc.vector.tensor_tensor(placed, chosen, place.unsqueeze(1).to_broadcast([P, TOP, TILES, N_EXP]), ALU.mult),
                 placed_made, 1)
            done(nc.vector.tensor_reduce(spot, placed, op=ALU.add, axis=AX.X), spot_made, 1)
            done(nc.vector.tensor_copy(spot_i[:, 0], spot), spot_int, 1)
            nc.vector.tensor_scalar(spot_i[:, 1], spot_i[:, 0], P.bit_length() - 1, None, ALU.logical_shift_right).then_inc(spot_parts, 1)
            dve.wait_ge(spot_parts, 1)
            done(nc.vector.tensor_scalar(spot_i[:, 0], spot_i[:, 0], P - 1, None, ALU.bitwise_and), spot_parts, 2)
            flat = "p k t -> p (k t)"
            nc.vector.tensor_copy(spot_slot, spot_i[:, 1].rearrange(flat)).then_inc(spot_back, 1)
            done(nc.vector.tensor_copy(spot_row, spot_i[:, 0].rearrange(flat)), spot_back, 2)
            n_pairs = TOP * TILES
            nc.vector.tensor_tensor(is_row, spot_row.unsqueeze(2).to_broadcast([P, n_pairs, P]),
                                    count.unsqueeze(1).to_broadcast([P, n_pairs, P]), ALU.is_equal).then_inc(rows_marked, 1)
            done(nc.vector.tensor_tensor(is_slot[:, :, SLOTS:], spot_slot.unsqueeze(2).to_broadcast([P, n_pairs, SLOTS]),
                                         count[:, 0:SLOTS].unsqueeze(1).to_broadcast([P, n_pairs, SLOTS]), ALU.is_equal),
                 slot_hits, 1)
            nc.vector.tensor_tensor(is_slot[:, :, 0:SLOTS], is_slot[:, :, SLOTS:],
                                    consts[:, AT_TILE:AT_TILE + n_pairs].unsqueeze(2).to_broadcast([P, n_pairs, SLOTS]),
                                    ALU.mult).then_inc(slots_marked, 1)
            dve.wait_ge(slots_marked, 1)
            nc.vector.tensor_scalar(is_slot[:, :, SLOTS:], is_slot[:, :, SLOTS:], consts[:, AT_ROW:AT_ROW + 1], None,
                                    ALU.mult).then_inc(slots_marked, 1)
            done(nc.vector.tensor_tensor(slot_past, count[:, 0:SLOTS].unsqueeze(2).to_broadcast([P, SLOTS, N_EXP]),
                                         lots_end.unsqueeze(1).to_broadcast([P, SLOTS, N_EXP]), ALU.is_ge), past_made, 1)
            done(nc.vector.tensor_reduce(slot_f[:, 0, :], slot_past, op=ALU.add, axis=AX.X), past_made, 2)
            done(nc.vector.tensor_scalar(slot_f[:, 0, :], slot_f[:, 0, :], float(N_EXP - 1), None, ALU.min), past_made, 3)
            half = SLOTS // 2
            words, word_sum = slot_f[:, 1, 0:half], slot_f[:, 1, half:]
            done(nc.vector.scalar_tensor_tensor(words, slot_f[:, 0, 1::2], float(N_EXP), slot_f[:, 0, 0::2], ALU.mult, ALU.add),
                 past_made, 4)
            done(nc.vector.tensor_copy(word_sum, words), past_made, 5)
            for back in (1, 2):
                done(nc.vector.scalar_tensor_tensor(word_sum[:, back:], words[:, 0:half - back], float(N_EXP ** (2 * back)),
                                                    word_sum[:, back:], ALU.mult, ALU.add), past_made, 5 + back)
            done(nc.vector.tensor_copy(slot_word, word_sum), past_made, 8)
            dve.wait_ge(gap_exp, 1)
            done(nc.vector.tensor_scalar(top_v[:, 0, :], top_v[:, 1, :], 1.0, None, ALU.add), gap_plus1, 1)
            done(nc.vector.reciprocal(top_v[:, 0, :], top_v[:, 0, :]), gate1_made, 1)
            done(nc.vector.tensor_tensor(top_v[:, 1, :], top_v[:, 1, :], top_v[:, 0, :], ALU.mult), gates_made, 1)
            nc.vector.tensor_scalar(top_v, top_v, y_scale2, None, ALU.mult).then_inc(gates_made, 1)
            dve.wait_ge(table_done, 1)
            n_slot = 0

            def slot_done(ins):
                nonlocal n_slot
                n_slot += 1
                done(ins, slot_step, n_slot)
            slot_done(nc.vector.tensor_copy(slot_f[:, 3, :], psum[:, 2, SLOTS:2 * SLOTS]))
            slot_done(nc.vector.scalar_tensor_tensor(slot_f[:, 1, :], psum[:, 2, 0:SLOTS], float(P), slot_f[:, 3, :],
                                                     ALU.mult, ALU.add))
            slot_done(nc.vector.tensor_scalar(slot_f[:, 2, :], slot_f[:, 1, :], 0.0, None, ALU.is_equal))
            slot_done(nc.vector.tensor_tensor(slot_f[:, 3, :], slot_f[:, 1, :], slot_f[:, 2, :], ALU.add))
            slot_done(nc.vector.tensor_scalar(slot_src, slot_f[:, 3, :], -1.0, None, ALU.add))
            slot_done(nc.vector.tensor_scalar(slot_src, slot_src, T - 1, None, ALU.bitwise_and))
            slot_done(nc.vector.tensor_tensor(slot_f[:, 2, :], slot_f[:, 2, :], consts[:, AT_SPILL:AT_SPILL + SLOTS], ALU.mult))
            slot_done(nc.vector.tensor_tensor(slot_f[:, 1, :], slot_f[:, 1, :], slot_f[:, 2, :], ALU.add))
            nc.vector.tensor_scalar(slot_dst, slot_f[:, 1, :], -1.0, None, ALU.add).then_inc(routed, 1)

            def lot(s, u, i):
                dve.wait_ge(rows_high, s + 1)
                nc.vector.scalar_tensor_tensor(rows_lo[:, u, :], psum[:, u, 0:E], 2.0 ** X_BITS, rows_hi[:, u, :], ALU.mult,
                                               ALU.subtract).then_inc(rows_low, 1)
                if past(s, 3):
                    result_out(s - 3, 1 - u, i - 2 + u)
                if past(s, 1):
                    split_hidden(s - 1, 1 - u)

            def split_hidden(s, u):
                dve.wait_ge(gelu_done, s + 1)
                if past(s, 2):
                    dve.wait_ge(down_done, s - 1)
                done(nc.vector.tensor_scalar(hid_hi[:, u, :], hid[:, u, :], hid_scale, None, ALU.mult), hid_high, s + 1)
                nc.vector.scalar_tensor_tensor(hid_lo[:, u, :], hid[:, u, :], hid_scale, hid_hi[:, u, :], ALU.mult,
                                               ALU.subtract).then_inc(hid_low, 1)

            def result_out(s, u, i):
                dve.wait_ge(down_done, s + 1)
                if past(s, 2):
                    dve.wait_ge(ys_stored[u], 16 * i)
                dve.wait_ge(y_beside, s + 1)
                nc.vector.scalar_tensor_tensor(y_rows[:, u, :], psum[:, 6 + u, 0:E], y_scale1, y_side[:, u, :], ALU.mult,
                                               ALU.add).then_inc(y_copied, 1)
            dve.wait_ge(routed, 1)
            steps(dve, SLOTS, lot, 6)
            result_out(SLOTS - 3, 1, SLOTS // 2 - 2)
            split_hidden(SLOTS - 1, 1)
            result_out(SLOTS - 2, 0, SLOTS // 2 - 1)
            result_out(SLOTS - 1, 1, SLOTS // 2 - 1)

            dve.wait_ge(gates_made, 2)

            def finish(g, u, i):
                dve.wait_ge(y_loaded[u], 32 * i + 32)
                if past(g, 2):
                    dve.wait_ge(out_ready, QT * (g - 1))
                for t in range(QT):
                    nc.vector.scalar_tensor_tensor(sum3[:, u, t, :], y_pick[0][:, u, t, :], top_v[:, 0, bass.ds(QT * g + t, 1)],
                                                   x2[:, bass.ds(QT * g + t, 1), :].rearrange("p a e -> p (a e)"),
                                                   ALU.mult, ALU.add).then_inc(mix1_done, 1)
                for t in range(QT):
                    dve.wait_ge(mix1_done, QT * g + t + 1)
                    nc.vector.scalar_tensor_tensor(sum3[:, u, t, :], y_pick[1][:, u, t, :], top_v[:, 1, bass.ds(QT * g + t, 1)],
                                                   sum3[:, u, t, :], ALU.mult, ALU.add).then_inc(mix2_done, 1)
                if past(g, 1):
                    shift3(g - 1, 1 - u)
                for t in range(QT):
                    dve.wait_ge(mix2_done, QT * g + t + 1).then_inc(dve_waited, 1)
                    nc.vector.bn_stats(stats3[:, u, t, :], sum3[:, u, t, :]).then_inc(stats3_done, 1)
                dve.wait_ge(stats3_done, QT * (g + 1))
                moments(stats3[:, u], mean3[:, u, :], rstd3[:, u, :], GROUPS + B + g)

            def shift3(g, u):
                dve.wait_ge(rstd_ready, GROUPS + B + g + 1)
                nc.vector.scalar_tensor_tensor(mean3[:, u, :], mean3[:, u, :], -1.0, rstd3[:, u, :], ALU.mult,
                                               ALU.mult).then_inc(shift3_made, 1)
            steps(dve, TILES // QT, finish)
            shift3(TILES // QT - 1, 1)


def kernel(x, ctx_1024, L0_attn_Wq, L0_attn_Wkv, L0_attn_q_g, L0_attn_q_b, L0_attn_k_g, L0_attn_k_b, L0_attn_Wwin,
           L0_attn_bwin, L0_attn_Wout, L0_ffn_router_w, L0_ffn_expert_w1, L0_ffn_expert_w2):
    import numpy as np
    import concourse.bacc as bacc
    from concourse.bass_utils import run_bass_kernel_spmd

    laid = np.ascontiguousarray
    tokens = np.asarray(x).reshape(T, E)
    ctx = np.asarray(ctx_1024)
    arrays = {
        "x": laid(tokens),
        "x_steps": laid(tokens.reshape(P, CHUNK, E).transpose(1, 2, 0)),
        "ctx": laid(ctx),
        "ctx_t": laid(ctx.transpose(0, 2, 1)),
        "Wq": laid(L0_attn_Wq), "Wkv": laid(L0_attn_Wkv),
        "q_g": laid(L0_attn_q_g), "q_b": laid(L0_attn_q_b), "k_g": laid(L0_attn_k_g), "k_b": laid(L0_attn_k_b),
        "Wwin": laid(L0_attn_Wwin), "bwin": laid(L0_attn_bwin), "Wout": laid(L0_attn_Wout),
        "router_t": laid(np.asarray(L0_ffn_router_w).T),
        "w1_t": laid(np.asarray(L0_ffn_expert_w1).transpose(0, 2, 1)),
        "w2_t": laid(np.asarray(L0_ffn_expert_w2).transpose(0, 2, 1)),
        "shape_consts": host_consts(),
    }
    nc = bacc.Bacc("TRN2", target_bir_lowering=False, num_devices=1)
    aps = {n: nc.dram_tensor(n, a.shape, mybir.dt.from_np(a.dtype), kind="ExternalInput").ap() for n, a in arrays.items()}
    out = nc.dram_tensor("out", (T, E), F32, kind="ExternalOutput").ap()
    decoder_layer(nc, out=out, **aps)
    got = run_bass_kernel_spmd(nc, [arrays], core_ids=[0])
    return got.results[0]["out"].reshape(B, L, E)
```

```python
from contextlib import ExitStack

import concourse.bass as bass
from concourse import mybir

F32 = mybir.dt.float32
I32 = mybir.dt.int32
U32 = mybir.dt.uint32
BF16 = mybir.dt.bfloat16
F16 = mybir.dt.float16
ALU = mybir.AluOpType
ACT = mybir.ActivationFunctionType
AX = mybir.AxisListType

P = 128
B, L, E = 8, 512, 256
T = B * L
C = E // P
H, D = 16, 16
K = 17
R = K // 2
CHUNK = T // P
ROWS = CHUNK + 2 * R
GROUPS = 4
GROUP = CHUNK // GROUPS
PER = L // CHUNK
QKVW = 3 * E + 2 * H
EPS = 1e-5
SCALE = D ** -0.5
PENALTY = 1e4
W0 = (K + 1) // 2
WEIGHT_LOADS = 16 * (4 * C + 5 + 2)
QT = L // P
TILES = T // P
MASKED = 1e10
LOW = 10856
N_EXP, TOP, F = 8, 2, 1024
FB = F // P
EW = C * F
PIECES = CHUNK
PIECE = N_EXP * EW // PIECES
F32_BIAS, F32_MANT = 127, 23
TOP_BITS = 15
X_BITS = 11
SLOTS = TOP * T // P + N_EXP
EXP_BITS = N_EXP.bit_length() - 1
PART = TOP * T // P // 4
AT_IDENT = 0
AT_REACH = AT_IDENT + P
AT_MASK = AT_REACH + K
AT_BELOW = AT_MASK + P
AT_COUNT = AT_BELOW + P
AT_TILE = AT_COUNT + P
AT_ROW = AT_TILE + TOP * TILES
AT_SPILL = AT_ROW + 1
N_CONST = AT_SPILL + SLOTS


def host_consts():
    import numpy as np
    i, j = np.arange(P)[:, None], np.arange(P)[None, :]
    wide = lambda a: np.broadcast_to(a, (P, len(a)))
    parts = [
        i == j,
        wide(np.abs(np.arange(K) - R)),
        np.where(j > i, -MASKED, 0.0),
        i < j,
        wide(np.arange(P)),
        wide(np.arange(TOP * TILES)),
        i + 1.0,
        TOP * T + P * np.arange(SLOTS)[None, :] + i + 1.0,
    ]
    return np.ascontiguousarray(np.concatenate(parts, axis=1).astype(np.float32))


def steps(eng, n, body, peeled=2, start=0, unrolled=2):
    first = max(start, peeled)
    for t in range(start, first):
        body(t, t % 2, t // 2)
    if first < n:
        with eng.Fori(first // unrolled, n // unrolled) as i:
            for v in range(unrolled):
                body(unrolled * i + v, v % 2, unrolled // 2 * i + v // 2)


def past(t, k):
    return not isinstance(t, int) or t >= k


def group(ap, g):
    return ap[:, g * GROUP:(g + 1) * GROUP]


def row(ap, t):
    return ap[:, bass.ds(t, 1)]


def decoder_layer(nc, x, x_steps, ctx, ctx_t, Wq, Wkv, q_g, q_b, k_g, k_b, Wwin, bwin, Wout,
                  router_t, w1_t, w2_t, shape_consts, out):
    stack = ExitStack()
    with stack:
        def sb(name, shape, dt=F32):
            return stack.enter_context(nc.sbuf_tensor(name, shape, dt))

        def sem(name):
            return stack.enter_context(nc.semaphore(name))

        x1_dram = nc.dram_tensor("x1_dram", [T, E], F32, kind="Internal").ap()
        x_chunk = x.rearrange("(p s) e -> p s e", s=CHUNK)
        x1_seq = x1_dram.rearrange("(b l) e -> b l e", l=L)
        x1_chunk = x1_dram.rearrange("(p s) e -> p s e", s=CHUNK)

        arena = sb("arena", [P, LOW + (CHUNK + 2 * ROWS) * E])
        low = arena[:, 0:LOW]
        big = arena[:, LOW:]
        mid = sb("mid", [P, 2 * K * E])
        low_used = {}

        def carve(region, start, *shape):
            n = 1
            for m in shape:
                n *= m
            names = " ".join("abcd"[:len(shape)])
            ap = region[:, start:start + n]
            if len(shape) > 1:
                ap = ap.rearrange(f"p ({names}) -> p {names}", **dict(zip("abcd", shape)))
            return ap

        def next_low(phase, *shape):
            start = low_used.get(phase, 0)
            n = 1
            for m in shape:
                n *= m
            low_used[phase] = start + n
            assert start + n <= LOW, (phase, start + n)
            return carve(low, start, *shape)

        consts = sb("consts", [P, N_CONST])
        ident = consts[:, AT_IDENT:AT_IDENT + P]
        reach = consts[:, AT_REACH:AT_REACH + K]
        ones_pp = sb("ones_pp", [P, P])
        ones_row = ones_pp[0:1, :]
        b_win = sb("b_win", [1, 2 * H])
        minus_half = sb("minus_half", [P, 2 * H])

        router_w = sb("router_w", [P, C, N_EXP])

        x2_dram = nc.dram_tensor("x2_dram", [T, E], F32, kind="Internal").ap()
        x2_seq = x2_dram.rearrange("(b l) e -> b l e", l=L)
        x2 = carve(mid, 0, TILES, E)
        ctx_sb = next_low("cross", 2, QT, E)
        ctx_ts = next_low("cross", 2, C, L)
        x1_n = next_low("cross", 2, QT, E)
        x1_t = next_low("cross", C, L)
        probs = next_low("cross", 2, L)
        x2_t = carve(low, low_used["cross"], C, L)
        probs_t = next_low("cross", 2, QT, P)
        top_peak = next_low("cross", 2, QT)
        bias2 = next_low("cross", 2, QT)
        row_sum = next_low("cross", 2, QT)
        inv_row = next_low("cross", 2, QT)
        stats2 = next_low("cross", 2, QT, 6)
        mean2 = next_low("cross", 2, QT)
        rstd2 = next_low("cross", 2, QT)
        logits = next_low("cross", 2, QT, N_EXP)
        top8 = next_low("cross", 2, QT, 8)
        where8 = next_low("cross", 2, QT, 8)
        assert low_used["cross"] <= LOW - EW // 2

        keep_at = TILES * E
        slot_src = carve(mid, keep_at, SLOTS).bitcast(I32)
        slot_dst = carve(mid, keep_at + SLOTS, SLOTS).bitcast(I32)
        slot_word = carve(mid, keep_at + 2 * SLOTS, SLOTS // 2).bitcast(I32)
        top_v = carve(mid, keep_at + 3 * SLOTS, TOP, TILES)
        top_i = carve(mid, keep_at + 3 * SLOTS + TOP * TILES, TOP, TILES)
        chosen = next_low("route", TOP, TILES, N_EXP)
        picked = next_low("route", TILES, N_EXP)
        upto = [next_low("route", TILES, N_EXP) for _ in range(2)]
        place = next_low("route", TILES, N_EXP)
        placed = next_low("route", TOP, TILES, N_EXP)
        is_row = carve(low, 0, TOP * TILES, P // 2).bitcast(BF16)
        low_used["route"] = TOP * TILES * P // 2
        lots = next_low("route", 2, N_EXP)
        lots_n = next_low("route", N_EXP)
        lots_i = next_low("route", N_EXP).bitcast(I32)
        rest_at = keep_at + 3 * SLOTS + 2 * TOP * TILES
        spot = carve(mid, rest_at, TOP, TILES)
        spot_i = next_low("route", 2, TOP, TILES).bitcast(I32)
        spot_row = carve(mid, rest_at + TOP * TILES, TOP * TILES)
        spot_slot = next_low("route", TOP * TILES)
        slot_past = next_low("route", SLOTS, N_EXP)
        slot_f = next_low("route", 4, SLOTS)
        is_slot = next_low("route", TOP * TILES, SLOTS).bitcast(BF16)
        assert low_used["route"] <= LOW - EW // 2

        ys_dram = nc.dram_tensor("ys_dram", [(TOP * TILES + SLOTS) * P, E], F32, kind="Internal").ap()
        ys_group = ys_dram[0:TOP * T, :].rearrange("(g l) e -> g l e", l=QT * P)
        out_group = out.rearrange("(g l) e -> g l e", l=QT * P)
        w_f32 = carve(big, 0, N_EXP, 2, EW)
        arena16 = arena[:, :].bitcast(F16)
        w_low = arena16[:, 2 * LOW:2 * LOW + 4 * N_EXP * EW].rearrange("p (e k x) -> p e k x", k=2, x=2 * EW)
        w_high = arena16[:, 2 * LOW - EW:2 * LOW - EW + 4 * N_EXP * EW].rearrange("p (e k x) -> p e k x", k=2, x=2 * EW)
        w_parts = arena16[:, 2 * LOW - EW:2 * LOW - EW + 4 * N_EXP * EW].rearrange("p (e k x) -> p e k x", k=4, x=EW)
        scale_at = rest_at + 2 * TOP * TILES
        scale_bits = carve(mid, scale_at, 8).bitcast(I32)
        w_scale = carve(mid, scale_at, 8)
        w1_scale, w2_scale, up_scale, hid_scale, y_scale1, y_scale2 = (w_scale[:, k:k + 1] for k in range(6))
        w_exp = carve(mid, scale_at + 8, 2).bitcast(I32)
        assert scale_at + 10 <= 2 * K * E
        src_col = next_low("experts", 2, 1).bitcast(I32)
        dst_col = next_low("experts", 2, 1).bitcast(I32)
        rows = next_low("experts", 2, E)
        rows_hi = next_low("experts", 2, E // 2).bitcast(F16)
        rows_lo = next_low("experts", 2, E // 2).bitcast(F16)
        hid = next_low("experts", 2, F)
        hid_hi = next_low("experts", 2, F // 2).bitcast(F16)
        hid_lo = next_low("experts", 2, F // 2).bitcast(F16)
        y_side = next_low("experts", 2, E)
        y_rows = next_low("experts", 2, E)

        y_pick = [next_low("end", 2, QT, E) for _ in range(TOP)]
        sum3 = next_low("end", 2, QT, E)
        out_rows = next_low("end", 2, QT, E)
        stats3 = next_low("end", 2, QT, 6)
        mean3 = next_low("end", 2, QT)
        rstd3 = next_low("end", 2, QT)

        q_all = carve(big, 0, CHUNK, E)
        k_all = carve(big, CHUNK * E, ROWS, E)
        v_all = carve(big, (CHUNK + ROWS) * E, ROWS, E)
        qk_prod = mid[:, 0:K * E]
        av_prod = [carve(mid, K * E, W0, E), carve(mid, (K + W0) * E, K - W0, E)]
        act_qk = carve(mid, 0, 2, 2 * E)
        cen_qk = carve(mid, 4 * E, 2, 2 * E)
        sq_qk = carve(mid, 8 * E, 2, 2 * E)
        head_var = carve(mid, 12 * E, CHUNK, 2 * H)
        head_rstd = carve(mid, 16 * E, CHUNK, 2 * H)
        newton = carve(mid, 20 * E, CHUNK, 2 * H)
        w_in = next_low("window", C, QKVW)
        x_step = next_low("window", 2, C, P)
        win = next_low("window", CHUNK, 2 * H)
        gains = next_low("window", 2, D)
        head_sum = next_low("window", 2, 2 * H)
        gate = carve(low, 0, CHUNK, R + 1, H)
        low_used["window"] = CHUNK * (R + 1) * H
        w_out = next_low("window", C, E)
        biases = next_low("window", 2, D)
        sharp = next_low("window", CHUNK, H)
        edge = next_low("window", CHUNK, H)
        stats = next_low("window", CHUNK, 6)
        mean1 = next_low("window", CHUNK)
        rstd1 = next_low("window", CHUNK)
        score = next_low("window", 2, K * H)
        prob = next_low("window", 2, K * H)
        peak = next_low("window", 2, H)
        total = next_low("window", 2, H)
        inv_total = next_low("window", 2, H)
        w_piece = next_low("window", 2, PIECE)
        w_squares = next_low("window", 2, PIECES)
        w_sum = next_low("window", 2)
        mixed_t = next_low("window", 2, C, P)
        tanh_y = next_low("window", 2, E)
        x_res = next_low("window", 2, E)
        y_sb = next_low("window", 2, E)
        bn6 = next_low("window", 2, 6)

        psum = stack.enter_context(nc.psum_tensor("psum", [P, 8, 512], F32))

        weights_loaded = sem("weights_loaded")
        fills_made = sem("fills_made")
        halo_zeroed = sem("halo_zeroed")
        x_step_loaded = [sem("x_step_loaded0"), sem("x_step_loaded1")]
        qkv_done = sem("qkv_done")
        silu_done = sem("silu_done")
        centred = sem("centred")
        squared = sem("squared")
        var_done = sem("var_done")
        halo_loaded = sem("halo_loaded")
        sig_done = sem("sig_done")
        gained = sem("gained")
        var_eps = sem("var_eps")
        root_done = sem("root_done")
        gate_done = sem("gate_done")
        gate_args = sem("gate_args")
        rstd_heads = sem("rstd_heads")
        q_scaled = sem("q_scaled")
        newton_step = sem("newton_step")
        k_scaled = sem("k_scaled")
        k_ready = sem("k_ready")
        q_ready = sem("q_ready")
        width_done = sem("width_done")
        gate_arg = sem("gate_arg")
        score_ready = sem("score_ready")
        exp_done = sem("exp_done")
        inv_ready = sem("inv_ready")
        prob_ready = sem("prob_ready")
        av_ready = sem("av_ready")
        av_used = sem("av_used")
        mixed_done = sem("mixed_done")
        mixed_copied = sem("mixed_copied")
        y_done = sem("y_done")
        tanh_done = sem("tanh_done")
        x1_last = sem("x1_last")
        norm1_shift = sem("norm1_shift")
        y_parts = sem("y_parts")
        x_res_loaded = [sem("x_res_loaded0"), sem("x_res_loaded1")]
        res_done = sem("res_done")
        res_kept = sem("res_kept")
        mean_diff = sem("mean_diff")
        mean_diff_sq = sem("mean_diff_sq")
        mean_added = sem("mean_added")
        var_between = sem("var_between")
        var_even = sem("var_even")
        var_made = sem("var_made")
        rstd_ready = sem("rstd_ready")
        x1_ready = sem("x1_ready")
        x1_stored = sem("x1_stored")
        prob_made = sem("prob_made")
        head_mean_summed = sem("head_mean_summed")
        silu_y_made = sem("silu_y_made")
        res_summed = sem("res_summed")
        qk_multiplied = sem("qk_multiplied")
        qk_summed = sem("qk_summed")
        penalised = sem("penalised")
        peak_found = sem("peak_found")
        total_found = sem("total_found")

        pool_waited = sem("pool_waited")
        dve_waited = sem("dve_waited")
        normed2 = sem("normed2")
        stats2_done = sem("stats2_done")
        stats3_done = sem("stats3_done")
        slot_hits = sem("slot_hits")
        slot_tiles = sem("slot_tiles")
        x1t_done = sem("x1t_done")
        tok_copied = sem("tok_copied")
        s_done = sem("s_done")
        peak_ready = sem("peak_ready")
        masked = sem("masked")
        peak_found2 = sem("peak_found2")
        exp2_done = sem("exp2_done")
        pt_done = sem("pt_done")
        pt_copied = sem("pt_copied")
        av_done = sem("av_done")
        inv2_made = sem("inv2_made")
        sum2_done = sem("sum2_done")
        x2_ready = sem("x2_ready")
        x2t_done = sem("x2t_done")
        x2t_copied = sem("x2t_copied")
        router_done = sem("router_done")
        logits_copied = sem("logits_copied")
        top_found = sem("top_found")
        where_found = sem("where_found")
        top_kept = sem("top_kept")
        w_loaded = sem("w_loaded")
        w_piece_loaded = sem("w_piece_loaded")
        w_squared = sem("w_squared")
        w_summed = sem("w_summed")
        w_total = sem("w_total")
        w_exps = sem("w_exps")
        w_scaled = sem("w_scaled")
        w_multiplied = sem("w_multiplied")
        w_high_made = sem("w_high_made")
        w_low_made = sem("w_low_made")
        gap_made = sem("gap_made")
        gap_exp = sem("gap_exp")
        gap_plus1 = sem("gap_plus1")
        gate1_made = sem("gate1_made")
        gates_made = sem("gates_made")
        chosen_made = sem("chosen_made")
        picked_made = sem("picked_made")
        counted = sem("counted")
        tile_sums = sem("tile_sums")
        scan_step = sem("scan_step")
        place_made = sem("place_made")
        lots_step = sem("lots_step")
        placed_made = sem("placed_made")
        spot_made = sem("spot_made")
        spot_int = sem("spot_int")
        spot_parts = sem("spot_parts")
        spot_back = sem("spot_back")
        rows_marked = sem("rows_marked")
        slots_marked = sem("slots_marked")
        table_done = sem("table_done")
        slot_step = sem("slot_step")
        routed = sem("routed")
        past_made = sem("past_made")
        src_copied = sem("src_copied")
        dst_copied = sem("dst_copied")
        rows_t_done = sem("rows_t_done")
        rows_high = sem("rows_high")
        rows_low = sem("rows_low")
        up_done = sem("up_done")
        gelu_done = sem("gelu_done")
        hid_high = sem("hid_high")
        hid_low = sem("hid_low")
        down_done = sem("down_done")
        y_copied = sem("y_copied")
        y_beside = sem("y_beside")
        mix1_done = sem("mix1_done")
        mix2_done = sem("mix2_done")
        out_ready = sem("out_ready")
        shift3_made = sem("shift3_made")
        x1_loaded = [sem("x1_loaded0"), sem("x1_loaded1")]
        ctx_loaded = [sem("ctx_loaded0"), sem("ctx_loaded1")]
        out_stored = [sem("out_stored0"), sem("out_stored1")]
        rows_loaded = [sem("rows_loaded0"), sem("rows_loaded1")]
        x2_stored = [sem("x2_stored0"), sem("x2_stored1")]
        y_loaded = [sem("y_loaded0"), sem("y_loaded1")]
        ys_stored = [sem("ys_stored0"), sem("ys_stored1")]

        block = stack.enter_context(nc.Block())

        @block.sync
        def _(sp):
            sp.dma_start(consts[:, :], shape_consts).then_inc(weights_loaded, 16)
            for c in range(C):
                for w, a in ((Wq, 0), (Wkv, E), (Wwin, 3 * E)):
                    sp.dma_start(w_in[:, c, a:a + w.shape[1]], w[c * P:(c + 1) * P, :]).then_inc(weights_loaded, 16)
                sp.dma_start(w_out[:, c, :], Wout[c * P:(c + 1) * P, :]).then_inc(weights_loaded, 16)
            sp.dma_start(router_w[:, :, :], router_t.rearrange("(c p) n -> p c n", p=P)).then_inc(weights_loaded, 16)
            for m, (g, b) in enumerate(((q_g, q_b), (k_g, k_b))):
                sp.dma_start(gains[:, m, :], g.partition_broadcast(P)).then_inc(weights_loaded, 16)
                sp.dma_start(biases[:, m, :], b.partition_broadcast(P)).then_inc(weights_loaded, 16)
            sp.dma_start(b_win[:, :], bwin.rearrange("(a n) -> a n", a=1)).then_inc(weights_loaded, 16)

            def load_x_step(t, u, i):
                if past(t, 2):
                    sp.wait_ge(qkv_done, t - 1)
                src = x_steps[bass.ds(t, 1)].rearrange("a (c q) p -> q (a c) p", q=P)
                sp.dma_start(x_step[:, u], src).then_inc(x_step_loaded[u], 16)
            steps(sp, CHUNK, load_x_step)

            sp.wait_ge(halo_zeroed, 4)
            sp.wait_ge(silu_done, CHUNK)
            for kv, left in ((v_all, False), (v_all, True), (k_all, False), (k_all, True)):
                if kv is k_all:
                    sp.wait_ge(k_ready, GROUPS if left else R // GROUP)
                for b in range(B):
                    a, z = b * PER, (b + 1) * PER
                    if left:
                        sp.dma_start(kv[a + 1:z, 0:R, :], kv[a:z - 1, CHUNK:CHUNK + R, :]).then_inc(halo_loaded, 16)
                    else:
                        sp.dma_start(kv[a:z - 1, R + CHUNK:ROWS, :], kv[a + 1:z, R:2 * R, :]).then_inc(halo_loaded, 16)

            def load_x_res(t, u, i):
                if past(t, 1):
                    sp.wait_ge(w_squared, 2 * t)
                for k, w in enumerate((w1_t, w2_t)):
                    parts = w.rearrange("e r c -> (e r c)").rearrange("(n p x) -> n p x", p=P, x=PIECE)
                    sp.dma_start(w_piece[:, k, :], parts[bass.ds(t, 1)].rearrange("a p x -> p (a x)")).then_inc(w_piece_loaded, 16)
                if past(t, 2):
                    sp.wait_ge(res_kept, t - 1)
                sp.dma_start(x_res[:, u, :], x_chunk[:, bass.ds(t, 1), :].rearrange("p a e -> p (a e)")).then_inc(x_res_loaded[u], 16)
            steps(sp, CHUNK, load_x_res)

            for g in range(GROUPS):
                if g < GROUPS - 1:
                    sp.wait_ge(x1_ready, GROUP * (g + 1))
                else:
                    sp.wait_ge(x1_last, GROUP)
                part = slice(g * GROUP, (g + 1) * GROUP)
                sp.dma_start(x1_chunk[:, part, :], q_all[:, part, :]).then_inc(x1_stored, 16)
            def load_sequence(b, u, i):
                if past(b, 2):
                    sp.wait_ge(sum2_done, QT * (b - 1))
                rows_of = "a (t p) e -> p (a t) e"
                if past(b, 2):
                    sp.wait_ge(x2t_done, b - 1)
                    sp.wait_ge(x2_ready, QT * (b - 1))
                else:
                    sp.wait_ge(x1_stored, 16 * GROUPS)
                sp.dma_start(x1_n[:, u], x1_seq[bass.ds(b, 1)].rearrange(rows_of, p=P)).then_inc(x1_loaded[u], 16)
                sp.dma_start(ctx_ts[:, u], ctx_t[bass.ds(b, 1)].rearrange("a (c p) l -> p (a c) l", p=P)).then_inc(ctx_loaded[u], 16)
                sp.dma_start(ctx_sb[:, u], ctx[bass.ds(b, 1)].rearrange(rows_of, p=P)).then_inc(ctx_loaded[u], 16)
                for k, (w, x) in enumerate(((w1_t, F), (w2_t, E))):
                    sp.dma_start(w_f32[:, bass.ds(b, 1), k, :].rearrange("p a (r x) -> p (a r) x", x=x),
                                 w[bass.ds(b, 1)].rearrange("a (r p) x -> p (a r) x", p=P)).then_inc(w_loaded, 16)
                if past(b, 1):
                    store_x2(b - 1, 1 - u)

            def store_x2(b, u):
                sp.wait_ge(x2_ready, QT * (b + 1))
                sp.dma_start(x2_seq[bass.ds(b, 1)].rearrange("a (t p) e -> p (a t) e", p=P),
                             x2[:, bass.ds(QT * b, QT), :]).then_inc(x2_stored[u], 16)
            steps(sp, B, load_sequence)
            store_x2(B - 1, 1)

            def load_picked(g, u, i):
                if past(g, 2):
                    sp.wait_ge(mix2_done, QT * (g - 1))
                for k in range(TOP):
                    sp.dma_start(y_pick[k][:, u], ys_group[bass.ds(k * (TILES // QT) + g, 1)].rearrange(
                        "a (t p) e -> p (a t) e", p=P)).then_inc(y_loaded[u], 16)
            for u in (0, 1):
                sp.wait_ge(ys_stored[u], 16 * (SLOTS // 2))
            steps(sp, TILES // QT, load_picked)
            for u in (0, 1):
                sp.wait_ge(out_stored[u], 16 * (TILES // QT // 2))

        @block.tensor
        def _(pe):
            pe.wait_ge(weights_loaded, WEIGHT_LOADS)
            pe.wait_ge(fills_made, 2)

            def project(t, u, i):
                pe.wait_ge(x_step_loaded[u], 16 * i + 16)
                if past(t, 2):
                    pe.wait_ge(silu_done, t - 1)
                for c in range(C):
                    nc.tensor.matmul(psum[:, u, :], x_step[:, u, c, :], w_in[:, c, 0:512],
                                     start=(c == 0), stop=(c == C - 1))
                for c in range(C):
                    nc.tensor.matmul(psum[:, 2 + u, 0:QKVW - 512], x_step[:, u, c, :], w_in[:, c, 512:QKVW],
                                     start=(c == 0), stop=False, skip_group_check=True)
                nc.tensor.matmul(psum[:, 2 + u, E:E + 2 * H], ones_row, b_win[:, :],
                                 start=False, stop=True, skip_group_check=True).then_inc(qkv_done, 1)
            steps(pe, CHUNK, project)
            pe.wait_ge(silu_done, CHUNK)

            def mix(t, u, i):
                if past(t, 2):
                    pe.wait_ge(mixed_copied, t - 1)
                for half, (a, n) in enumerate(((0, W0), (W0, K - W0))):
                    pe.wait_ge(av_ready, 2 * t + half + 1)
                    for w in range(n):
                        for c in range(C):
                            last = nc.tensor.matmul(psum[:, 2 * u + c, 0:P], av_prod[half][:, w, c * P:(c + 1) * P],
                                                    ident, start=(a + w == 0), stop=(a + w == K - 1))
                    last.then_inc(av_used, 1)
                pe.wait_ge(mixed_copied, t + 1)
                if past(t, 2):
                    pe.wait_ge(y_parts, t - 1)
                for c in range(C):
                    last = nc.tensor.matmul(psum[:, 4 + u, 0:E], mixed_t[:, u, c, :], w_out[:, c, :],
                                            start=(c == 0), stop=(c == C - 1))
                last.then_inc(y_done, 1)
            steps(pe, CHUNK, mix, 4)
            pe.wait_ge(y_parts, CHUNK)
            pe.wait_ge(w_summed, 1)
            nc.tensor.matmul(psum[:, 0, 0:2], ones_pp[:, :], w_sum[:, :], start=True, stop=True).then_inc(w_total, 1)

            def transpose_x1(u, c):
                for t in range(QT):
                    last = nc.tensor.transpose(psum[:, 4 + c, t * P:(t + 1) * P], x1_n[:, u, t, c * P:(c + 1) * P], ident)
                last.then_inc(x1t_done, 1)

            def attend(b, u, i, more=True):
                pe.wait_ge(ctx_loaded[u], 32 * i + 32)
                pe.wait_ge(tok_copied, 2 * b + 2)
                for t in range(QT):
                    if past(b, 1):
                        pe.wait_ge(exp2_done, QT * b - QT + t + 1)
                    for c in range(C):
                        last = nc.tensor.matmul(psum[:, t, 0:(t + 1) * P], x1_t[:, c, t * P:(t + 1) * P],
                                                ctx_ts[:, u, c, 0:(t + 1) * P], start=(c == 0), stop=(c == C - 1))
                    last.then_inc(s_done, 1)
                    if t == QT - 2 and past(b, 1):
                        transpose_x2(b - 1, 1 - u)
                if past(b, 1):
                    route(b - 1)
                for t in range(QT + 1):
                    if t < QT:
                        pe.wait_ge(exp2_done, QT * b + t + 1)
                        if t >= 2:
                            pe.wait_ge(pt_copied, QT * b + t - 1)
                        elif past(b, 1):
                            pe.wait_ge(pt_copied, QT * b + t - 1)
                        for k in range(t + 1):
                            last = nc.tensor.transpose(psum[:, 4 + t % 2, k * P:(k + 1) * P],
                                                       probs[:, t % 2, k * P:(k + 1) * P], ident)
                        last.then_inc(pt_done, 1)
                    if t:
                        q = t - 1
                        pe.wait_ge(pt_copied, QT * b + q + 1)
                        if q >= 2:
                            pe.wait_ge(sum2_done, QT * b + q - 1)
                        elif past(b, 1):
                            pe.wait_ge(logits_copied, b)
                        for k in range(q + 1):
                            last = nc.tensor.matmul(psum[:, 6 + q % 2, 0:E], probs_t[:, q % 2, k, :], ctx_sb[:, u, k, :],
                                                    start=(k == 0), stop=(k == q))
                        last.then_inc(av_done, 1)
                        if more and q == QT - 2:
                            pe.wait_ge(x1_loaded[1 - u], 16 * (i + u) + 16)
                            transpose_x1(1 - u, 0)
                        if more and q == QT - 1:
                            transpose_x1(1 - u, 1)

            def transpose_x2(b, b_u):
                pe.wait_ge(normed2, QT * (b + 1))
                for c in range(C):
                    for t in range(QT):
                        last = nc.tensor.transpose(psum[:, 6 + c, t * P:(t + 1) * P],
                                                   x1_n[:, b_u, t, c * P:(c + 1) * P], ident)
                last.then_inc(x2t_done, 1)

            def route(b):
                pe.wait_ge(x2t_copied, b + 1)
                for t in range(QT):
                    for c in range(C):
                        last = nc.tensor.matmul(psum[:, 7, t * N_EXP:(t + 1) * N_EXP], x2_t[:, c, t * P:(t + 1) * P],
                                                router_w[:, c, :], start=(c == 0), stop=(c == C - 1))
                last.then_inc(router_done, 1)
            pe.wait_ge(w_exps, 1)
            pe.wait_ge(x1_loaded[0], 16)
            for c in range(C):
                transpose_x1(0, c)
            steps(pe, B - 2, attend)
            attend(B - 2, 0, B // 2 - 1)
            attend(B - 1, 1, B // 2 - 1, more=False)
            pe.wait_ge(sum2_done, T // P)
            transpose_x2(B - 1, 1)
            route(B - 1)

            pe.wait_ge(picked_made, 1)
            nc.tensor.matmul(psum[:, 0, 0:TILES * N_EXP], consts[:, AT_BELOW:AT_BELOW + P],
                             picked.rearrange("p t n -> p (t n)"), start=True, stop=True)
            nc.tensor.matmul(psum[:, 1, 0:TILES * N_EXP], ones_pp[:, :],
                             picked.rearrange("p t n -> p (t n)"), start=True, stop=True).then_inc(counted, 1)
            for j in range(TOP * TILES):
                if j % PART == 0:
                    pe.wait_ge(rows_marked, j // PART + 1)
                    pe.wait_ge(slots_marked, j // PART + 1)
                last = nc.tensor.matmul(psum[:, 2, 0:2 * SLOTS], is_row[:, j, :], is_slot[:, j, :],
                                        start=(j == 0), stop=(j == TOP * TILES - 1))
            last.then_inc(table_done, 1)

            pe.wait_ge(routed, 1)
            pe.wait_ge(w_low_made, 2 * N_EXP)

            def block_of(w, e, k, at, n):
                return w[:, bass.ds(e, 1), k, at:at + n].rearrange("p a n -> p (a n)")

            def transpose_rows(s, u, i):
                pe.wait_ge(rows_loaded[u], 16 * i + 16)
                for c in range(C):
                    last = nc.tensor.transpose(psum[:, u, c * P:(c + 1) * P], rows[:, u, c * P:(c + 1) * P], ident)
                last.then_inc(rows_t_done, 1)

            def up(u, e, j):
                dst = psum[:, 2 + 2 * u + j // 4, j % 4 * P:(j % 4 + 1) * P]
                for k, (w, x) in enumerate(((w_high, rows_hi), (w_high, rows_lo), (w_low, rows_hi))):
                    for c in range(C):
                        last = nc.tensor.matmul(dst, block_of(w, e, 0, c * F + j * P, P), x[:, u, c * P:(c + 1) * P],
                                                start=(k == 0 and c == 0), stop=(k == 2 and c == C - 1))
                return last

            def down(u, e, j):
                both = w_parts[:, bass.ds(e, 1), 2:4, j * E:(j + 1) * E].rearrange("p a k n -> p (a k) n")
                high = w_parts[:, bass.ds(e, 1), 2:3, j * E:(j + 1) * E].rearrange("p a k n -> p (a k) n")
                nc.tensor.matmul(psum[:, 6 + u, :], hid_hi[:, u, j * P:(j + 1) * P], both, start=(j == 0), stop=False,
                                 skip_group_check=True)
                return nc.tensor.matmul(psum[:, 6 + u, E:2 * E], hid_lo[:, u, j * P:(j + 1) * P], high, start=False,
                                        stop=(j == FB - 1), skip_group_check=True)

            def products(s, u, e_up, e_down):
                if e_up is not None:
                    pe.wait_ge(rows_low, s)
                if e_down is not None:
                    pe.wait_ge(hid_low, s - 2)
                    if past(s, 5):
                        pe.wait_ge(y_copied, s - 4)
                for j in range(FB):
                    if e_up is not None:
                        last_up = up(1 - u, e_up, j)
                    if e_down is not None:
                        last_down = down(1 - u, e_down, j)
                if e_up is not None:
                    last_up.then_inc(up_done, 1)
                if e_down is not None:
                    last_down.then_inc(down_done, 1)

            def expert(word, at):
                pair, second = divmod(at, 2)
                return (word >> (EXP_BITS * (second - 2 * pair))) & (N_EXP - 1)

            def load_word(i):
                return pe.value_load(slot_word[0:1, bass.ds(i, 1)], min_val=0, max_val=N_EXP ** 8 - 1)

            def four_lots(i):
                word = load_word(2 * i + 1)
                for v in range(4):
                    s, u = 4 * i + v, v % 2
                    transpose_rows(s, u, 2 * i + v // 2)
                    products(s, u, expert(word, v - 3) if past(s, 1) else None, expert(word, v - 5) if past(s, 3) else None)
            four_lots(0)
            four_lots(1)
            with pe.Fori(2, SLOTS // 4) as i:
                four_lots(i)
            word = load_word(SLOTS // 2 - 1)
            products(SLOTS, 0, expert(word, 1), expert(word, -1))
            products(SLOTS + 1, 1, None, expert(word, 0))
            products(SLOTS + 2, 0, None, expert(word, 1))

        @block.scalar
        def _(act):
            def square(t, u):
                act.wait_ge(centred, t + 1)
                if past(t, 2):
                    act.wait_ge(var_done, t - 1)
                nc.scalar.activation(sq_qk[:, u, :], cen_qk[:, u, :], ACT.Square).then_inc(squared, 1)

            def silu(t, u, i):
                act.wait_ge(qkv_done, t + 1)
                if past(t, 2):
                    act.wait_ge(centred, t - 1)
                nc.scalar.activation(act_qk[:, u, :], psum[:, u, :], ACT.Silu)
                nc.scalar.activation(row(v_all, t + R), psum[:, 2 + u:3 + u, 0:E], ACT.Silu)
                nc.scalar.activation(row(win, t), psum[:, 2 + u:3 + u, E:E + 2 * H], ACT.Silu).then_inc(silu_done, 1)
                if past(t, 1):
                    square(t - 1, 1 - u)
            def head_roots(g):
                act.wait_ge(var_eps, g + 1)
                nc.scalar.activation(group(head_rstd, g), group(head_var, g), ACT.Sqrt).then_inc(root_done, 1)
            for g in range(GROUPS):
                steps(act, (g + 1) * GROUP, silu, 4, g * GROUP)
                if g:
                    head_roots(g - 1)
            square(CHUNK - 1, 1)
            head_roots(GROUPS - 1)
            act.wait_ge(silu_done, CHUNK)
            nc.scalar.activation(win[:, :, :], win[:, :, :], ACT.Sigmoid).then_inc(sig_done, 1)
            for half in range(2):
                act.wait_ge(gate_arg, half + 1)
                part = slice(half * CHUNK // 2, (half + 1) * CHUNK // 2)
                nc.scalar.activation(gate[:, part], gate[:, part], ACT.Sigmoid).then_inc(gate_done, 1)

            def mixed_out(t, u):
                act.wait_ge(av_used, 2 * t + 2)
                if past(t, 2):
                    act.wait_ge(y_done, t - 1)
                nc.scalar.activation(mixed_t[:, u], psum[:, 2 * u:2 * u + 2, 0:P], ACT.Copy).then_inc(mixed_copied, 1)
                act.wait_ge(y_done, t + 1)
                if past(t, 2):
                    act.wait_ge(res_summed, t - 1)
                nc.scalar.activation(tanh_y[:, u, :], psum[:, 4 + u, 0:E], ACT.Tanh, scale=0.5).then_inc(tanh_done, 1)
                nc.scalar.activation(y_sb[:, u, :], psum[:, 4 + u, 0:E], ACT.Copy)
                act.wait_ge(tanh_done, t + 1)
                nc.scalar.activation(tanh_y[:, u, :], tanh_y[:, u, :], ACT.Copy, scale=0.5, bias=0.5).then_inc(y_parts, 1)

            def window(t, u, i):
                act.wait_ge(score_ready, t + 1)
                nc.scalar.activation(score[:, u, :], score[:, u, :], ACT.Exp, scale=SCALE).then_inc(exp_done, 1)
                if past(t, 2):
                    mixed_out(t - 2, u)
                if past(t, 3):
                    keep(t - 3, 1 - u)
                square_weights(t, u, i)

            def square_weights(t, u, i):
                act.wait_ge(w_piece_loaded, 32 * t + 32)
                for k in range(2):
                    nc.scalar.activation(w_piece[:, k, :], w_piece[:, k, :], ACT.Square,
                                         accum_out=w_squares[:, k, bass.ds(t, 1)]).then_inc(w_squared, 1)

            def keep(t, u):
                act.wait_ge(res_done, t + 1)
                nc.scalar.activation(row(q_all, t), x_res[:, u:u + 1, :], ACT.Copy)
                nc.scalar.activation(row(stats, t), bn6[:, u:u + 1, :], ACT.Copy).then_inc(res_kept, 1)

            def norm1(g):
                act.wait_ge(norm1_shift, g + 1)
                for t in range(g * GROUP, (g + 1) * GROUP):
                    nc.scalar.activation(q_all[:, t, :], q_all[:, t, :], ACT.Identity, bias=mean1[:, t:t + 1],
                                         scale=rstd1[:, t:t + 1]).then_inc(x1_ready, 1)
            for g in range(GROUPS):
                steps(act, (g + 1) * GROUP, window, 6, g * GROUP)
                if g >= 2:
                    norm1(g - 2)
            mixed_out(CHUNK - 2, 0)
            keep(CHUNK - 3, 1)
            mixed_out(CHUNK - 1, 1)
            keep(CHUNK - 2, 0)
            keep(CHUNK - 1, 1)
            norm1(GROUPS - 2)

            def copy_x1t(b):
                for c in range(C):
                    act.wait_ge(x1t_done, 2 * b + c + 1)
                    if past(b, 2):
                        act.wait_ge(router_done, b - 1)
                    nc.scalar.activation(x1_t[:, c, :], psum[:, 4 + c, :], ACT.Copy).then_inc(tok_copied, 1)

            def attend(b, u, i, more=True):
                if past(b, 2):
                    high_part(b - 2, 1)

                def exp(t):
                    act.wait_ge(peak_ready, 2 * b + t // (QT // 2) + 1)
                    if t >= 2:
                        act.wait_ge(pt_done, QT * b + t - 1)
                    elif past(b, 1):
                        act.wait_ge(pt_done, QT * b + t - 1)
                    nc.scalar.activation(probs[:, t % 2, 0:(t + 1) * P], psum[:, t, 0:(t + 1) * P], ACT.Exp,
                                         bias=bias2[:, u, t:t + 1], scale=1.0 / E ** 0.5,
                                         accum_out=row_sum[:, u, t:t + 1]).then_inc(exp2_done, 1)

                def copy(t):
                    act.wait_ge(pt_done, QT * b + t + 1)
                    if t < 2 and past(b, 1):
                        act.wait_ge(router_done, b)
                    if t >= 2:
                        act.wait_ge(av_done, QT * b + t - 1)
                    elif past(b, 1):
                        act.wait_ge(av_done, QT * b + t - 1)
                    nc.scalar.activation(probs_t[:, t % 2, 0:t + 1, :], psum[:, 4 + t % 2, 0:(t + 1) * P].rearrange(
                        "p (k n) -> p k n", n=P), ACT.Copy).then_inc(pt_copied, 1)
                if past(b, 1):
                    keep_x2(b - 1, 1 - u)
                    x2_transposed(b - 1)
                exp(0)
                exp(1)
                if past(b, 1):
                    high_part(b - 1, 0)
                copy(0)
                exp(2)
                copy(1)
                exp(3)
                copy(2)
                copy(3)
                if more:
                    copy_x1t(b + 1)

            def high_part(e, k):
                act.wait_ge(w_multiplied, 2 * e + k + 1)
                if k or past(e, 1):
                    act.wait_ge(w_low_made, 2 * e + k)
                nc.scalar.activation(w_high[:, bass.ds(e, 1), k, 0:EW], w_f32[:, bass.ds(e, 1), k, :],
                                     ACT.Copy).then_inc(w_high_made, 1)

            def keep_x2(b, u):
                act.wait_ge(normed2, QT * (b + 1))
                nc.scalar.activation(x2[:, bass.ds(QT * b, QT), :], x1_n[:, u], ACT.Copy).then_inc(x2_ready, QT)

            def x2_transposed(b):
                act.wait_ge(x2t_done, b + 1)
                nc.scalar.activation(x2_t[:, :, :], psum[:, 6:8, :], ACT.Copy).then_inc(x2t_copied, 1)
            act.wait_ge(x1_last, GROUP)
            copy_x1t(0)
            steps(act, B - 2, attend)
            attend(B - 2, 0, B // 2 - 1)
            attend(B - 1, 1, B // 2 - 1, more=False)
            high_part(N_EXP - 2, 1)
            keep_x2(B - 1, 1)
            x2_transposed(B - 1)
            high_part(N_EXP - 1, 0)
            high_part(N_EXP - 1, 1)

            act.wait_ge(gap_made, 1)
            nc.scalar.activation(top_v[:, 1, :], top_v[:, 1, :], ACT.Exp).then_inc(gap_exp, 1)

            def lot(s, u, i):
                act.wait_ge(rows_t_done, s + 1)
                nc.scalar.activation(rows_hi[:, u, :], psum[:, u, 0:E], ACT.Copy, scale=2.0 ** X_BITS).then_inc(rows_high, 1)
                if past(s, 3):
                    result_beside(s - 3, 1 - u)
                if past(s, 1):
                    gelu(s - 1, 1 - u)

            def result_beside(s, u):
                act.wait_ge(down_done, s + 1)
                if past(s, 2):
                    act.wait_ge(y_copied, s - 1)
                nc.scalar.activation(y_side[:, u, :], psum[:, 6 + u, E:2 * E], ACT.Identity, scale=y_scale1).then_inc(y_beside, 1)

            def gelu(s, u):
                act.wait_ge(up_done, s + 1)
                if past(s, 2):
                    act.wait_ge(hid_low, s - 1)
                nc.scalar.activation(hid[:, u, :].rearrange("p (h f) -> p h f", h=2), psum[:, 2 + 2 * u:4 + 2 * u, :], ACT.Gelu,
                                     scale=up_scale).then_inc(gelu_done, 1)
            for i in range(TOP * TILES // PART):
                act.wait_ge(slot_tiles, i + 1)
                nc.scalar.activation(is_slot[:, i * PART:(i + 1) * PART, SLOTS:], is_slot[:, i * PART:(i + 1) * PART, SLOTS:],
                                     ACT.Copy, scale=consts[:, AT_ROW:AT_ROW + 1]).then_inc(slots_marked, 1)
            act.wait_ge(routed, 1)
            steps(act, SLOTS, lot, 6)
            result_beside(SLOTS - 3, 1)
            gelu(SLOTS - 1, 1)
            result_beside(SLOTS - 2, 0)
            result_beside(SLOTS - 1, 1)

            def norm3(g, u, i):
                if past(g, 2):
                    act.wait_ge(out_stored[u], 16 * i)
                act.wait_ge(shift3_made, g + 1)
                for t in range(QT):
                    nc.scalar.activation(out_rows[:, u, t, :], sum3[:, u, t, :], ACT.Identity, bias=mean3[:, u, t:t + 1],
                                         scale=rstd3[:, u, t:t + 1]).then_inc(out_ready, 1)
                act.wait_ge(out_ready, QT * (g + 1))
                act.dma_start(out_group[bass.ds(g, 1)].rearrange("a (t p) e -> p (a t) e", p=P),
                              out_rows[:, u]).then_inc(out_stored[u], 16)
            steps(act, TILES // QT, norm3)

        @block.gpsimd
        def _(pool):
            def done(ins, signal, count):
                ins.then_inc(signal, 1)
                pool.wait_ge(signal, count)

            nc.gpsimd.memset(k_all[:, 0:R, :], 0.0).then_inc(halo_zeroed, 1)
            nc.gpsimd.memset(k_all[:, R + CHUNK:ROWS, :], 0.0).then_inc(halo_zeroed, 1)
            nc.gpsimd.memset(v_all[:, 0:R, :], 0.0).then_inc(halo_zeroed, 1)
            nc.gpsimd.memset(v_all[:, R + CHUNK:ROWS, :], 0.0).then_inc(halo_zeroed, 1)
            nc.gpsimd.memset(ones_pp[:, :], 1.0).then_inc(fills_made, 1)
            nc.gpsimd.memset(minus_half[:, :], -0.5).then_inc(fills_made, 1)
            pool.wait_ge(fills_made, 2)

            def gain_qk(t, u, i):
                pool.wait_ge(centred, t + 1)
                for m, dst in enumerate((row(q_all, t), row(k_all, t + R))):
                    heads = cen_qk[:, u, m * E:(m + 1) * E].rearrange("p (h d) -> p h d", d=D)
                    nc.gpsimd.tensor_tensor(dst.rearrange("p a (h d) -> p (a h) d", d=D), heads,
                                            gains[:, m:m + 1, :].to_broadcast([P, H, D]), ALU.mult).then_inc(gained, 1)

            pool.wait_ge(weights_loaded, WEIGHT_LOADS)
            def finish_queries(g):
                pool.wait_ge(gained, 2 * GROUP * (g + 1))
                pool.wait_ge(rstd_heads, g + 1)
                part = group(q_all, g).rearrange("p s (h d) -> p s h d", d=D)
                scale = group(head_rstd, g)[:, :, 0:H].unsqueeze(3)
                done(nc.gpsimd.tensor_tensor(part, part, scale.to_broadcast([P, GROUP, H, D]), ALU.mult), q_scaled, g + 1)
                part = group(q_all, g).rearrange("p s (h d) -> p (s h) d", d=D)
                nc.gpsimd.tensor_tensor(part, part, biases[:, 0:1, :].to_broadcast([P, GROUP * H, D]), ALU.add).then_inc(q_ready, 1)
            for g in range(GROUPS):
                steps(pool, (g + 1) * GROUP, gain_qk, 2, g * GROUP)
                if g:
                    finish_queries(g - 1)
            finish_queries(GROUPS - 1)
            pool.wait_ge(gate_done, 1)

            def weigh_values(t, u):
                pool.wait_ge(inv_ready, t + 1)
                done(nc.gpsimd.tensor_tensor(prob[:, u, :].rearrange("p (w h) -> p w h", h=H),
                                             score[:, u, :].rearrange("p (w h) -> p w h", h=H),
                                             inv_total[:, u, :].unsqueeze(1).to_broadcast([P, K, H]), ALU.mult), prob_made, t + 1)
                for half, (a, n) in enumerate(((0, W0), (W0, K - W0))):
                    if past(t, 1):
                        pool.wait_ge(av_used, 2 * t + half - 1)
                    values = v_all[:, bass.ds(t + a, n), :].rearrange("p w (h d) -> p (w h) d", d=D)
                    weights = prob[:, u, a * H:(a + n) * H].unsqueeze(2).to_broadcast([P, n * H, D])
                    nc.gpsimd.tensor_tensor(av_prod[half][:, :, :].rearrange("p w (h d) -> p (w h) d", d=D),
                                            values, weights, ALU.mult).then_inc(av_ready, 1)

            def silu(t, u):
                pool.wait_ge(y_parts, t + 1)
                nc.gpsimd.tensor_tensor(tanh_y[:, u, :], tanh_y[:, u, :], y_sb[:, u, :], ALU.mult).then_inc(silu_y_made, 1)

            def window(t, u, i):
                pool.wait_ge(peak_found, t + 1)
                scores = score[:, u, :].rearrange("p (w h) -> p w h", h=H)
                nc.gpsimd.tensor_tensor(scores, scores, peak[:, u, :].unsqueeze(1).to_broadcast([P, K, H]),
                                        ALU.subtract).then_inc(score_ready, 1)
                if past(t, 1):
                    weigh_values(t - 1, 1 - u)
                if past(t, 2):
                    silu(t - 2, u)

            def root(var, n, count):
                pool.wait_ge(var_made, count)
                nc.gpsimd.tensor_tensor(var, var, minus_half[:, 0:n], ALU.pow).then_inc(rstd_ready, 1)

            for g in range(GROUPS):
                steps(pool, (g + 1) * GROUP, window, 6, g * GROUP)
                if g >= 1:
                    root(rstd1[:, (g - 1) * GROUP:g * GROUP], GROUP, g)
            weigh_values(CHUNK - 1, 1)
            silu(CHUNK - 2, 0)
            silu(CHUNK - 1, 1)
            root(rstd1[:, CHUNK - GROUP:], GROUP, GROUPS)

            def low_part(e, k):
                pool.wait_ge(w_high_made, 2 * e + k + 1)
                nc.gpsimd.tensor_tensor(w_low[:, bass.ds(e, 1), k, 0:EW], w_f32[:, bass.ds(e, 1), k, :],
                                        w_high[:, bass.ds(e, 1), k, 0:EW], ALU.subtract).then_inc(w_low_made, 1)

            def attend(b, u, i):
                if past(b, 2):
                    low_part(b - 2, 1)
                if past(b, 1):
                    low_part(b - 1, 0)
                root(rstd2[:, u, :], QT, GROUPS + b + 1)
            steps(pool, B, attend)
            low_part(N_EXP - 2, 1)
            low_part(N_EXP - 1, 0)
            low_part(N_EXP - 1, 1)

            for i in range(TOP * TILES // PART):
                pool.wait_ge(slot_hits, i + 1)
                pairs = slice(i * PART, (i + 1) * PART)
                nc.gpsimd.tensor_tensor(is_slot[:, pairs, 0:SLOTS], is_slot[:, pairs, SLOTS:],
                                        consts[:, AT_TILE + i * PART:AT_TILE + (i + 1) * PART].unsqueeze(2)
                                        .to_broadcast([P, PART, SLOTS]), ALU.mult).then_inc(slot_tiles, 1)
            pool.wait_ge(routed, 1)
            for u in (0, 1):
                pool.wait_ge(x2_stored[u], 16 * (B // 2))

            def lot(s, u, i):
                if past(s, 2):
                    pool.wait_ge(rows_t_done, s - 1)
                nc.gpsimd.tensor_copy(src_col[:, u, :], slot_src[:, bass.ds(s, 1)]).then_inc(src_copied, 1)
                pool.wait_ge(src_copied, s + 1).then_inc(pool_waited, 1)
                nc.gpsimd.indirect_dma_start(rows[:, u, :], None, x2_dram, bass.IndirectOffsetOnAxis(src_col[:, u, :], 0)
                                             ).then_inc(rows_loaded[u], 16)
                if past(s, 4):
                    send(s - 4, u, i - 2)

            def send(s, u, i):
                pool.wait_ge(y_copied, s + 1)
                if past(s, 2):
                    pool.wait_ge(ys_stored[u], 16 * i)
                nc.gpsimd.tensor_copy(dst_col[:, u, :], slot_dst[:, bass.ds(s, 1)]).then_inc(dst_copied, 1)
                pool.wait_ge(dst_copied, s + 1).then_inc(pool_waited, 1)
                nc.gpsimd.indirect_dma_start(ys_dram, bass.IndirectOffsetOnAxis(dst_col[:, u, :], 0), y_rows[:, u, :], None
                                             ).then_inc(ys_stored[u], 16)
            steps(pool, SLOTS, lot, 6)
            send(SLOTS - 4, 0, SLOTS // 2 - 2)
            send(SLOTS - 3, 1, SLOTS // 2 - 2)
            send(SLOTS - 2, 0, SLOTS // 2 - 1)
            send(SLOTS - 1, 1, SLOTS // 2 - 1)
            steps(pool, TILES // QT, lambda g, u, i: root(rstd3[:, u, :], QT, GROUPS + B + g + 1))

        @block.vector
        def _(dve):
            def done(ins, signal, count):
                ins.then_inc(signal, 1)
                dve.wait_ge(signal, count)

            def moments(st, mean, var, count):
                done(nc.vector.tensor_tensor(mean, st[:, :, 1], st[:, :, 4], ALU.subtract), mean_diff, count + 1)
                done(nc.vector.tensor_tensor(var, mean, mean, ALU.mult), mean_diff_sq, count + 1)
                nc.vector.tensor_tensor(mean, st[:, :, 1], st[:, :, 4], ALU.add).then_inc(mean_added, 1)
                done(nc.vector.tensor_scalar(var, var, 0.25, EPS, ALU.mult, ALU.add), var_between, count + 1)
                done(nc.vector.scalar_tensor_tensor(var, st[:, :, 2], 1.0 / E, var, ALU.mult, ALU.add), var_even, count + 1)
                dve.wait_ge(mean_added, count + 1)
                nc.vector.tensor_scalar(mean, mean, 0.5, None, ALU.mult)
                nc.vector.scalar_tensor_tensor(var, st[:, :, 5], 1.0 / E, var, ALU.mult, ALU.add).then_inc(var_made, 1)

            def variance(t, u):
                dve.wait_ge(squared, t + 1).then_inc(dve_waited, 1)
                nc.vector.tensor_reduce(row(head_var, t).rearrange("p a x -> p (a x)"),
                                        sq_qk[:, u, :].rearrange("p (x d) -> p x d", d=D),
                                        op=ALU.add, axis=AX.X).then_inc(var_done, 1)

            def centre(t, u, i):
                dve.wait_ge(silu_done, t + 1)
                heads = act_qk[:, u, :].rearrange("p (x d) -> p x d", d=D)
                done(nc.vector.tensor_reduce(head_sum[:, u, :], heads, op=ALU.add, axis=AX.X), head_mean_summed, t + 1)
                if past(t, 2):
                    dve.wait_ge(gained, 2 * t - 2)
                nc.vector.scalar_tensor_tensor(cen_qk[:, u, :].rearrange("p (x d) -> p x d", d=D),
                                               head_sum[:, u, :].unsqueeze(2).to_broadcast([P, 2 * H, D]), -1.0 / D, heads,
                                               ALU.mult, ALU.add).then_inc(centred, 1)
                if past(t, 1):
                    variance(t - 1, 1 - u)
            dve.wait_ge(weights_loaded, WEIGHT_LOADS)

            def finish_keys(g):
                dve.wait_ge(var_done, (g + 1) * GROUP)
                var, rstd, part = group(head_var, g), group(head_rstd, g), group(newton, g)
                nc.vector.tensor_scalar(var, var, 1.0 / D, EPS, ALU.mult, ALU.add).then_inc(var_eps, 1)
                dve.wait_ge(root_done, g + 1)
                done(nc.vector.reciprocal(rstd, rstd), newton_step, 4 * g + 1)
                done(nc.vector.tensor_tensor(part, var, rstd, ALU.mult), newton_step, 4 * g + 2)
                done(nc.vector.tensor_tensor(part, part, rstd, ALU.mult), newton_step, 4 * g + 3)
                done(nc.vector.tensor_scalar(part, part, -0.5, 1.5, ALU.mult, ALU.add), newton_step, 4 * g + 4)
                done(nc.vector.tensor_tensor(rstd, rstd, part, ALU.mult), rstd_heads, g + 1)
                dve.wait_ge(gained, 2 * GROUP * (g + 1))
                of_group = group(k_all[:, R:R + CHUNK, :], g)
                keys = of_group.rearrange("p s (h d) -> p s h d", d=D)
                done(nc.vector.tensor_tensor(keys, keys, rstd[:, :, H:2 * H].unsqueeze(3).to_broadcast([P, GROUP, H, D]),
                                             ALU.mult), k_scaled, g + 1)
                keys = of_group.rearrange("p s (h d) -> p (s h) d", d=D)
                nc.vector.tensor_tensor(keys, keys, biases[:, 1:2, :].to_broadcast([P, GROUP * H, D]), ALU.add).then_inc(k_ready, 1)
            for g in range(GROUPS):
                steps(dve, (g + 1) * GROUP, centre, 4, g * GROUP)
                if g:
                    finish_keys(g - 1)
            variance(CHUNK - 1, 1)
            finish_keys(GROUPS - 1)

            dve.wait_ge(sig_done, 1)
            nc.vector.tensor_scalar(sharp[:, :, :], win[:, :, H:2 * H], 9.5, 0.5, ALU.mult, ALU.add).then_inc(width_done, 1)
            nc.vector.tensor_scalar(edge[:, :, :], win[:, :, 0:H], float(R), 0.5, ALU.mult, ALU.add).then_inc(width_done, 1)
            dve.wait_ge(width_done, 2)
            done(nc.vector.tensor_tensor(edge[:, :, :], edge[:, :, :], sharp[:, :, :], ALU.mult), width_done, 3)
            for half in range(2):
                part = slice(half * CHUNK // 2, (half + 1) * CHUNK // 2)
                for r in range(R + 1):
                    nc.vector.scalar_tensor_tensor(gate[:, part, r, :], sharp[:, part, :], float(r), edge[:, part, :], ALU.mult,
                                                   ALU.subtract).then_inc(gate_args, 1)
                dve.wait_ge(gate_args, (half + 1) * (R + 1)).then_inc(gate_arg, 1)
            dve.wait_ge(q_ready, GROUPS)
            dve.wait_ge(gate_done, 1)

            def window(t, u, i):
                queries = row(q_all, t).to_broadcast([P, K, E])
                nc.vector.tensor_tensor(qk_prod[:, :].rearrange("p (w c) -> p w c", c=E), queries,
                                        k_all[:, bass.ds(t, K), :], ALU.mult).then_inc(qk_multiplied, 1)
                if past(t, 1):
                    sum_up(t - 1, 1 - u)
                dve.wait_ge(qk_multiplied, t + 1)
                if past(t, 2):
                    dve.wait_ge(prob_made, t - 1)
                nc.vector.tensor_reduce(score[:, u, :], qk_prod[:, :].rearrange("p (x d) -> p x d", d=D),
                                        op=ALU.add, axis=AX.X).then_inc(qk_summed, 1)
                if past(t, 1):
                    invert(t - 1, 1 - u)
                by_offset = score[:, u, :].rearrange("p (w h) -> p w h", h=H)
                gates = row(gate, t).rearrange("p a r h -> p (a r) h")
                dve.wait_ge(qk_summed, t + 1)
                nc.vector.scalar_tensor_tensor(by_offset[:, R:, :], gates, -PENALTY / SCALE, by_offset[:, R:, :],
                                               ALU.mult, ALU.add).then_inc(penalised, 1)
                nc.vector.scalar_tensor_tensor(by_offset[:, R - 1::-1, :], gates[:, 1:, :], -PENALTY / SCALE,
                                               by_offset[:, R - 1::-1, :], ALU.mult, ALU.add).then_inc(penalised, 1)
                if past(t, 3):
                    add_x(t - 3, 1 - u, i - 2 + u)
                dve.wait_ge(penalised, 2 * t + 2)
                nc.vector.tensor_reduce(peak[:, u, :], score[:, u, :].rearrange("p (w h) -> p h w", h=H), op=ALU.max,
                                        axis=AX.X).then_inc(peak_found, 1)
                if past(t, 3):
                    take_stats(t - 3, 1 - u)

            def sum_up(t, u):
                dve.wait_ge(exp_done, t + 1)
                nc.vector.tensor_reduce(total[:, u, :], score[:, u, :].rearrange("p (w h) -> p h w", h=H), op=ALU.add,
                                        axis=AX.X).then_inc(total_found, 1)

            def invert(t, u):
                dve.wait_ge(total_found, t + 1)
                nc.vector.reciprocal(inv_total[:, u, :], total[:, u, :]).then_inc(inv_ready, 1)

            def add_x(t, u, i):
                dve.wait_ge(silu_y_made, t + 1)
                dve.wait_ge(x_res_loaded[u], 16 * i + 16)
                nc.vector.tensor_tensor(x_res[:, u, :], x_res[:, u, :], tanh_y[:, u, :], ALU.add).then_inc(res_summed, 1)

            def take_stats(t, u):
                dve.wait_ge(res_summed, t + 1)
                if past(t, 2):
                    dve.wait_ge(res_kept, t - 1)
                nc.vector.bn_stats(bn6[:, u, :], x_res[:, u, :]).then_inc(res_done, 1)

            def group_moments(g):
                part = slice(g * GROUP, (g + 1) * GROUP)
                dve.wait_ge(res_kept, (g + 1) * GROUP)
                moments(stats[:, part], mean1[:, part], rstd1[:, part], g)

            def group_shift(g):
                part = slice(g * GROUP, (g + 1) * GROUP)
                dve.wait_ge(rstd_ready, g + 1)
                nc.vector.scalar_tensor_tensor(mean1[:, part], mean1[:, part], -1.0, rstd1[:, part], ALU.mult,
                                               ALU.mult).then_inc(norm1_shift, 1)
            dve.wait_ge(halo_loaded, 16 * 4 * B)
            for g in range(GROUPS):
                if g == GROUPS // 2:
                    dve.wait_ge(gate_done, 2)
                steps(dve, (g + 1) * GROUP, window, 8, g * GROUP, 4)
                if g >= 2:
                    group_shift(g - 2)
                if g >= 1:
                    group_moments(g - 1)
            sum_up(CHUNK - 1, 1)
            invert(CHUNK - 1, 1)
            for t in range(CHUNK - 3, CHUNK):
                add_x(t, t % 2, t // 2)
                take_stats(t, t % 2)

            dve.wait_ge(w_squared, 2 * CHUNK).then_inc(dve_waited, 1)
            nc.vector.tensor_reduce(w_sum[:, :], w_squares[:, :, :], op=ALU.add, axis=AX.X).then_inc(w_summed, 1)

            group_shift(GROUPS - 2)
            group_moments(GROUPS - 1)
            dve.wait_ge(rstd_ready, GROUPS)
            for t in range(CHUNK - GROUP, CHUNK):
                nc.vector.tensor_scalar(q_all[:, t, :], q_all[:, t, :], mean1[:, t:t + 1], rstd1[:, t:t + 1], ALU.subtract,
                                        ALU.mult).then_inc(x1_last, 1)
            dve.wait_ge(w_total, 1)
            done(nc.vector.tensor_copy(w_sum[:, :], psum[:, 0, 0:2]), w_exps, 1)
            done(nc.vector.tensor_scalar(w_exp, w_sum[:, :].bitcast(I32), F32_MANT, None, ALU.logical_shift_right), w_exps, 2)
            done(nc.vector.tensor_scalar(w_exp, w_exp, F32_BIAS + 2, None, ALU.add), w_exps, 3)
            done(nc.vector.tensor_scalar(w_exp, w_exp, 1, None, ALU.logical_shift_right), w_exps, 4)
            hid_bits = TOP_BITS - (E.bit_length() - 1) // 2
            for col, k, sign, add in ((0, 0, -1, 2 * F32_BIAS + TOP_BITS), (1, 1, -1, 2 * F32_BIAS + TOP_BITS),
                                      (2, 0, 1, -X_BITS - TOP_BITS), (3, 0, -1, 2 * F32_BIAS + hid_bits),
                                      (4, 0, 1, -hid_bits), (5, 1, 1, -TOP_BITS)):
                nc.vector.tensor_scalar(scale_bits[:, col:col + 1], w_exp[:, k:k + 1], sign, add, ALU.mult, ALU.add).then_inc(w_exps, 1)
            dve.wait_ge(w_exps, 10)
            nc.vector.tensor_scalar(scale_bits[:, 0:6], scale_bits[:, 0:6], F32_MANT, None, ALU.logical_shift_left).then_inc(w_scaled, 1)

            def attend(b, u, i, more=True):
                def mask(t):
                    dve.wait_ge(s_done, QT * b + t + 1)
                    diag = psum[:, t, t * P:(t + 1) * P]
                    nc.vector.tensor_tensor(diag, diag, consts[:, AT_MASK:AT_MASK + P], ALU.add).then_inc(masked, 1)

                def find_peak(t):
                    dve.wait_ge(masked, QT * b + t + 1)
                    nc.vector.tensor_reduce(top_peak[:, u, t:t + 1], psum[:, t, 0:(t + 1) * P], op=ALU.max,
                                            axis=AX.X).then_inc(peak_found2, 1)
                def scale_peaks(half):
                    part = slice(half * QT // 2, (half + 1) * QT // 2)
                    dve.wait_ge(peak_found2, QT * b + part.stop)
                    nc.vector.tensor_scalar(bias2[:, u, part], top_peak[:, u, part], -1.0 / E ** 0.5, None,
                                            ALU.mult).then_inc(peak_ready, 1)
                mask(0)
                mask(1)
                if past(b, 1):
                    norm2(b - 1, 1 - u)
                find_peak(0)
                find_peak(1)
                mask(2)
                scale_peaks(0)
                if past(b, 1):
                    scale_weights(b - 1)
                mask(3)
                find_peak(2)
                find_peak(3)
                scale_peaks(1)
                if past(b, 1):
                    choose(b - 1, 1 - u)
                for t in range(QT):
                    dve.wait_ge(av_done, QT * b + t + 1)
                    done(nc.vector.reciprocal(inv_row[:, u, t:t + 1], row_sum[:, u, t:t + 1]), inv2_made, QT * b + t + 1)
                    nc.vector.scalar_tensor_tensor(x1_n[:, u, t, :], psum[:, 6 + t % 2, 0:E], inv_row[:, u, t:t + 1],
                                                   x1_n[:, u, t, :], ALU.mult, ALU.add).then_inc(sum2_done, 1)
                    dve.wait_ge(sum2_done, QT * b + t + 1)
                    nc.vector.bn_stats(stats2[:, u, t, :], x1_n[:, u, t, :]).then_inc(stats2_done, 1)
                dve.wait_ge(stats2_done, QT * (b + 1))
                moments(stats2[:, u], mean2[:, u, :], rstd2[:, u, :], GROUPS + b)

            def scale_weights(b):
                dve.wait_ge(w_scaled, 1)
                dve.wait_ge(w_loaded, 32 * b + 32)
                for k in range(2):
                    matrix = w_f32[:, bass.ds(b, 1), k, :].rearrange("p a x -> p (a x)")
                    nc.vector.tensor_scalar(matrix, matrix, w_scale[:, k:k + 1], None, ALU.mult).then_inc(w_multiplied, 1)

            def norm2(b, u):
                dve.wait_ge(rstd_ready, GROUPS + b + 1)
                for t in range(QT):
                    nc.vector.tensor_scalar(x1_n[:, u, t, :], x1_n[:, u, t, :], mean2[:, u, t:t + 1], rstd2[:, u, t:t + 1],
                                            ALU.subtract, ALU.mult).then_inc(normed2, 1)

            def choose(b, u):
                dve.wait_ge(router_done, b + 1)
                nc.vector.tensor_copy(logits[:, u].rearrange("p t n -> p (t n)"), psum[:, 7, 0:QT * N_EXP]).then_inc(logits_copied, 1)
                dve.wait_ge(logits_copied, b + 1).then_inc(dve_waited, 1)
                for t in range(QT):
                    nc.vector.max(top8[:, u, t, :], logits[:, u, t, :]).then_inc(top_found, 1)
                dve.wait_ge(top_found, QT * (b + 1)).then_inc(dve_waited, 1)
                for t in range(QT):
                    nc.vector.max_index(where8[:, u, t, :].bitcast(U32), top8[:, u, t, :], logits[:, u, t, :]).then_inc(where_found, 1)
                dve.wait_ge(where_found, QT * (b + 1))
                nc.vector.tensor_copy(top_v[:, :, bass.ds(QT * b, QT)], top8[:, u, :, 0:TOP].rearrange("p t k -> p k t"))
                nc.vector.tensor_copy(top_i[:, :, bass.ds(QT * b, QT)],
                                      where8[:, u, :, 0:TOP].bitcast(U32).rearrange("p t k -> p k t")).then_inc(top_kept, 1)
            steps(dve, B - 2, attend)
            attend(B - 2, 0, B // 2 - 1)
            attend(B - 1, 1, B // 2 - 1, more=False)
            scale_weights(N_EXP - 1)
            norm2(B - 1, 1)
            choose(B - 1, 1)

            dve.wait_ge(top_kept, B)
            dve.wait_ge(x2_ready, QT * B)
            nc.vector.tensor_tensor(top_v[:, 1, :], top_v[:, 1, :], top_v[:, 0, :], ALU.subtract).then_inc(gap_made, 1)
            count = consts[:, AT_COUNT:AT_COUNT + P]
            done(nc.vector.tensor_tensor(chosen, top_i.unsqueeze(3).to_broadcast([P, TOP, TILES, N_EXP]),
                                         count[:, 0:N_EXP].unsqueeze(1).unsqueeze(1).to_broadcast([P, TOP, TILES, N_EXP]),
                                         ALU.is_equal), chosen_made, 1)
            nc.vector.tensor_tensor(picked, chosen[:, 0], chosen[:, 1], ALU.add).then_inc(picked_made, 1)
            dve.wait_ge(counted, 1)
            tile_count = psum[:, 1, 0:TILES * N_EXP].rearrange("p (t n) -> p t n", n=N_EXP)
            n_scan = 1
            done(nc.vector.tensor_copy(upto[0], tile_count), scan_step, n_scan)
            at, hop = 0, 1
            while hop < TILES:
                nc.vector.tensor_copy(upto[1 - at][:, 0:hop, :], upto[at][:, 0:hop, :])
                n_scan += 1
                done(nc.vector.tensor_tensor(upto[1 - at][:, hop:, :], upto[at][:, hop:, :], upto[at][:, 0:TILES - hop, :],
                                             ALU.add), scan_step, n_scan)
                at, hop = 1 - at, 2 * hop
            n_lots = 0

            def lots_done(ins):
                nonlocal n_lots
                n_lots += 1
                done(ins, lots_step, n_lots)
            lots_done(nc.vector.tensor_scalar(lots_i, upto[at][:, TILES - 1, :], float(P - 1), None, ALU.add))
            lots_done(nc.vector.tensor_scalar(lots_i, lots_i, P.bit_length() - 1, None, ALU.logical_shift_right))
            lots_done(nc.vector.tensor_copy(lots_n, lots_i))
            lots_done(nc.vector.tensor_copy(lots[:, 0, :], lots_n))
            now, hop = 0, 1
            while hop < N_EXP:
                nc.vector.tensor_copy(lots[:, 1 - now, 0:hop], lots[:, now, 0:hop])
                lots_done(nc.vector.tensor_tensor(lots[:, 1 - now, hop:], lots[:, now, hop:], lots[:, now, 0:N_EXP - hop], ALU.add))
                now, hop = 1 - now, 2 * hop
            lots_end = lots[:, now, :]
            done(nc.vector.tensor_tensor(place, upto[at], tile_count, ALU.subtract), place_made, 1)
            done(nc.vector.tensor_tensor(place, place, psum[:, 0, 0:TILES * N_EXP].rearrange("p (t n) -> p t n", n=N_EXP),
                                         ALU.add), place_made, 2)
            lots_done(nc.vector.tensor_tensor(lots_n, lots_end, lots_n, ALU.subtract))
            lots_done(nc.vector.tensor_scalar(lots_n, lots_n, float(P), None, ALU.mult))
            done(nc.vector.tensor_tensor(place, place, lots_n.unsqueeze(1).to_broadcast([P, TILES, N_EXP]), ALU.add), place_made, 3)
            done(nc.vector.tensor_tensor(placed, chosen, place.unsqueeze(1).to_broadcast([P, TOP, TILES, N_EXP]), ALU.mult),
                 placed_made, 1)
            done(nc.vector.tensor_reduce(spot, placed, op=ALU.add, axis=AX.X), spot_made, 1)
            done(nc.vector.tensor_copy(spot_i[:, 0], spot), spot_int, 1)
            nc.vector.tensor_scalar(spot_i[:, 1], spot_i[:, 0], P.bit_length() - 1, None, ALU.logical_shift_right).then_inc(spot_parts, 1)
            dve.wait_ge(spot_parts, 1)
            done(nc.vector.tensor_scalar(spot_i[:, 0], spot_i[:, 0], P - 1, None, ALU.bitwise_and), spot_parts, 2)
            flat = "p k t -> p (k t)"
            nc.vector.tensor_copy(spot_slot, spot_i[:, 1].rearrange(flat)).then_inc(spot_back, 1)
            done(nc.vector.tensor_copy(spot_row, spot_i[:, 0].rearrange(flat)), spot_back, 2)
            n_pairs = TOP * TILES
            for part in range(0, n_pairs, PART):
                nc.vector.tensor_tensor(is_slot[:, part:part + PART, SLOTS:],
                                        spot_slot[:, part:part + PART].unsqueeze(2).to_broadcast([P, PART, SLOTS]),
                                        count[:, 0:SLOTS].unsqueeze(1).to_broadcast([P, PART, SLOTS]),
                                        ALU.is_equal).then_inc(slot_hits, 1)
            for part in range(0, n_pairs, PART):
                nc.vector.tensor_tensor(is_row[:, part:part + PART, :],
                                        spot_row[:, part:part + PART].unsqueeze(2).to_broadcast([P, PART, P]),
                                        count.unsqueeze(1).to_broadcast([P, PART, P]), ALU.is_equal).then_inc(rows_marked, 1)
            done(nc.vector.tensor_tensor(slot_past, count[:, 0:SLOTS].unsqueeze(2).to_broadcast([P, SLOTS, N_EXP]),
                                         lots_end.unsqueeze(1).to_broadcast([P, SLOTS, N_EXP]), ALU.is_ge), past_made, 1)
            done(nc.vector.tensor_reduce(slot_f[:, 0, :], slot_past, op=ALU.add, axis=AX.X), past_made, 2)
            done(nc.vector.tensor_scalar(slot_f[:, 0, :], slot_f[:, 0, :], float(N_EXP - 1), None, ALU.min), past_made, 3)
            half = SLOTS // 2
            words, word_sum = slot_f[:, 1, 0:half], slot_f[:, 1, half:]
            done(nc.vector.scalar_tensor_tensor(words, slot_f[:, 0, 1::2], float(N_EXP), slot_f[:, 0, 0::2], ALU.mult, ALU.add),
                 past_made, 4)
            done(nc.vector.tensor_copy(word_sum, words), past_made, 5)
            for back in (1, 2, 3):
                done(nc.vector.scalar_tensor_tensor(word_sum[:, back:], words[:, 0:half - back], float(N_EXP ** (2 * back)),
                                                    word_sum[:, back:], ALU.mult, ALU.add), past_made, 5 + back)
            done(nc.vector.tensor_copy(slot_word, word_sum), past_made, 9)
            dve.wait_ge(table_done, 1)
            n_slot = 0

            def slot_done(ins):
                nonlocal n_slot
                n_slot += 1
                done(ins, slot_step, n_slot)
            slot_done(nc.vector.tensor_copy(slot_f[:, 3, :], psum[:, 2, SLOTS:2 * SLOTS]))
            slot_done(nc.vector.scalar_tensor_tensor(slot_f[:, 1, :], psum[:, 2, 0:SLOTS], float(P), slot_f[:, 3, :],
                                                     ALU.mult, ALU.add))
            slot_done(nc.vector.tensor_scalar(slot_f[:, 2, :], slot_f[:, 1, :], 0.0, None, ALU.is_equal))
            slot_done(nc.vector.tensor_tensor(slot_f[:, 3, :], slot_f[:, 1, :], slot_f[:, 2, :], ALU.add))
            slot_done(nc.vector.tensor_scalar(slot_src, slot_f[:, 3, :], -1.0, None, ALU.add))
            slot_done(nc.vector.tensor_scalar(slot_src, slot_src, T - 1, None, ALU.bitwise_and))
            slot_done(nc.vector.tensor_tensor(slot_f[:, 2, :], slot_f[:, 2, :], consts[:, AT_SPILL:AT_SPILL + SLOTS], ALU.mult))
            slot_done(nc.vector.tensor_tensor(slot_f[:, 1, :], slot_f[:, 1, :], slot_f[:, 2, :], ALU.add))
            nc.vector.tensor_scalar(slot_dst, slot_f[:, 1, :], -1.0, None, ALU.add).then_inc(routed, 1)
            dve.wait_ge(gap_exp, 1)
            done(nc.vector.tensor_scalar(top_v[:, 0, :], top_v[:, 1, :], 1.0, None, ALU.add), gap_plus1, 1)
            done(nc.vector.reciprocal(top_v[:, 0, :], top_v[:, 0, :]), gate1_made, 1)
            done(nc.vector.tensor_tensor(top_v[:, 1, :], top_v[:, 1, :], top_v[:, 0, :], ALU.mult), gates_made, 1)
            nc.vector.tensor_scalar(top_v, top_v, y_scale2, None, ALU.mult).then_inc(gates_made, 1)

            def lot(s, u, i):
                dve.wait_ge(rows_high, s + 1)
                nc.vector.scalar_tensor_tensor(rows_lo[:, u, :], psum[:, u, 0:E], 2.0 ** X_BITS, rows_hi[:, u, :], ALU.mult,
                                               ALU.subtract).then_inc(rows_low, 1)
                if past(s, 3):
                    result_out(s - 3, 1 - u, i - 2 + u)
                if past(s, 1):
                    split_hidden(s - 1, 1 - u)

            def split_hidden(s, u):
                dve.wait_ge(gelu_done, s + 1)
                if past(s, 2):
                    dve.wait_ge(down_done, s - 1)
                done(nc.vector.tensor_scalar(hid_hi[:, u, :], hid[:, u, :], hid_scale, None, ALU.mult), hid_high, s + 1)
                nc.vector.scalar_tensor_tensor(hid_lo[:, u, :], hid[:, u, :], hid_scale, hid_hi[:, u, :], ALU.mult,
                                               ALU.subtract).then_inc(hid_low, 1)

            def result_out(s, u, i):
                dve.wait_ge(down_done, s + 1)
                if past(s, 2):
                    dve.wait_ge(ys_stored[u], 16 * i)
                dve.wait_ge(y_beside, s + 1)
                nc.vector.scalar_tensor_tensor(y_rows[:, u, :], psum[:, 6 + u, 0:E], y_scale1, y_side[:, u, :], ALU.mult,
                                               ALU.add).then_inc(y_copied, 1)
            dve.wait_ge(routed, 1)
            steps(dve, SLOTS, lot, 8, unrolled=4)
            result_out(SLOTS - 3, 1, SLOTS // 2 - 2)
            split_hidden(SLOTS - 1, 1)
            result_out(SLOTS - 2, 0, SLOTS // 2 - 1)
            result_out(SLOTS - 1, 1, SLOTS // 2 - 1)

            dve.wait_ge(gates_made, 2)

            def finish(g, u, i):
                dve.wait_ge(y_loaded[u], 32 * i + 32)
                if past(g, 2):
                    dve.wait_ge(out_ready, QT * (g - 1))
                for t in range(QT):
                    nc.vector.scalar_tensor_tensor(sum3[:, u, t, :], y_pick[0][:, u, t, :], top_v[:, 0, bass.ds(QT * g + t, 1)],
                                                   x2[:, bass.ds(QT * g + t, 1), :].rearrange("p a e -> p (a e)"),
                                                   ALU.mult, ALU.add).then_inc(mix1_done, 1)
                for t in range(QT):
                    dve.wait_ge(mix1_done, QT * g + t + 1)
                    nc.vector.scalar_tensor_tensor(sum3[:, u, t, :], y_pick[1][:, u, t, :], top_v[:, 1, bass.ds(QT * g + t, 1)],
                                                   sum3[:, u, t, :], ALU.mult, ALU.add).then_inc(mix2_done, 1)
                if past(g, 1):
                    shift3(g - 1, 1 - u)
                for t in range(QT):
                    dve.wait_ge(mix2_done, QT * g + t + 1).then_inc(dve_waited, 1)
                    nc.vector.bn_stats(stats3[:, u, t, :], sum3[:, u, t, :]).then_inc(stats3_done, 1)
                dve.wait_ge(stats3_done, QT * (g + 1))
                moments(stats3[:, u], mean3[:, u, :], rstd3[:, u, :], GROUPS + B + g)

            def shift3(g, u):
                dve.wait_ge(rstd_ready, GROUPS + B + g + 1)
                nc.vector.scalar_tensor_tensor(mean3[:, u, :], mean3[:, u, :], -1.0, rstd3[:, u, :], ALU.mult,
                                               ALU.mult).then_inc(shift3_made, 1)
            steps(dve, TILES // QT, finish)
            shift3(TILES // QT - 1, 1)


def kernel(x, ctx_1024, L0_attn_Wq, L0_attn_Wkv, L0_attn_q_g, L0_attn_q_b, L0_attn_k_g, L0_attn_k_b, L0_attn_Wwin,
           L0_attn_bwin, L0_attn_Wout, L0_ffn_router_w, L0_ffn_expert_w1, L0_ffn_expert_w2):
    import numpy as np
    import concourse.bacc as bacc
    from concourse.bass_utils import run_bass_kernel_spmd

    laid = np.ascontiguousarray
    tokens = np.asarray(x).reshape(T, E)
    ctx = np.asarray(ctx_1024)
    arrays = {
        "x": laid(tokens),
        "x_steps": laid(tokens.reshape(P, CHUNK, E).transpose(1, 2, 0)),
        "ctx": laid(ctx),
        "ctx_t": laid(ctx.transpose(0, 2, 1)),
        "Wq": laid(L0_attn_Wq), "Wkv": laid(L0_attn_Wkv),
        "q_g": laid(L0_attn_q_g), "q_b": laid(L0_attn_q_b), "k_g": laid(L0_attn_k_g), "k_b": laid(L0_attn_k_b),
        "Wwin": laid(L0_attn_Wwin), "bwin": laid(L0_attn_bwin), "Wout": laid(L0_attn_Wout),
        "router_t": laid(np.asarray(L0_ffn_router_w).T),
        "w1_t": laid(np.asarray(L0_ffn_expert_w1).transpose(0, 2, 1)),
        "w2_t": laid(np.asarray(L0_ffn_expert_w2).transpose(0, 2, 1)),
        "shape_consts": host_consts(),
    }
    nc = bacc.Bacc("TRN2", target_bir_lowering=False, num_devices=1)
    aps = {n: nc.dram_tensor(n, a.shape, mybir.dt.from_np(a.dtype), kind="ExternalInput").ap() for n, a in arrays.items()}
    out = nc.dram_tensor("out", (T, E), F32, kind="ExternalOutput").ap()
    decoder_layer(nc, out=out, **aps)
    got = run_bass_kernel_spmd(nc, [arrays], core_ids=[0])
    return got.results[0]["out"].reshape(B, L, E)
```
